# Optimizing a Trainium2 kernel written in Bass

```python
import numpy as np
import jax
import jax.numpy as jnp

def _softmax(x, axis=-1):
    return jax.nn.softmax(x, axis=axis)

def _gelu(x):
    return jax.nn.gelu(x, approximate=True)

def _silu(x):
    return jax.nn.silu(x)

def _sigmoid(x):
    return jax.nn.sigmoid(x)

def _layernorm(x, axis=-1, eps=1e-05):
    m = jnp.mean(x, axis=axis, keepdims=True)
    v = jnp.var(x, axis=axis, keepdims=True)
    return (x - m) / jnp.sqrt(v + eps)

def _scatter_add(tgt, idx, src, axis=0):
    return tgt.at[idx].add(src)

def _segment_sum(src, seg, n):
    return jax.ops.segment_sum(src, seg, n)
kernel_name = 'mk_gnn_resnorm_d2_gnn_r8_a479c0'

def setup_inputs(seed: int=0):
    np.random.seed(seed)
    _w = jnp.asarray

    def _rec_inputs():
        import jax
        import jax.numpy as jnp
        _gk = jax.random.key(seed)
        x = -0.0001538 + 1 * jax.random.normal(jax.random.fold_in(_gk, 1), (1024, 768), jnp.float32)
        src = jax.random.randint(jax.random.fold_in(_gk, 2), (16384,), 0, 1024, jnp.int32)
        dst = jax.random.randint(jax.random.fold_in(_gk, 3), (16384,), 0, 1024, jnp.int32)
        _o = jnp.argsort(dst, stable=True)
        src = src[_o]
        dst = dst[_o]
        return (x, src, dst)
    x, src, dst = _rec_inputs()

    def _L0_gnn_setup():
        import jax, jax.numpy as jnp
        import numpy as np
        NEG_SLOPE = 0.2
        EPS = 1e-16
        N_NODES = 1024
        N_EDGES = 8192
        D_IN = 768
        D_HID = 768
        H1 = 8
        H2 = 1

        def gat_layer(x, W, a_s, a_d, b, edge_index, concat):
            n = x.shape[0]
            H, C = a_s.shape
            h = (x @ W).reshape(n, H, C)
            src, dst = (edge_index[0], edge_index[1])
            alpha_s = jnp.einsum('nhc,hc->nh', h, a_s)
            alpha_d = jnp.einsum('nhc,hc->nh', h, a_d)
            e = jax.nn.leaky_relu(alpha_s[src] + alpha_d[dst], NEG_SLOPE)
            m = jax.ops.segment_max(e, dst, num_segments=n)
            e = jnp.exp(e - m[dst])
            denom = jax.ops.segment_sum(e, dst, num_segments=n)
            alpha = e / (denom[dst] + EPS)
            msg = h[src] * alpha[:, :, None]
            out = jax.ops.segment_sum(msg, dst, num_segments=n)
            out = out.reshape(n, H * C) if concat else out.mean(axis=1)
            return out + b
        key = jax.random.key(seed)
        ks = jax.random.split(key, 10)
        x = jax.random.normal(ks[0], (N_NODES, D_IN), dtype=jnp.float32)
        edge_list = jax.random.randint(ks[1], (2, N_EDGES), 0, N_NODES, dtype=jnp.int32)
        s = 0.05
        W1 = jax.random.normal(ks[2], (D_IN, H1 * D_HID), dtype=jnp.float32) * s
        a_src1 = jax.random.normal(ks[3], (H1, D_HID), dtype=jnp.float32) * s
        a_dst1 = jax.random.normal(ks[4], (H1, D_HID), dtype=jnp.float32) * s
        b1 = jnp.zeros((H1 * D_HID,), dtype=jnp.float32)
        W2 = jax.random.normal(ks[5], (H1 * D_HID, H2 * D_HID), dtype=jnp.float32) * s
        a_src2 = jax.random.normal(ks[6], (H2, D_HID), dtype=jnp.float32) * s
        a_dst2 = jax.random.normal(ks[7], (H2, D_HID), dtype=jnp.float32) * s
        b2 = jnp.zeros((H2 * D_HID,), dtype=jnp.float32)
        return {'x': x, 'W1': W1, 'a_src1': a_src1, 'a_dst1': a_dst1, 'b1': b1, 'W2': W2, 'a_src2': a_src2, 'a_dst2': a_dst2, 'b2': b2, 'edge_list': edge_list}
    _L0_gnn_all = _L0_gnn_setup()
    _L0_gnn_in = {k: v for k, v in _L0_gnn_all.items() if k in ('W1', 'a_src1', 'a_dst1', 'b1', 'W2', 'a_src2', 'a_dst2', 'b2')}
    del _L0_gnn_all

    def _L1_gnn_setup():
        import jax, jax.numpy as jnp
        import numpy as np
        N_NODES = 1250
        D = 768
        N_EDGES = 20000

        def gcn_conv(x, W, b, src, dst, n_nodes):
            h = x @ W
            deg = jax.ops.segment_sum(jnp.ones_like(dst, dtype=h.dtype), dst, num_segments=n_nodes)
            dinv = jnp.where(deg > 0, jax.lax.rsqrt(deg), 0.0)
            norm = dinv[src] * dinv[dst]
            msgs = h[src] * norm[:, None]
            out = jax.ops.segment_sum(msgs, dst, num_segments=n_nodes)
            return out + b

        def add_self_loops(edge_index, n_nodes):
            loop = jnp.arange(n_nodes, dtype=edge_index.dtype)
            src = jnp.concatenate([edge_index[0], loop])
            dst = jnp.concatenate([edge_index[1], loop])
            return (src, dst)
        key = jax.random.key(seed)
        k1, k2, k3, k4 = jax.random.split(key, 4)
        x = jax.random.normal(k1, (N_NODES, D), dtype=jnp.float32)
        edge_index = jax.random.randint(k2, (2, N_EDGES), 0, N_NODES, dtype=jnp.int32)
        glorot = float(np.sqrt(6.0 / (D + D)))
        W1 = jax.random.uniform(k3, (D, D), jnp.float32, -glorot, glorot)
        W2 = jax.random.uniform(k4, (D, D), jnp.float32, -glorot, glorot)
        b1 = jnp.zeros((D,), jnp.float32)
        b2 = jnp.zeros((D,), jnp.float32)
        return {'x': x, 'W1': W1, 'b1': b1, 'W2': W2, 'b2': b2, 'edge_index': edge_index}
    _L1_gnn_all = _L1_gnn_setup()
    _L1_gnn_in = {k: v for k, v in _L1_gnn_all.items() if k in ('W1', 'b1', 'W2', 'b2')}
    del _L1_gnn_all
    return {'x': x, 'src': src, 'dst': dst, 'L0_gnn_W1': _L0_gnn_in['W1'], 'L0_gnn_a_src1': _L0_gnn_in['a_src1'], 'L0_gnn_a_dst1': _L0_gnn_in['a_dst1'], 'L0_gnn_b1': _L0_gnn_in['b1'], 'L0_gnn_W2': _L0_gnn_in['W2'], 'L0_gnn_a_src2': _L0_gnn_in['a_src2'], 'L0_gnn_a_dst2': _L0_gnn_in['a_dst2'], 'L0_gnn_b2': _L0_gnn_in['b2'], 'L1_gnn_W1': _L1_gnn_in['W1'], 'L1_gnn_b1': _L1_gnn_in['b1'], 'L1_gnn_W2': _L1_gnn_in['W2'], 'L1_gnn_b2': _L1_gnn_in['b2']}

def reference(x, src, dst, L0_gnn_W1, L0_gnn_a_src1, L0_gnn_a_dst1, L0_gnn_b1, L0_gnn_W2, L0_gnn_a_src2, L0_gnn_a_dst2, L0_gnn_b2, L1_gnn_W1, L1_gnn_b1, L1_gnn_W2, L1_gnn_b2):
    import jax
    import jax.numpy as jnp

    def _L0_gnn_ref(x, W1, a_src1, a_dst1, b1, W2, a_src2, a_dst2, b2, edge_list):
        import jax, jax.numpy as jnp
        import numpy as np
        NEG_SLOPE = 0.2
        EPS = 1e-16
        N_NODES = 1024
        N_EDGES = 8192
        D_IN = 768
        D_HID = 768
        H1 = 8
        H2 = 1

        def gat_layer(x, W, a_s, a_d, b, edge_index, concat):
            n = x.shape[0]
            H, C = a_s.shape
            h = (x @ W).reshape(n, H, C)
            src, dst = (edge_index[0], edge_index[1])
            alpha_s = jnp.einsum('nhc,hc->nh', h, a_s)
            alpha_d = jnp.einsum('nhc,hc->nh', h, a_d)
            e = jax.nn.leaky_relu(alpha_s[src] + alpha_d[dst], NEG_SLOPE)
            m = jax.ops.segment_max(e, dst, num_segments=n)
            e = jnp.exp(e - m[dst])
            denom = jax.ops.segment_sum(e, dst, num_segments=n)
            alpha = e / (denom[dst] + EPS)
            msg = h[src] * alpha[:, :, None]
            out = jax.ops.segment_sum(msg, dst, num_segments=n)
            out = out.reshape(n, H * C) if concat else out.mean(axis=1)
            return out + b
        h = gat_layer(x, W1, a_src1, a_dst1, b1, edge_list, concat=True)
        h = jax.nn.elu(h)
        out = gat_layer(h, W2, a_src2, a_dst2, b2, edge_list, concat=True)
        return out

    def _L1_gnn_ref(x, W1, b1, W2, b2, edge_index):
        import jax, jax.numpy as jnp
        import numpy as np
        N_NODES = 1250
        D = 768
        N_EDGES = 20000

        def gcn_conv(x, W, b, src, dst, n_nodes):
            h = x @ W
            deg = jax.ops.segment_sum(jnp.ones_like(dst, dtype=h.dtype), dst, num_segments=n_nodes)
            dinv = jnp.where(deg > 0, jax.lax.rsqrt(deg), 0.0)
            norm = dinv[src] * dinv[dst]
            msgs = h[src] * norm[:, None]
            out = jax.ops.segment_sum(msgs, dst, num_segments=n_nodes)
            return out + b

        def add_self_loops(edge_index, n_nodes):
            loop = jnp.arange(n_nodes, dtype=edge_index.dtype)
            src = jnp.concatenate([edge_index[0], loop])
            dst = jnp.concatenate([edge_index[1], loop])
            return (src, dst)
        n = x.shape[0]
        src, dst = add_self_loops(edge_index, n)
        h = gcn_conv(x, W1, b1, src, dst, n)
        h = jax.nn.relu(h)
        out = gcn_conv(h, W2, b2, src, dst, n)
        return out
    edge_index = jnp.stack([src, dst])
    x = _layernorm(x + _L0_gnn_ref(x, L0_gnn_W1, L0_gnn_a_src1, L0_gnn_a_dst1, L0_gnn_b1, L0_gnn_W2, L0_gnn_a_src2, L0_gnn_a_dst2, L0_gnn_b2, edge_index), axis=-1)
    x = _layernorm(x + _L1_gnn_ref(x, L1_gnn_W1, L1_gnn_b1, L1_gnn_W2, L1_gnn_b2, edge_index), axis=-1)
    return x

_drawn_inputs = setup_inputs


def setup_inputs(seed=0):
    import zlib

    import numpy as np

    out = dict(_drawn_inputs(seed))
    spreads = {'L0_gnn_b1': (0.0, 0.1),
     'L0_gnn_b2': (0.0, 0.1),
     'L1_gnn_b1': (0.0, 0.1),
     'L1_gnn_b2': (0.0, 0.1)}
    factors = {}
    for name, (base, spread) in spreads.items():
        noise = np.random.default_rng([zlib.crc32(name.encode()), seed]).standard_normal(out[name].shape)
        drawn = base * np.exp(spread * noise) if base else spread * noise
        out[name] = jnp.asarray(drawn.astype(out[name].dtype))
    for name, factor in factors.items():
        out[name] = (out[name] * factor).astype(out[name].dtype)
    return out
```

```python
import concourse.bass as bass
from concourse import mybir
from contextlib import ExitStack

F32 = mybir.dt.float32
F32R = mybir.dt.float32r
BF16 = mybir.dt.bfloat16
F16 = mybir.dt.float16
I16 = mybir.dt.int16
I32 = mybir.dt.int32
ALU = mybir.AluOpType
ACT = mybir.ActivationFunctionType
AX = mybir.AxisListType

P = 128
N = 1024
NB = N // P
D = 768
FB = D // P
HC = D // 2
H = 8
E = 16384
ET = E // P
HALF = N // 2
HNB = HALF // P
LN_EPS = 1e-5
DEN_EPS = 1e-16
SLOPE = 0.2
NOT_LINKED = -1e30
LOWEST = -3.0e38

SBUF_FROM = 16512
SBUF_TO = 229344


def split_products(nc, out, stationary, moving, first, last, grouped=True):
    (sh, sl), (mh, ml) = stationary, moving
    nc.tensor.matmul(out, sh, mh, start=first, stop=False, skip_group_check=not grouped)
    nc.tensor.matmul(out, sh, ml, start=False, stop=False, skip_group_check=not grouped)
    return nc.tensor.matmul(out, sl, mh, start=False, stop=last, skip_group_check=not grouped)


def gnn_resnorm(nc, x, src, dst, gat_w1, gat_a_src1, gat_a_dst1, gat_b1, gat_w2, gat_a_src2, gat_a_dst2, gat_b2,
                gcn_w1, gcn_b1, gcn_w2, gcn_b2, out):
    ctx = ExitStack()
    held = []

    def sem(name):
        held.append(nc.alloc_semaphore(name=name))
        return held[-1]

    def end_of_stage():
        nc.clear_and_free_semaphores(held)
        held.clear()
        nc.all_engine_barrier()

    with ctx:
        place = [SBUF_FROM]

        def sb(name, shape, dt, at=place):
            size = 2 if dt in (BF16, F16, I16) else 4
            for n in shape[1:]:
                size *= n
            t = nc.alloc_sbuf_tensor_at(name, shape, dt, offset=at[0])
            at[0] += -(-size // 32) * 32
            assert at[0] <= SBUF_TO, (name, at[0])
            return t

        countT = sb("countT", [P, NB, N], I16)
        ident = sb("ident", [P, P], F32)
        ones = sb("ones", [P, P], F32)
        zero_r = sb("zero_r", [P, P], F32R)
        src_logit = sb("src_logit", [P, H, NB], F32)
        src_logit02 = sb("src_logit02", [P, H, NB], F32)
        bias1 = sb("bias1", [P, H * FB], F32)
        deg_parts = sb("deg_parts", [P, NB, 2], F32)
        dinv = sb("dinv", [P, NB], F32)
        gcn_bias1 = sb("gcn_bias1", [P, FB], F32)
        FREE = place[0]

        banks = [ctx.enter_context(nc.psum_tensor(f"bank{i}", [P, 512], F32)) for i in range(8)]

        logits_d = nc.dram_tensor("logits_scratch", [2 * H, N], F32, kind="Internal").ap()
        expo_d = nc.dram_tensor("expo_scratch", [2 * H, N], F32, kind="Internal").ap()
        logits2_d = nc.dram_tensor("logits2_scratch", [NB, P], F32, kind="Internal").ap()
        expo2_d = nc.dram_tensor("expo2_scratch", [2, NB, P], F32, kind="Internal").ap()
        dinv_d = nc.dram_tensor("dinv_scratch", [NB, P], F32, kind="Internal").ap()
        mask_d = nc.dram_tensor("mask_scratch", [P, NB * N], BF16, kind="Internal").ap()
        h2_d = nc.dram_tensor("h2_scratch", [N, D], F32, kind="Internal").ap()
        g_d = nc.dram_tensor("g_scratch", [N, D], F32, kind="Internal").ap()
        x1_d = nc.dram_tensor("x1_scratch", [N, D], F32, kind="Internal").ap()

        graph_and_logits(nc, ctx, sb, sem, FREE, banks, locals())
        end_of_stage()
        for half in range(2):
            attention_heads(nc, ctx, sb, sem, FREE, banks, half, locals())
            hidden_to_rows(nc, ctx, sb, sem, FREE, banks, half, locals())
            end_of_stage()
        x1 = second_attention(nc, ctx, sb, sem, FREE, banks, locals())
        graph_convolution(nc, ctx, sb, sem, banks, x1, locals())


def graph_and_logits(nc, ctx, sb, sem, FREE, banks, t):
    x, countT, ident, ones, zero_r = t["x"], t["countT"], t["ident"], t["ones"], t["zero_r"]
    src_logit, src_logit02, bias1 = t["src_logit"], t["src_logit02"], t["bias1"]
    deg_parts, dinv, gcn_bias1 = t["deg_parts"], t["dinv"], t["gcn_bias1"]
    logits_d, expo_d, dinv_d, mask_d = t["logits_d"], t["expo_d"], t["dinv_d"], t["mask_d"]
    gat_w1, gat_a_src1, gat_a_dst1 = t["gat_w1"], t["gat_a_src1"], t["gat_a_dst1"]

    at = [FREE]
    xr = sb("pro_x", [P, NB, D], F32, at)
    xT = sb("pro_xT", [P, FB, N], F32, at)
    w = [sb(f"pro_w{i}", [P, FB, D], F32, at) for i in range(2)]
    a_bc = [sb(f"pro_a{i}", [P, 2, D], F32, at) for i in range(2)]
    junk = [sb(f"pro_junk{i}", [P, N], BF16, at) for i in range(2)]
    hot_src = [sb(f"hot_src{i}", [P, N], BF16, at) for i in range(4)]
    hot_dst = [sb(f"hot_dst{i}", [P, P], BF16, at) for i in range(4)]
    node_i = sb("node_i", [P, N], I32, at)
    node_h = sb("node_h", [P, N], F16, at)
    count = [sb(f"count{i}", [P, N], F32, at) for i in range(2)]
    mask = sb("mask", [P, NB, N], BF16, at)
    edge_i = sb("edge_i", [P, 2, P], I32, at)
    edge_f = sb("edge_f", [P, 2, P], F32, at)
    edgeT = sb("edgeT", [P, 2, 2 * P], F32, at)
    quad_i = sb("quad_i", [P, P], I32, at)
    quad = sb("quad", [P, P], F32, at)
    quad_end = sb("quad_end", [P, P], F32, at)
    block_i = sb("block_i", [P, NB], I32, at)
    block_f = sb("block_f", [P, NB], F32, at)
    span = sb("span", [P, 2], F32, at)
    touch = sb("touch", [P, 2, NB], F32, at)
    touchT = sb("touchT", [P, 2, P], F32, at)
    range_f = sb("range_f", [P, 4], F32, at)
    range_i = sb("range_i", [P, 2], I32, at)
    zero_b = sb("zero_b", [P, 512], BF16, at)
    v_head = [sb(f"v_head{i}", [P, 2, FB], F32, at) for i in range(2)]
    v = sb("v", [P, H, 2, FB], F32, at)
    logitT = sb("logitT", [2 * H, N], F32, at)
    logit = sb("logit", [P, NB, 2 * H], F32, at)
    row_bc = [sb(f"row_bc{i}", [P, N], F32, at) for i in range(2)]
    top = sb("top", [P, H, NB], F32, at)
    expo = sb("expo", [P, NB, 2, H], F32, at)
    expoT = sb("expoT", [2 * H, N], F32, at)
    b1_rows = sb("b1_rows", [H * FB, P], F32, at)
    gb_rows = sb("gb_rows", [FB, P], F32, at)
    dinvT = sb("dinvT", [NB, P], F32, at)
    deg = sb("deg", [P, NB], F32, at)

    edges_in, x_in, b_in = sem("edges_in"), sem("x_in"), sem("b_in")
    w_in = [sem(f"w_in{i}") for i in range(2)]
    const_g, const_v, edge_cast, edgeT_full, edgeT_done = (sem(n) for n in ("const_g", "const_v", "edge_cast", "edgeT_full", "edgeT_done"))
    span_done, span_full, range_done = sem("span_done"), sem("span_full"), sem("range_done")
    hot_ready = [sem(f"hot_ready{b}") for b in range(NB)]
    hot_free = [sem(f"hot_free{b}") for b in range(NB)]
    count_full, count_out, mask_done, turned_full, turned_out = (sem(n) for n in ("count_full", "count_out", "mask_done", "turned_full", "turned_out"))
    xT_full, xT_done = sem("xT_full"), sem("xT_done")
    bT_full, bT_done = sem("bT_full"), sem("bT_done")
    v_sum, v_done = sem("v_sum"), sem("v_done")
    logitT_full, logitT_done, logit_full, logit_done = (sem(n) for n in ("logitT_full", "logitT_done", "logit_full", "logit_done"))
    logits_out = sem("logits_out")
    row_in = [sem(f"row_in{i}") for i in range(2)]
    top_sum, expo_step, expo_full, expoT_done, expo_out = (sem(n) for n in ("top_sum", "expo_step", "expo_full", "expoT_done", "expo_out"))
    deg_step, root_done, dinv_done, dinvT_full, dinvT_done, dinv_out, mask_out = (sem(n) for n in ("deg_step", "root_done", "dinv_done", "dinvT_full", "dinvT_done", "dinv_out", "mask_out"))

    with nc.Block() as block:
        @block.sync
        def _(sp):
            sp.dma_start(edge_i[:, 0, :], t["src"].rearrange("(t p) -> t p", p=P)).then_inc(edges_in, 16)
            sp.dma_start(edge_i[:, 1, :], t["dst"].rearrange("(t p) -> t p", p=P)).then_inc(edges_in, 16)
            sp.dma_start(xr[:, :, :], x.rearrange("(b p) f -> p b f", p=P)).then_inc(x_in, 16)
            sp.dma_start(b1_rows[:, :], t["gat_b1"].rearrange("(k p) -> k p", p=P)).then_inc(b_in, 16)
            sp.dma_start(gb_rows[:, :], t["gcn_b1"].rearrange("(k p) -> k p", p=P)).then_inc(b_in, 16)

            def load_head(h, i):
                sp.dma_start(w[i][:, :, :], gat_w1[:, bass.ds(h * D, D)].rearrange("(f p) c -> p f c", p=P)).then_inc(w_in[i], 16)
                sp.dma_start(a_bc[i][:, 0, :], gat_a_src1[bass.ds(h, 1), :].rearrange("a c -> (a c)").partition_broadcast(P)).then_inc(w_in[i], 16)
                sp.dma_start(a_bc[i][:, 1, :], gat_a_dst1[bass.ds(h, 1), :].rearrange("a c -> (a c)").partition_broadcast(P)).then_inc(w_in[i], 16)

            load_head(0, 0)
            load_head(1, 1)
            with sp.Fori(1, H // 2) as pair:
                for i in range(2):
                    sp.wait_ge(v_done, pair * 2 + (i - 1))
                    load_head(pair * 2 + i, i)
            sp.wait_ge(logitT_done, 2)
            sp.dma_start(logits_d, logitT[:, :]).then_inc(logits_out, 16)
            sp.wait_ge(logits_out, 16)

            def load_row(h, i):
                sp.dma_start(row_bc[i][:, :], logits_d[bass.ds(h * 2, 1), :].rearrange("a n -> (a n)").partition_broadcast(P)).then_inc(row_in[i], 16)

            load_row(0, 0)
            load_row(1, 1)
            sp.wait_ge(mask_done, NB)
            sp.dma_start(mask_d, mask[:, :, :].rearrange("p b n -> p (b n)")).then_inc(mask_out, 16)
            with sp.Fori(1, H // 2) as pair:
                for i in range(2):
                    sp.wait_ge(top_sum, pair * 2 * NB + (i - 1) * NB)
                    load_row(pair * 2 + i, i)
            sp.wait_ge(expoT_done, 2)
            sp.dma_start(expo_d, expoT[:, :]).then_inc(expo_out, 16)
            sp.wait_ge(dinvT_done, 1)
            sp.dma_start(dinv_d, dinvT[:, :]).then_inc(dinv_out, 16)
            sp.wait_ge(expo_out, 16)
            sp.wait_ge(dinv_out, 16)
            sp.wait_ge(mask_out, 16)

        @block.gpsimd
        def _(pool):
            nc.gpsimd.memset(ident[:, :], 0.0).then_inc(const_g, 1)
            nc.gpsimd.iota(node_i[:, :], pattern=[[1, N]], base=0, channel_multiplier=0).then_inc(const_g, 1)
            nc.gpsimd.iota(quad_i[:, :], pattern=[[1, ET // 4], [0, 4]], base=0, channel_multiplier=0).then_inc(const_g, 1)
            nc.gpsimd.iota(block_i[:, :], pattern=[[P, NB]], base=0, channel_multiplier=0).then_inc(const_g, 1)
            pool.wait_ge(const_g, 4)
            nc.gpsimd.affine_select(out=ident[:, :], in_=ident[:, :], compare_op=ALU.not_equal, fill=1.0, base=0,
                                    pattern=[[-1, P]], channel_multiplier=1).then_inc(const_g, 1)

        @block.vector
        def _(dve):
            nc.vector.memset(zero_b[:, :], 0.0).then_inc(const_v, 1)
            nc.vector.memset(ones[:, :], 1.0).then_inc(const_v, 1)
            dve.wait_ge(const_g, 5)
            nc.vector.tensor_copy(node_h[:, :], node_i[:, :]).then_inc(const_v, 1)
            nc.vector.tensor_copy(quad[:, :], quad_i[:, :]).then_inc(const_v, 1)
            nc.vector.tensor_copy(block_f[:, :], block_i[:, :]).then_inc(const_v, 1)
            dve.wait_ge(const_v, 5)
            nc.vector.tensor_scalar(quad_end[:, :], quad[:, :], -1.0, float(ET // 4), ALU.mult, ALU.add).then_inc(const_v, 1)
            nc.vector.tensor_scalar(zero_r[:, :], ones[:, :], 0.0, None, ALU.mult).then_inc(const_v, 1)
            dve.wait_ge(const_v, 7)
            nc.vector.tensor_scalar(quad[:, :], quad[:, :], 1.0, None, ALU.add).then_inc(const_v, 1)
            dve.wait_ge(edges_in, 32)
            nc.vector.tensor_copy(edge_f[:, :, :], edge_i[:, :, :]).then_inc(edge_cast, 1)
            dve.wait_ge(edge_cast, 1)
            nc.vector.tensor_reduce(span[:, 0:1], edge_f[:, 1, :], AX.X, ALU.min).then_inc(span_done, 1)
            nc.vector.tensor_reduce(span[:, 1:2], edge_f[:, 1, :], AX.X, ALU.max).then_inc(span_done, 1)
            dve.wait_ge(span_done, 2)
            nc.vector.tensor_scalar(touch[:, 0, :], block_f[:, :], span[:, 0:1], float(-P), ALU.subtract, ALU.is_gt).then_inc(span_done, 1)
            nc.vector.tensor_scalar(touch[:, 1, :], block_f[:, :], span[:, 1:2], None, ALU.is_le).then_inc(span_done, 1)
            dve.wait_ge(span_done, 4)
            nc.vector.tensor_tensor(touch[:, 0, :], touch[:, 0, :], touch[:, 1, :], ALU.mult).then_inc(span_done, 1)
            dve.wait_ge(edgeT_full, 2)
            nc.vector.tensor_copy(edgeT[:, 0, 0:P], banks[4][:, 0:P]).then_inc(edgeT_done, 1)
            nc.vector.tensor_copy(edgeT[:, 1, 0:P], banks[5][:, 0:P]).then_inc(edgeT_done, 1)
            dve.wait_ge(span_full, 1)
            dve.wait_ge(const_v, 8)
            nc.vector.tensor_tensor(touchT[0:NB, 0, :], banks[6][0:NB, 0:P], quad_end[0:NB, :], ALU.mult).then_inc(range_done, 1)
            nc.vector.tensor_tensor(touchT[0:NB, 1, :], banks[6][0:NB, 0:P], quad[0:NB, :], ALU.mult).then_inc(range_done, 1)
            dve.wait_ge(range_done, 2)
            nc.vector.tensor_reduce(range_f[0:NB, 0:1], touchT[0:NB, 0, :], AX.X, ALU.max).then_inc(range_done, 1)
            nc.vector.tensor_reduce(range_f[0:NB, 1:2], touchT[0:NB, 1, :], AX.X, ALU.max).then_inc(range_done, 1)
            dve.wait_ge(range_done, 4)
            nc.vector.tensor_scalar(range_f[0:NB, 0:1], range_f[0:NB, 0:1], 1.0, -1.0, ALU.max, ALU.mult).then_inc(range_done, 1)
            dve.wait_ge(range_done, 5)
            nc.vector.tensor_scalar(range_f[0:NB, 2:3], range_f[0:NB, 0:1], float(ET // 4), None, ALU.add).then_inc(range_done, 1)
            dve.wait_ge(range_done, 6)
            nc.vector.tensor_tensor(range_f[0:NB, 3:4], range_f[0:NB, 1:2], range_f[0:NB, 2:3], ALU.subtract).then_inc(range_done, 1)
            dve.wait_ge(range_done, 7)
            nc.vector.tensor_scalar(range_f[0:NB, 3:4], range_f[0:NB, 3:4], 1.0, None, ALU.max).then_inc(range_done, 1)
            dve.wait_ge(range_done, 8)
            nc.vector.tensor_copy(range_i[0:NB, :], range_f[0:NB, 2:4]).then_inc(range_done, 1)
            dve.wait_ge(range_done, 9)
            dve.wait_ge(edgeT_done, 2)
            for b in range(NB):
                first_quad = dve.value_load(range_i[b:b + 1, 0:1], min_val=0, max_val=ET // 4 - 1)
                quads = dve.value_load(range_i[b:b + 1, 1:2], min_val=1, max_val=ET // 4)
                with dve.Fori(0, quads) as q:
                    for j in range(4):
                        tile = (q + first_quad) * 4 + j
                        dve.wait_ge(hot_free[b], q * 4 + (j + 1))
                        nc.vector.tensor_scalar(hot_src[j][:, :], node_h[:, :], edgeT[:, 0, bass.ds(tile, 1)], None, ALU.is_equal)
                        nc.vector.tensor_scalar(hot_dst[j][:, :], node_h[:, b * P:(b + 1) * P], edgeT[:, 1, bass.ds(tile, 1)], None,
                                                ALU.is_equal).then_inc(hot_ready[b], 1)
                if b >= 1:
                    dve.wait_ge(count_out, 2 * b)
                    nc.vector.tensor_scalar(mask[:, b - 1, :], count[(b - 1) % 2][:, :], 0.0, NOT_LINKED, ALU.is_equal, ALU.mult).then_inc(mask_done, 1)
            dve.wait_ge(count_out, 2 * NB)
            nc.vector.tensor_scalar(mask[:, NB - 1, :], count[(NB - 1) % 2][:, :], 0.0, NOT_LINKED, ALU.is_equal, ALU.mult).then_inc(mask_done, 1)
            nc.vector.tensor_tensor(deg[:, :], deg_parts[:, :, 0], deg_parts[:, :, 1], ALU.add).then_inc(deg_step, 1)
            dve.wait_ge(deg_step, 1)
            nc.vector.tensor_scalar(deg[:, :], deg[:, :], 1.0, None, ALU.add).then_inc(deg_step, 1)

            dve.sem_inc(v_sum, 2)
            with dve.Fori(0, H // 2) as pair:
                for i in range(2):
                    dve.wait_ge(w_in[i], pair * 48 + 48)
                    for k in range(2):
                        for f in range(FB):
                            dve.wait_ge(v_sum, pair * 24 + (12 * i + FB * k + f + 1))
                            nc.vector.tensor_tensor_reduce(out=junk[f % 2][:, 0:D], in0=w[i][:, f, :], in1=a_bc[i][:, k, :], scale=1.0, scalar=0.0,
                                                           op0=ALU.mult, op1=ALU.add, accum_out=v_head[i][:, k, f:f + 1]).then_inc(v_sum, 1)
                    dve.wait_ge(v_sum, pair * 24 + (12 * i + 14))
                    nc.vector.tensor_copy(v[:, bass.ds(pair * 2 + i, 1), :, :], v_head[i][:, :, :].unsqueeze(1)).then_inc(v_done, 1)

            dve.wait_ge(root_done, 1)
            nc.vector.reciprocal(dinv[:, :], deg[:, :]).then_inc(dinv_done, 1)
            dve.wait_ge(logit_full, 1)
            nc.vector.tensor_copy(logit[:, :, :], banks[6][:, 0:NB * 2 * H].rearrange("p (b r) -> p b r", b=NB)).then_inc(logit_done, 1)
            dve.wait_ge(logit_done, 1)
            by_head = logit[:, :, :].rearrange("p b (h k) -> p k h b", k=2)
            nc.vector.tensor_copy(src_logit[:, :, :], by_head[:, 0, :, :]).then_inc(logit_done, 1)
            nc.vector.tensor_scalar(src_logit02[:, :, :], by_head[:, 0, :, :], SLOPE, None, ALU.mult).then_inc(logit_done, 1)

            for h in range(H):
                dve.wait_ge(row_in[h % 2], 16 * (h // 2 + 1))
                for b in range(NB):
                    if h * NB + b >= 2:
                        dve.wait_ge(top_sum, h * NB + b - 1)
                    nc.vector.tensor_tensor_reduce(out=junk[b % 2][:, :], in0=mask[:, b, :], in1=row_bc[h % 2][:, :], scale=1.0, scalar=LOWEST,
                                                   op0=ALU.add, op1=ALU.max, accum_out=top[:, h, b:b + 1]).then_inc(top_sum, 1)
            dve.wait_ge(top_sum, H * NB)
            nc.vector.tensor_tensor(top[:, :, :], top[:, :, :], by_head[:, 1, :, :], ALU.add).then_inc(expo_step, 1)
            dve.wait_ge(expo_step, 1)
            nc.vector.scalar_tensor_tensor(out=top[:, :, :], in0=top[:, :, :], scalar=SLOPE, in1=top[:, :, :], op0=ALU.mult, op1=ALU.max).then_inc(expo_step, 1)
            dve.wait_ge(expo_step, 2)
            nc.vector.tensor_tensor(expo[:, :, 0, :].rearrange("p b h -> p h b"), by_head[:, 1, :, :], top[:, :, :], ALU.subtract).then_inc(expo_step, 1)
            nc.vector.scalar_tensor_tensor(out=expo[:, :, 1, :].rearrange("p b h -> p h b"), in0=by_head[:, 1, :, :], scalar=SLOPE, in1=top[:, :, :],
                                           op0=ALU.mult, op1=ALU.subtract).then_inc(expo_step, 1)

        @block.scalar
        def _(act):
            for g in range(2 * FB):
                f, hf = g // 2, g % 2
                act.wait_ge(xT_full, g + 1)
                nc.scalar.copy(xT[:, f, hf * 512:(hf + 1) * 512], banks[4 + g % 2][:, :]).then_inc(xT_done, 1)
            act.wait_ge(bT_full, 2)
            nc.scalar.copy(bias1[:, :], banks[7][:, 0:H * FB]).then_inc(bT_done, 1)
            nc.scalar.copy(gcn_bias1[:, :], banks[7][:, P:P + FB]).then_inc(bT_done, 1)

            def turn_out(b):
                act.wait_ge(turned_full, b + 1)
                for i in range(2):
                    nc.scalar.copy(countT[:, 4 * i:4 * i + 4, b * P:(b + 1) * P],
                                   banks[4 + i][:, :].rearrange("p (s d) -> p s d", s=4)).then_inc(turned_out, 1)

            for b in range(NB):
                act.wait_ge(count_full, b + 1)
                if b >= 2:
                    act.wait_ge(turned_full, b - 1)
                    act.wait_ge(mask_done, b - 1)
                for i in range(2):
                    nc.scalar.activation(count[b % 2][:, i * 512:(i + 1) * 512], banks[2 * (b % 2) + i][:, :], ACT.Copy,
                                         accum_out=deg_parts[:, b, i:i + 1]).then_inc(count_out, 1)
                if b >= 1:
                    turn_out(b - 1)
            turn_out(NB - 1)
            act.wait_ge(deg_step, 2)
            nc.scalar.activation(deg[:, :], deg[:, :], ACT.Sqrt).then_inc(root_done, 1)
            for i in range(2):
                act.wait_ge(logitT_full, i + 1)
                nc.scalar.copy(logitT[:, i * 512:(i + 1) * 512], banks[i][0:2 * H, :]).then_inc(logitT_done, 1)
            act.wait_ge(dinvT_full, 1)
            nc.scalar.copy(dinvT[:, :], banks[7][0:NB, 0:P]).then_inc(dinvT_done, 1)
            act.wait_ge(expo_full, 1)
            for i in range(2):
                nc.scalar.copy(expoT[:, i * 512:(i + 1) * 512], banks[i][0:2 * H, :]).then_inc(expoT_done, 1)

        @block.tensor
        def _(pe):
            pe.wait_ge(const_g, 5)
            pe.wait_ge(edge_cast, 1)
            for i in range(2):
                nc.tensor.transpose(banks[4 + i][:, 0:P], edge_f[:, i, :], ident[:, :]).then_inc(edgeT_full, 1)
            pe.wait_ge(span_done, 5)
            nc.tensor.transpose(banks[6][0:NB, 0:P], touch[:, 0, :], ident[:, :]).then_inc(span_full, 1)
            pe.wait_ge(b_in, 32)
            nc.tensor.transpose(banks[7][:, 0:H * FB], b1_rows[:, :], ident[0:H * FB, 0:H * FB]).then_inc(bT_full, 1)
            nc.tensor.transpose(banks[7][:, P:P + FB], gb_rows[:, :], ident[0:FB, 0:FB]).then_inc(bT_full, 1)
            pe.wait_ge(x_in, 16)
            pe.wait_ge(edgeT_done, 2)
            for g in range(2 * FB):
                f, hf = g // 2, g % 2
                if g >= 2:
                    pe.wait_ge(xT_done, g - 1)
                for j in range(4):
                    last = nc.tensor.transpose(banks[4 + g % 2][:, j * P:(j + 1) * P], xr[:, 4 * hf + j, f * P:(f + 1) * P], ident[:, :])
                last.then_inc(xT_full, 1)

            def turn(b):
                pe.wait_ge(count_out, 2 * b + 2)
                if b == 0:
                    pe.wait_ge(xT_done, 2 * FB)
                else:
                    pe.wait_ge(turned_out, 2 * b)
                for s in range(NB):
                    last = nc.tensor.transpose(banks[4 + s // 4][:, (s % 4) * P:(s % 4 + 1) * P], count[b % 2][:, s * P:(s + 1) * P], ident[:, :])
                last.then_inc(turned_full, 1)

            pe.wait_ge(const_v, 1)
            pe.wait_ge(range_done, 9)
            for b in range(NB):
                quads = pe.value_load(range_i[b:b + 1, 1:2], min_val=1, max_val=ET // 4)
                pair = banks[2 * (b % 2)], banks[2 * (b % 2) + 1]
                if b >= 2:
                    pe.wait_ge(count_out, 2 * (b - 1))
                for i in range(2):
                    last = nc.tensor.matmul(pair[i][:, :], zero_b[:, 0:P], zero_b[:, :], start=True, stop=False, skip_group_check=True)
                last.then_inc(hot_free[b], 4)
                with pe.Fori(0, quads) as q:
                    for j in range(4):
                        pe.wait_ge(hot_ready[b], q * 4 + (j + 1))
                        for i in range(2):
                            last = nc.tensor.matmul(pair[i][:, :], hot_dst[j][:, :], hot_src[j][:, i * 512:(i + 1) * 512],
                                                    start=False, stop=False, skip_group_check=True)
                        last.then_inc(hot_free[b], 1)
                for i in range(2):
                    last = nc.tensor.matmul(pair[i][:, :], zero_b[:, 0:P], zero_b[:, :], start=False, stop=True, skip_group_check=True)
                last.then_inc(count_full, 1)
                if b >= 1:
                    turn(b - 1)
            turn(NB - 1)

            pe.wait_ge(v_done, H)
            for i in range(2):
                for f in range(FB):
                    last = nc.tensor.matmul(banks[i][0:2 * H, :], v[:, :, :, f].rearrange("p h k -> p (h k)"), xT[:, f, i * 512:(i + 1) * 512],
                                            start=(f == 0), stop=(f == FB - 1))
                last.then_inc(logitT_full, 1)
            pe.wait_ge(logitT_done, 2)
            for b in range(NB):
                last = nc.tensor.transpose(banks[6][:, b * 2 * H:(b + 1) * 2 * H], logitT[:, b * P:(b + 1) * P], ident[0:2 * H, 0:2 * H])
            last.then_inc(logit_full, 1)
            pe.wait_ge(dinv_done, 1)
            pe.wait_ge(bT_done, 2)
            nc.tensor.transpose(banks[7][0:NB, 0:P], dinv[:, :], ident[:, :]).then_inc(dinvT_full, 1)
            pe.wait_ge(expo_step, 4)
            for b in range(NB):
                last = nc.tensor.transpose(banks[b // 4][0:2 * H, (b % 4) * P:(b % 4 + 1) * P], expo[:, b, :, :].rearrange("p k h -> p (k h)"), ident[:, :])
            last.then_inc(expo_full, 1)


STEPS = [("B", 0), ("B", 1)] + [s for k in range(2, FB) for s in (("C", k - 2), ("B", k))] + [("C", FB - 2), ("C", FB - 1)]
AT = {s: n for n, s in enumerate(STEPS)}
NS = len(STEPS)
RAW, PARTS = 3, 4


def attention_heads(nc, ctx, sb, sem, FREE, banks, half, t):
    x, countT, ident, ones, zero_r = t["x"], t["countT"], t["ident"], t["ones"], t["zero_r"]
    src_logit, src_logit02, bias1, expo_d = t["src_logit"], t["src_logit02"], t["bias1"], t["expo_d"]
    gat_w1, gat_w2 = t["gat_w1"], t["gat_w2"]
    n = f"_{half}"
    at = [FREE]
    xh = sb("xh" + n, [P, NB, D], F32R, at)
    xl = sb("xl" + n, [P, NB, D], F32R, at)
    ph = sb("ph" + n, [P, NB, HALF], F32R, at)
    pl = sb("pl" + n, [P, NB, HALF], F32R, at)
    yh = sb("yh" + n, [P, FB, HALF], F32R, at)
    yl = sb("yl" + n, [P, FB, HALF], F32R, at)
    hh = sb("hh" + n, [P, 3, HALF], F32R, at)
    hl = sb("hl" + n, [P, 3, HALF], F32R, at)
    wh = sb("wh" + n, [P, PARTS, D], F32R, at)
    wl = sb("wl" + n, [P, PARTS, D], F32R, at)
    wr = sb("wr" + n, [P, RAW, D], F32, at)
    xraw = nc.alloc_sbuf_tensor_at("xraw" + n, [P, NB, D], F32, offset=at[0] - 4 * D * (2 * PARTS + RAW))
    expo_bc = sb("expo_bc" + n, [P, 2, HALF], F32, at)
    e1 = sb("e1" + n, [P, 2, HALF], F32, at)
    e2 = sb("e2" + n, [P, 2, HALF], F32, at)
    pf = sb("pf" + n, [P, 2, HALF], F32, at)
    psum_rows = sb("psum_rows" + n, [P, HALF], F32, at)
    rden = sb("rden" + n, [P, HALF], F32, at)
    yf = sb("yf" + n, [P, 2, HALF], F32, at)
    he = sb("he" + n, [P, 2, HALF], F32, at)
    hr = sb("hr" + n, [P, 2, HALF], F32, at)

    x_in = sem("hx_in" + n)
    x_hi, x_lo = sem("x_hi" + n), sem("x_lo" + n)
    expo_in = sem("expo_in" + n)
    w_in = [sem(f"w_in{i}" + n) for i in range(RAW)]
    w_hi = sem("w_hi" + n)
    w_lo = sem("w_lo" + n)
    w_used = sem("w_used" + n)
    e_done = sem("e_done" + n)
    e_max = sem("e_max" + n)
    p_full = sem("p_full" + n)
    p_hi, p_lo = sem("p_hi" + n), sem("p_lo" + n)
    p_sum = sem("p_sum" + n)
    den_full, den_out, rden_done = sem("den_full" + n), sem("den_out" + n), sem("rden_done" + n)
    y_full = sem("y_full" + n)
    y_out = sem("y_out" + n)
    y_hi = sem("y_hi" + n)
    y_lo = sem("y_lo" + n)
    h_out = sem("h_out" + n)
    h_sum, h_hi = sem("h_sum" + n), sem("h_hi" + n)
    h_lo = sem("h_lo" + n)

    with nc.Block() as block:
        @block.sync
        def _(sp):
            def load_exponents(h):
                for k in range(2):
                    sp.dma_start(expo_bc[:, k, :], expo_d[bass.ds(h + k * H, 1), half * HALF:(half + 1) * HALF].rearrange("a n -> (a n)").partition_broadcast(P)).then_inc(expo_in, 16)

            def head(h, build_next):
                if build_next:
                    sp.wait_ge(e_done, h * 8 + 8)
                    load_exponents(h + 1)
                for s, (kind, k) in enumerate(STEPS):
                    i = s % RAW
                    sp.wait_ge(w_lo, h * NS + (s + 1))
                    if kind == "B":
                        sp.dma_start(wr[:, i, :].rearrange("p (f c) -> p f c", f=FB),
                                     gat_w1[:, bass.ds(h * D + k * P, P)].rearrange("(f p) c -> p f c", p=P)).then_inc(w_in[i], 16)
                    else:
                        sp.dma_start(wr[:, i, :], gat_w2[bass.ds(h * D + k * P, P), :]).then_inc(w_in[i], 16)

            sp.dma_start(xraw[:, :, :], x.rearrange("(b p) f -> p b f", p=P)).then_inc(x_in, 16)
            load_exponents(0)
            with sp.Fori(0, H - 1) as h:
                head(h, True)
            head(H - 1, False)

        @block.gpsimd
        def _(pool):
            pool.sem_inc(p_sum, 2)

            def sum_rows(v):
                for i in range(1, NB):
                    pool.wait_ge(p_full, v * 8 + (i + 3))
                    if i >= 2:
                        pool.wait_ge(p_sum, v * 7 + (i + 1))
                    before = pf[:, 0, :] if i == 1 else psum_rows[:, :]
                    nc.gpsimd.tensor_tensor(psum_rows[:, :], before, pf[:, i % 2, :], ALU.add).then_inc(p_sum, 1)

            sum_rows(0)
            with pool.Fori(0, H - 1) as h:
                pool.wait_ge(den_full, h + 1)
                sum_rows(h + 1)

        @block.scalar
        def _(act):
            def exponentials(v, i):
                if i == 0:
                    act.wait_ge(expo_in, v * 32 + 32)
                act.wait_ge(p_full, v * 8 + (i + 1))
                nc.scalar.activation(e1[:, i % 2, :], expo_bc[:, 0, :], ACT.Exp, bias=src_logit[:, bass.ds(v, 1), i])
                nc.scalar.activation(e2[:, i % 2, :], expo_bc[:, 1, :], ACT.Exp, bias=src_logit02[:, bass.ds(v, 1), i]).then_inc(e_done, 1)

            def weight_high(v, i):
                act.wait_ge(p_full, v * 8 + (i + 3))
                nc.scalar.copy(ph[:, i, :], pf[:, i % 2, :]).then_inc(p_hi, 1)

            def chunk_high(h, s):
                act.wait_ge(w_in[s % RAW], h * (NS // RAW * 16) + (s // RAW + 1) * 16)
                act.wait_ge(w_used, h * NS + (s + 1))
                nc.scalar.copy(wh[:, s % PARTS, :], wr[:, s % RAW, :]).then_inc(w_hi, 1)

            def build_first():
                for i in range(NB + 1):
                    if i < NB:
                        exponentials(0, i)
                    if i >= 1:
                        weight_high(0, i - 1)

            def head(h, build_next):
                for f in range(FB):
                    if f < PARTS:
                        chunk_high(h, f)
                    act.wait_ge(y_out, h * FB + (f + 2))
                    nc.scalar.copy(yh[:, f, :], yf[:, f % 2, :]).then_inc(y_hi, 1)
                if build_next:
                    act.wait_ge(y_full, h * FB + FB)
                for s, (kind, k) in enumerate(STEPS):
                    if build_next and s < NB:
                        exponentials(h + 1, s)
                    if kind == "B":
                        act.wait_ge(w_used, h * NS + (s + 1 + PARTS))
                        act.wait_ge(h_lo, h * FB + (k + 2))
                        b = bias1[:, bass.ds(h * FB + k, 1)]
                        nc.scalar.activation(he[:, k % 2, :], banks[6 + (k + 1) % 2][:, :], ACT.Exp, bias=b)
                        nc.scalar.activation(hr[:, k % 2, :], banks[6 + (k + 1) % 2][:, :], ACT.Relu, bias=b).then_inc(h_out, 1)
                    if build_next and 1 <= s < NB + 1:
                        weight_high(h + 1, s - 1)
                    if s + PARTS < NS:
                        chunk_high(h, s + PARTS)

            act.wait_ge(x_in, 16)
            for i in range(NB):
                nc.scalar.copy(xh[:, i, :], xraw[:, i, :]).then_inc(x_hi, 1)
            act.wait_ge(x_lo, NB)
            act.sem_inc(h_out, 2)
            build_first()
            with act.Fori(0, H - 1) as h:
                head(h, True)
            head(H - 1, False)

        @block.vector
        def _(dve):
            def weight_products(v, i):
                dve.wait_ge(e_done, v * 8 + (i + 1))
                nc.vector.tensor_tensor(e1[:, i % 2, :], e1[:, i % 2, :], e2[:, i % 2, :], ALU.max).then_inc(e_max, 1)
                dve.wait_ge(e_max, v * 8 + (i + 1))
                dve.wait_ge(p_sum, v * 7 + (i + 1 if i < 2 else max(i - 2, 1) + 2))
                dve.wait_ge(p_lo, v * 8 + (i + 1))
                nc.vector.scalar_tensor_tensor(out=pf[:, i % 2, :], in0=e1[:, i % 2, :], scalar=1.0,
                                               in1=countT[:, i, half * HALF:(half + 1) * HALF], op0=ALU.min, op1=ALU.mult).then_inc(p_full, 1)

            def weight_low(v, i):
                dve.wait_ge(p_hi, v * 8 + (i + 1))
                nc.vector.tensor_tensor(pl[:, i, :], pf[:, i % 2, :], ph[:, i, :].bitcast(F32), ALU.subtract).then_inc(p_lo, 1)

            def chunk_low(h, s):
                dve.wait_ge(w_hi, h * NS + (s + 1))
                nc.vector.tensor_tensor(wl[:, s % PARTS, :], wr[:, s % RAW, :], wh[:, s % PARTS, :].bitcast(F32), ALU.subtract).then_inc(w_lo, 1)

            def y_low(h, f):
                dve.wait_ge(y_hi, h * FB + (f + 1))
                nc.vector.tensor_tensor(yl[:, f, :], yf[:, f % 2, :], yh[:, f, :].bitcast(F32), ALU.subtract).then_inc(y_lo, 1)

            def head(h, build_next):
                dve.wait_ge(den_full, h + 1)
                dve.wait_ge(y_out, h * FB + 1)
                nc.vector.tensor_scalar(rden[:, :], banks[6][:, :], DEN_EPS, None, ALU.add).then_inc(den_out, 1)
                dve.wait_ge(den_out, h + 1)
                nc.vector.reciprocal(rden[:, :], rden[:, :]).then_inc(rden_done, 1)
                dve.wait_ge(rden_done, h + 1)
                for f in range(FB + 1):
                    if f < PARTS:
                        chunk_low(h, f)
                    if f < FB:
                        dve.wait_ge(y_full, h * FB + (f + 1))
                        dve.wait_ge(y_lo, h * FB + (f + 1))
                        nc.vector.tensor_tensor(yf[:, f % 2, :], banks[6 + (f + 1) % 2][:, :], rden[:, :], ALU.mult).then_inc(y_out, 1)
                    if f >= 1:
                        y_low(h, f - 1)
                for s, (kind, k) in enumerate(STEPS):
                    if build_next and s < NB:
                        weight_products(h + 1, s)
                    if kind == "B":
                        dve.wait_ge(h_out, h * FB + (k + 3))
                        nc.vector.scalar_tensor_tensor(out=he[:, k % 2, :], in0=he[:, k % 2, :], scalar=1.0, in1=hr[:, k % 2, :],
                                                       op0=ALU.min, op1=ALU.add).then_inc(h_sum, 1)
                        dve.wait_ge(h_sum, h * FB + (k + 1))
                        dve.wait_ge(h_lo, h * FB + (k + 1))
                        nc.vector.tensor_scalar(hh[:, k % 3, :], he[:, k % 2, :], 1.0, None, ALU.subtract).then_inc(h_hi, 1)
                        dve.wait_ge(h_hi, h * FB + (k + 1))
                        nc.vector.scalar_tensor_tensor(out=hl[:, k % 3, :], in0=he[:, k % 2, :], scalar=1.0, in1=hh[:, k % 3, :].bitcast(F32),
                                                       op0=ALU.subtract, op1=ALU.subtract).then_inc(h_lo, 1)
                    if build_next and 1 <= s < NB + 1:
                        weight_low(h + 1, s - 1)
                    if s + PARTS < NS:
                        chunk_low(h, s + PARTS)

            dve.sem_inc(w_lo, RAW)
            dve.sem_inc(p_full, 2)
            dve.sem_inc(p_lo, 2)
            dve.sem_inc(y_lo, 2)
            dve.sem_inc(h_lo, 3)
            dve.sem_inc(y_out, 1)
            for i in range(NB):
                dve.wait_ge(x_hi, i + 1)
                nc.vector.tensor_tensor(xl[:, i, :], xraw[:, i, :], xh[:, i, :].bitcast(F32), ALU.subtract).then_inc(x_lo, 1)
            dve.wait_ge(x_lo, NB)
            for i in range(NB + 1):
                if i < NB:
                    weight_products(0, i)
                if i >= 1:
                    weight_low(0, i - 1)
            with dve.Fori(0, H - 1) as h:
                head(h, True)
            head(H - 1, False)

        @block.tensor
        def _(pe):
            pe.wait_ge(x_lo, NB)
            for f in range(FB):
                nc.tensor.matmul(banks[f][:, :], zero_r[:, :], xl[:, 0, 0:HALF], start=True, stop=False, skip_group_check=True)
            pe.sem_inc(w_used, PARTS)

            def head(h):
                pe.wait_ge(p_sum, h * 7 + 9)
                pe.wait_ge(h_out, h * FB + 2)
                nc.tensor.matmul(banks[6][:, :], ones[:, :], psum_rows[:, :], start=True, stop=True).then_inc(den_full, 1)
                pe.wait_ge(p_lo, h * 8 + 10)
                for f in range(FB):
                    if f == 1:
                        pe.wait_ge(den_out, h + 1)
                    if f >= 2:
                        pe.wait_ge(y_out, h * FB + f)
                    fs = slice(f * P, (f + 1) * P)
                    for b in range(NB):
                        last = split_products(nc, banks[6 + (f + 1) % 2][:, :], (xh[:, b, fs], xl[:, b, fs]), (ph[:, b, :], pl[:, b, :]),
                                              b == 0, b == NB - 1)
                    last.then_inc(y_full, 1)
                for s, (kind, k) in enumerate(STEPS):
                    i = s % PARTS
                    pe.wait_ge(w_lo, h * NS + (s + 1 + RAW))
                    if kind == "B":
                        if k == 0:
                            pe.wait_ge(y_lo, h * FB + (FB + 2))
                        if k >= 2:
                            pe.wait_ge(h_out, h * FB + (k + 1))
                        for f in range(FB):
                            fs = slice(f * P, (f + 1) * P)
                            last = split_products(nc, banks[6 + (k + 1) % 2][:, :], (wh[:, i, fs], wl[:, i, fs]), (yh[:, f, :], yl[:, f, :]),
                                                  f == 0, f == FB - 1)
                    else:
                        pe.wait_ge(h_lo, h * FB + (k + 4))
                        for f in range(FB):
                            fs = slice(f * P, (f + 1) * P)
                            last = split_products(nc, banks[f][:, :], (wh[:, i, fs], wl[:, i, fs]), (hh[:, k % 3, :], hl[:, k % 3, :]),
                                                  False, False, grouped=False)
                    last.then_inc(w_used, 1)

            with pe.Fori(0, H) as h:
                head(h)
            for f in range(FB):
                nc.tensor.matmul(banks[f][:, :], zero_r[:, :], xl[:, 0, 0:HALF], start=False, stop=True, skip_group_check=True)


def hidden_to_rows(nc, ctx, sb, sem, FREE, banks, half, t):
    ident, h2_d = t["ident"], t["h2_d"]
    n = f"_{half}"
    at = [FREE]
    cols = sb("h2_cols" + n, [P, FB, HALF], F32, at)
    rows = sb("h2_rows" + n, [P, HNB, D], F32, at)
    cols_done, turned, rows_done, rows_out = (sem(s + n) for s in ("cols_done", "turned", "rows_done", "rows_out"))
    with nc.Block() as block:
        @block.scalar
        def _(act):
            for f in range(FB):
                nc.scalar.copy(cols[:, f, :], banks[f][:, :]).then_inc(cols_done, 1)

        @block.tensor
        def _(pe):
            pe.wait_ge(cols_done, FB)
            for b in range(HNB):
                pair = 2 * (b % 2)
                if b >= 2:
                    pe.wait_ge(rows_done, 2 * (b - 1))
                for i in range(2):
                    for j in range(3):
                        f = 3 * i + j
                        last = nc.tensor.transpose(banks[pair + i][:, j * P:(j + 1) * P], cols[:, f, b * P:(b + 1) * P], ident[:, :])
                    last.then_inc(turned, 1)

        @block.vector
        def _(dve):
            for b in range(HNB):
                for i in range(2):
                    dve.wait_ge(turned, 2 * b + i + 1)
                    nc.vector.tensor_copy(rows[:, b, i * HC:(i + 1) * HC], banks[2 * (b % 2) + i][:, 0:HC]).then_inc(rows_done, 1)

        @block.sync
        def _(sp):
            for b in range(HNB):
                sp.wait_ge(rows_done, 2 * b + 2)
                sp.dma_start(h2_d[half * HALF + b * P:half * HALF + (b + 1) * P, :], rows[:, b, :]).then_inc(rows_out, 16)
            sp.wait_ge(rows_out, 16 * HNB)


NORM_STEPS, NORM_ROOT = 6, 4


def normalise(nc, dve, row, stats, moments, root, n, added, step, root_done):
    dve.wait_ge(added, 2 * n + 2)
    for i in range(2):
        nc.vector.bn_stats(stats[:, i, :], row[:, i * HC:(i + 1) * HC]).then_inc(step, 1)
    dve.wait_ge(step, NORM_STEPS * n + 2)
    nc.vector.bn_aggr(moments, stats.rearrange("p i s -> p (i s)")).then_inc(step, 1)
    dve.wait_ge(step, NORM_STEPS * n + 3)
    nc.vector.tensor_scalar(root, moments[:, 1:2], LN_EPS, None, ALU.add).then_inc(step, 1)
    dve.wait_ge(root_done, n + 1)
    nc.vector.reciprocal(root, root).then_inc(step, 1)
    dve.wait_ge(step, NORM_STEPS * n + 5)
    nc.vector.tensor_scalar(row, row, moments[:, 0:1], root, ALU.subtract, ALU.mult).then_inc(step, 1)


def second_attention(nc, ctx, sb, sem, FREE, banks, t):
    x, countT, ident = t["x"], t["countT"], t["ident"]
    h2_d, mask_d, logits2_d, expo2_d = t["h2_d"], t["mask_d"], t["logits2_d"], t["expo2_d"]
    DX = D + 2
    at = [FREE]
    x1 = sb("x1", [P, NB, D], F32, at)
    b2_bc = sb("b2_bc", [P, D], F32, at)
    a2_bc = sb("a2_bc", [P, 2, D], F32, at)
    h2 = sb("h2", [P, 4, D], F32, at)
    gh = sb("gh", [P, NB, DX], F32R, at)
    gl = sb("gl", [P, NB, DX], F32R, at)
    ph = [sb(f"p2h{i}", [P, NB, HALF], F32R, at) for i in range(2)]
    pl = [sb(f"p2l{i}", [P, NB, HALF], F32R, at) for i in range(2)]
    mask_at = at[0]
    expo_bc = sb("expo2_bc", [P, 2, N], F32, at)
    e1 = sb("e1_2", [P, 2, HALF], F32, at)
    e2 = sb("e2_2", [P, 2, HALF], F32, at)
    pf = sb("pf_2", [P, 2, HALF], F32, at)
    row_bc = sb("row2_bc", [P, N], F32, at)
    junk = [sb(f"junk2{i}", [P, N], BF16, at) for i in range(2)]
    logit2 = sb("logit2", [P, 2, NB], F32, at)
    logit02 = sb("logit2_02", [P, NB], F32, at)
    logit2T = sb("logit2T", [NB, P], F32, at)
    top = sb("top2", [P, NB], F32, at)
    expo = sb("expo2", [P, 2, NB], F32, at)
    expoT = sb("expo2T", [2 * NB, P], F32, at)
    rden = sb("rden2", [P, NB], F32, at)
    stats = sb("stats1", [P, NB, 2, 6], F32, at)
    moments = sb("moments1", [P, NB, 2], F32, at)
    root = sb("root1", [P, NB], F32, at)
    mask = nc.alloc_sbuf_tensor_at("mask2", [P, NB, N], BF16, offset=mask_at - 4 * NB * HALF * 4)

    in_sem = {k: sem("in2_" + k) for k in ("x", "b", "a", "mask", "row", "expo")}
    h2_in = [sem(f"h2_in{i}") for i in range(4)]
    logit_sum, g_hi, g_lo, g_one = sem("logit2_sum"), sem("g_hi"), sem("g_lo"), sem("g_one")
    xb_done, turned, turned_out, logits_out, small = (sem(n) for n in ("xb_done", "turned2", "turned2_out", "logits2_out", "small2"))
    top_sum, e_done, e_max, p_full, p_hi, p_lo = (sem(n) for n in ("top2_sum", "e2_done", "e2_max", "p2_full", "p2_hi", "p2_lo"))
    agg_full, bank_free, agg_step, norm_step, root_sem = (sem(n) for n in ("agg2_full", "agg2_free", "agg2_step", "norm1_step", "root1_done"))

    with nc.Block() as block:
        @block.sync
        def _(sp):
            for b in range(NB):
                if b >= 4:
                    sp.wait_ge(g_lo, b - 3)
                    sp.wait_ge(logit_sum, 2 * (b - 3))
                sp.dma_start(h2[:, b % 4, :], h2_d[b * P:(b + 1) * P, :]).then_inc(h2_in[b % 4], 16)
                if b == 0:
                    sp.dma_start(a2_bc[:, 0, :], t["gat_a_src2"].rearrange("a c -> (a c)").partition_broadcast(P)).then_inc(in_sem["a"], 16)
                    sp.dma_start(a2_bc[:, 1, :], t["gat_a_dst2"].rearrange("a c -> (a c)").partition_broadcast(P)).then_inc(in_sem["a"], 16)
                if b == 3:
                    sp.dma_start(mask[:, :, :].rearrange("p b n -> p (b n)"), mask_d).then_inc(in_sem["mask"], 16)
                    sp.dma_start(x1[:, :, :], x.rearrange("(b p) f -> p b f", p=P)).then_inc(in_sem["x"], 16)
                    sp.dma_start(b2_bc[:, :], t["gat_b2"].partition_broadcast(P)).then_inc(in_sem["b"], 16)
            sp.wait_ge(turned_out, 1)
            sp.dma_start(logits2_d, logit2T[:, :]).then_inc(logits_out, 16)
            sp.wait_ge(logits_out, 16)
            sp.dma_start(row_bc[:, :], logits2_d.rearrange("b p -> (b p)").partition_broadcast(P)).then_inc(in_sem["row"], 16)
            sp.wait_ge(turned_out, 2)
            sp.dma_start(expo2_d.rearrange("k b p -> (k b) p"), expoT[:, :]).then_inc(logits_out, 16)
            sp.wait_ge(logits_out, 32)
            sp.dma_start(expo_bc[:, :, :].rearrange("p k n -> p (k n)"), expo2_d.rearrange("k b p -> (k b p)").partition_broadcast(P)).then_inc(in_sem["expo"], 16)

        @block.scalar
        def _(act):
            for b in range(NB):
                act.wait_ge(h2_in[b % 4], 16 * (b // 4 + 1))
                nc.scalar.copy(gh[:, b, 0:D], h2[:, b % 4, :]).then_inc(g_hi, 1)
            act.wait_ge(turned, 1)
            nc.scalar.copy(logit2T[:, :], banks[0][0:NB, 0:P]).then_inc(turned_out, 1)
            act.wait_ge(turned, 2)
            nc.scalar.copy(expoT[:, :], banks[1][0:2 * NB, 0:P]).then_inc(turned_out, 1)
            act.wait_ge(in_sem["expo"], 16)
            for half in range(2):
                for i in range(NB + 1):
                    c = half * NB + i
                    if i < NB:
                        if c >= 2:
                            act.wait_ge(p_full, c - 1)
                        hs = slice(half * HALF, (half + 1) * HALF)
                        nc.scalar.activation(e1[:, i % 2, :], expo_bc[:, 0, hs], ACT.Exp, bias=logit2[:, 0, i:i + 1])
                        nc.scalar.activation(e2[:, i % 2, :], expo_bc[:, 1, hs], ACT.Exp, bias=logit02[:, i:i + 1]).then_inc(e_done, 1)
                    if i >= 1:
                        act.wait_ge(p_full, c)
                        nc.scalar.copy(ph[half][:, i - 1, :], pf[:, (i - 1) % 2, :]).then_inc(p_hi, 1)
            for b in range(NB):
                act.wait_ge(norm_step, NORM_STEPS * b + NORM_ROOT)
                nc.scalar.activation(root[:, b:b + 1], root[:, b:b + 1], ACT.Sqrt).then_inc(root_sem, 1)

        @block.vector
        def _(dve):
            nc.vector.tensor_scalar(gh[:, :, D:DX], ident[:, 0:2 * NB].rearrange("p (b c) -> p b c", c=2), 0.0, 1.0, ALU.mult, ALU.add).then_inc(g_one, 1)
            nc.vector.tensor_scalar(gl[:, :, D:DX], ident[:, 0:2 * NB].rearrange("p (b c) -> p b c", c=2), 0.0, None, ALU.mult).then_inc(g_one, 1)
            dve.wait_ge(in_sem["a"], 32)
            for b in range(NB):
                dve.wait_ge(h2_in[b % 4], 16 * (b // 4 + 1))
                for k in range(2):
                    if b >= 1:
                        dve.wait_ge(logit_sum, 2 * b + k - 1)
                    nc.vector.tensor_tensor_reduce(out=junk[k][:, 0:D], in0=h2[:, b % 4, :], in1=a2_bc[:, k, :], scale=1.0, scalar=0.0,
                                                   op0=ALU.mult, op1=ALU.add, accum_out=logit2[:, k, b:b + 1]).then_inc(logit_sum, 1)
                dve.wait_ge(g_hi, b + 1)
                nc.vector.tensor_tensor(gl[:, b, 0:D], h2[:, b % 4, :], gh[:, b, 0:D].bitcast(F32), ALU.subtract).then_inc(g_lo, 1)
            dve.wait_ge(logit_sum, 2 * NB)
            nc.vector.tensor_scalar(logit02[:, :], logit2[:, 0, :], SLOPE, None, ALU.mult).then_inc(small, 1)
            dve.wait_ge(in_sem["x"], 16)
            dve.wait_ge(in_sem["b"], 16)
            for b in range(NB):
                nc.vector.tensor_tensor(x1[:, b, :], x1[:, b, :], b2_bc[:, :], ALU.add).then_inc(xb_done, 1)
            dve.wait_ge(in_sem["row"], 16)
            dve.wait_ge(in_sem["mask"], 16)
            for b in range(NB):
                if b >= 2:
                    dve.wait_ge(top_sum, b - 1)
                nc.vector.tensor_tensor_reduce(out=junk[b % 2][:, :], in0=mask[:, b, :], in1=row_bc[:, :], scale=1.0, scalar=LOWEST,
                                               op0=ALU.add, op1=ALU.max, accum_out=top[:, b:b + 1]).then_inc(top_sum, 1)
            dve.wait_ge(top_sum, NB)
            nc.vector.tensor_tensor(top[:, :], top[:, :], logit2[:, 1, :], ALU.add).then_inc(small, 1)
            dve.wait_ge(small, 2)
            nc.vector.scalar_tensor_tensor(out=top[:, :], in0=top[:, :], scalar=SLOPE, in1=top[:, :], op0=ALU.mult, op1=ALU.max).then_inc(small, 1)
            dve.wait_ge(small, 3)
            nc.vector.tensor_tensor(expo[:, 0, :], logit2[:, 1, :], top[:, :], ALU.subtract).then_inc(small, 1)
            nc.vector.scalar_tensor_tensor(out=expo[:, 1, :], in0=logit2[:, 1, :], scalar=SLOPE, in1=top[:, :], op0=ALU.mult, op1=ALU.subtract).then_inc(small, 1)
            for half in range(2):
                for i in range(NB + 1):
                    c = half * NB + i
                    if i < NB:
                        dve.wait_ge(e_done, c + 1)
                        nc.vector.tensor_tensor(e1[:, i % 2, :], e1[:, i % 2, :], e2[:, i % 2, :], ALU.max).then_inc(e_max, 1)
                        dve.wait_ge(e_max, c + 1)
                        if c >= 2:
                            dve.wait_ge(p_lo, c - 1)
                        nc.vector.scalar_tensor_tensor(out=pf[:, i % 2, :], in0=e1[:, i % 2, :], scalar=1.0,
                                                       in1=countT[:, i, half * HALF:(half + 1) * HALF], op0=ALU.min, op1=ALU.mult).then_inc(p_full, 1)
                    if i >= 1:
                        dve.wait_ge(p_hi, c)
                        nc.vector.tensor_tensor(pl[half][:, i - 1, :], pf[:, (i - 1) % 2, :], ph[half][:, i - 1, :].bitcast(F32), ALU.subtract).then_inc(p_lo, 1)
            for b in range(NB):
                left, right = banks[2 * (b % 4)], banks[2 * (b % 4) + 1]
                dve.wait_ge(agg_full, b + 1)
                nc.vector.tensor_scalar(rden[:, b:b + 1], right[:, HC:HC + 1], DEN_EPS, None, ALU.add).then_inc(agg_step, 1)
                dve.wait_ge(agg_step, 2 * b + 1)
                nc.vector.reciprocal(rden[:, b:b + 1], rden[:, b:b + 1]).then_inc(agg_step, 1)
                dve.wait_ge(agg_step, 2 * b + 2)
                dve.wait_ge(xb_done, NB)
                for i, bank in enumerate((left, right)):
                    cs = slice(i * HC, (i + 1) * HC)
                    nc.vector.scalar_tensor_tensor(out=x1[:, b, cs], in0=bank[:, 0:HC], scalar=rden[:, b:b + 1], in1=x1[:, b, cs],
                                                   op0=ALU.mult, op1=ALU.add).then_inc(bank_free, 1)
                normalise(nc, dve, x1[:, b, :], stats[:, b, :, :], moments[:, b, :], root[:, b:b + 1], b, bank_free, norm_step, root_sem)

        @block.tensor
        def _(pe):
            pe.wait_ge(logit_sum, 2 * NB)
            nc.tensor.transpose(banks[0][0:NB, 0:P], logit2[:, 0, :], ident[:, :]).then_inc(turned, 1)
            pe.wait_ge(small, 5)
            nc.tensor.transpose(banks[1][0:2 * NB, 0:P], expo[:, :, :].rearrange("p k b -> p (k b)"), ident[:, :]).then_inc(turned, 1)
            pe.wait_ge(turned_out, 2)
            pe.wait_ge(g_lo, NB)
            pe.wait_ge(g_one, 2)
            for b in range(NB):
                half, c = b // HNB, b % HNB
                pe.wait_ge(p_lo, NB * (half + 1))
                if b >= 4:
                    pe.wait_ge(bank_free, 2 * (b - 3))
                for i in range(2):
                    cs = slice(i * HC, (i + 1) * HC + 2 * i)
                    for s in range(NB):
                        bs = slice(c * P, (c + 1) * P)
                        last = split_products(nc, banks[2 * (b % 4) + i][:, 0:HC + 2 * i], (ph[half][:, s, bs], pl[half][:, s, bs]),
                                              (gh[:, s, cs], gl[:, s, cs]), s == 0, s == NB - 1)
                last.then_inc(agg_full, 1)
    return x1


def graph_convolution(nc, ctx, sb, sem, banks, x1, t):
    countT, ident, dinv, gcn_bias1 = t["countT"], t["ident"], t["dinv"], t["gcn_bias1"]
    dinv_d, g_d, x1_d, gcn_w1, gcn_w2, out = t["dinv_d"], t["g_d"], t["x1_d"], t["gcn_w1"], t["gcn_w2"], t["out"]
    at = [t["FREE"]]
    x1_at = at[0]
    wh = sb("gwh", [P, PARTS, D], F32R, at)
    wl = sb("gwl", [P, PARTS, D], F32R, at)
    assert at[0] == x1_at + 4 * NB * D
    xh = sb("gxh", [P, NB, D], F32R, at)
    xl = sb("gxl", [P, NB, D], F32R, at)
    ch = sb("gch", [P, NB, HALF], F32R, at)
    cl = sb("gcl", [P, NB, HALF], F32R, at)
    y_at = at[0]
    yh = sb("gyh", [P, FB, HALF], F32R, at)
    yl = sb("gyl", [P, FB, HALF], F32R, at)
    hh = sb("ghh", [P, FB, HALF], F32R, at)
    hl = sb("ghl", [P, FB, HALF], F32R, at)
    wr = sb("gwr", [P, RAW, D], F32, at)
    dinv_bc = sb("gdinv_bc", [P, N], F32, at)
    yf = sb("gyf", [P, 2, HALF], F32, at)
    hf = sb("ghf", [P, 2, HALF], F32, at)
    cf = sb("gcf", [P, 2, HALF], F32, at)
    rows = sb("grows", [P, 2, D], F32, at)
    b2_bc = nc.alloc_sbuf_tensor_at("gb2_bc", [P, D], F32, offset=y_at + 4 * NB * HALF * 2)
    stats = sb("gstats", [P, NB, 2, 6], F32, at)
    moments = sb("gmoments", [P, NB, 2], F32, at)
    root = sb("groot", [P, NB], F32, at)
    ch2 = nc.alloc_sbuf_tensor_at("gch2", [P, NB, HALF], F32R, offset=y_at)
    cl2 = nc.alloc_sbuf_tensor_at("gcl2", [P, NB, HALF], F32R, offset=y_at + 4 * NB * HALF)
    counts = [(ch, cl, 0), (ch, cl, 1), (ch2, cl2, 0)]

    dinv_in, x1_out, x1_in, b2_in = (sem(n) for n in ("gdinv_in", "gx1_out", "gx1_in", "gb2_in"))
    w_in = [sem(f"gw_in{i}") for i in range(RAW)]
    w_hi, w_lo, w_used = sem("gw_hi"), sem("gw_lo"), sem("gw_used")
    x_f, x_hi, x_lo = sem("gx_f"), sem("gx_hi"), sem("gx_lo")
    c_step, c_f, c_hi, c_lo = sem("gc_step"), sem("gc_f"), sem("gc_hi"), sem("gc_lo")
    y_full, y_out, y_hi, y_lo = (sem(n) for n in ("gy_full", "gy_out", "gy_hi", "gy_lo"))
    h_out, h_lo = sem("gh_out"), sem("gh_lo")
    row_done = [sem("grow_s"), sem("grow_v")]
    rows_out = [sem(f"grows_out{i}") for i in range(2)]
    g_in = [sem(f"gg_in{i}") for i in range(2)]
    g_hi, g_lo, xb = sem("gg_hi"), sem("gg_lo"), sem("gxb")
    agg_full, added, norm_step, root_done, out_done = (sem(n) for n in ("gagg_full", "gadded", "gnorm_step", "groot_done", "gout_done"))
    CH = 2 * FB

    with nc.Block() as block:
        @block.sync
        def _(sp):
            sp.dma_start(x1_d.rearrange("(b p) f -> p b f", p=P), x1[:, :, :]).then_inc(x1_out, 16)
            sp.dma_start(dinv_bc[:, :], dinv_d.rearrange("b p -> (b p)").partition_broadcast(P)).then_inc(dinv_in, 16)
            for half in range(2):
                for s in range(CH):
                    g, k = half * CH + s, s % FB
                    if g >= RAW:
                        sp.wait_ge(w_lo, g - RAW + 1)
                    if s < FB:
                        sp.dma_start(wr[:, g % RAW, :].rearrange("p (f c) -> p f c", f=FB),
                                     gcn_w1[:, k * P:(k + 1) * P].rearrange("(f p) c -> p f c", p=P)).then_inc(w_in[g % RAW], 16)
                    else:
                        sp.dma_start(wr[:, g % RAW, :], gcn_w2[k * P:(k + 1) * P, :]).then_inc(w_in[g % RAW], 16)
                for c in range(HNB):
                    b = half * HNB + c
                    for i in range(2):
                        sp.wait_ge(row_done[i], b + 1)
                    sp.dma_start(g_d[b * P:(b + 1) * P, :], rows[:, b % 2, :]).then_inc(rows_out[b % 2], 16)
            sp.wait_ge(w_used, 2 * CH)
            for i in range(2):
                sp.wait_ge(rows_out[i], 16 * HNB)
            for b in range(NB):
                if b >= 2:
                    sp.wait_ge(g_lo, b - 1)
                sp.dma_start(rows[:, b % 2, :], g_d[b * P:(b + 1) * P, :]).then_inc(g_in[b % 2], 16)
                if b == 1:
                    sp.wait_ge(x1_out, 16)
                    sp.dma_start(x1[:, :, :], x1_d.rearrange("(b p) f -> p b f", p=P)).then_inc(x1_in, 16)
                    sp.dma_start(b2_bc[:, :], t["gcn_b2"].partition_broadcast(P)).then_inc(b2_in, 16)
            for n in range(NB):
                b = (n + HNB) % NB
                sp.wait_ge(norm_step, NORM_STEPS * (n + 1))
                sp.dma_start(out[b * P:(b + 1) * P, :], x1[:, b, :]).then_inc(out_done, 16)
            sp.wait_ge(out_done, 16 * NB)

        @block.gpsimd
        def _(pool):
            pool.wait_ge(x1_in, 16)
            pool.wait_ge(b2_in, 16)
            for n in range(NB):
                b = (n + HNB) % NB
                nc.gpsimd.tensor_tensor(x1[:, b, :], x1[:, b, :], b2_bc[:, :], ALU.add).then_inc(xb, 1)

        @block.scalar
        def _(act):
            def chunk_high(g):
                act.wait_ge(w_in[g % RAW], 16 * (g // RAW + 1))
                if g >= PARTS:
                    act.wait_ge(w_used, g - PARTS + 1)
                nc.scalar.copy(wh[:, g % PARTS, :], wr[:, g % RAW, :]).then_inc(w_hi, 1)

            def counts_high(m):
                for i in range(NB):
                    act.wait_ge(c_f, m * NB + i + 1)
                    nc.scalar.copy(counts[m][0][:, i, :], cf[:, i % 2, :]).then_inc(c_hi, 1)

            for b in range(NB):
                act.wait_ge(x_f, b + 1)
                nc.scalar.copy(xh[:, b, :], rows[:, b % 2, :]).then_inc(x_hi, 1)
            counts_high(0)
            act.wait_ge(x1_out, 16)
            for half in range(2):
                for f in range(FB):
                    if f < PARTS:
                        chunk_high(half * CH + f)
                    act.wait_ge(y_out, half * FB + f + 1)
                    nc.scalar.copy(yh[:, f, :], yf[:, f % 2, :]).then_inc(y_hi, 1)
                for k in range(FB):
                    n = half * FB + k
                    act.wait_ge(w_used, half * CH + k + 1)
                    if n >= 2:
                        act.wait_ge(h_lo, n - 1)
                    nc.scalar.activation(hh[:, k, :], banks[2 + k % 2][:, :], ACT.Relu, bias=gcn_bias1[:, k:k + 1])
                    nc.scalar.activation(hf[:, k % 2, :], banks[2 + k % 2][:, :], ACT.Relu, bias=gcn_bias1[:, k:k + 1]).then_inc(h_out, 1)
                    if k + PARTS < CH:
                        chunk_high(half * CH + k + PARTS)
                if half == 0:
                    counts_high(1)
                for s in range(FB + PARTS, CH):
                    chunk_high(half * CH + s)
                act.wait_ge(w_used, (half + 1) * CH)
                for c in range(HNB):
                    b = half * HNB + c
                    if b >= 2:
                        act.wait_ge(rows_out[b % 2], 16 * (b // 2))
                    nc.scalar.activation(rows[:, b % 2, 0:HC], banks[2 * c][:, 0:HC], ACT.Copy, scale=dinv[:, b:b + 1]).then_inc(row_done[0], 1)
            counts_high(2)
            for b in range(NB):
                act.wait_ge(g_in[b % 2], 16 * (b // 2 + 1))
                nc.scalar.copy(xh[:, b, :], rows[:, b % 2, :]).then_inc(g_hi, 1)
            for n in range(NB):
                b = (n + HNB) % NB
                act.wait_ge(norm_step, NORM_STEPS * n + NORM_ROOT)
                nc.scalar.activation(root[:, b:b + 1], root[:, b:b + 1], ACT.Sqrt).then_inc(root_done, 1)

        @block.vector
        def _(dve):
            def chunk_low(g):
                dve.wait_ge(w_hi, g + 1)
                nc.vector.tensor_tensor(wl[:, g % PARTS, :], wr[:, g % RAW, :], wh[:, g % PARTS, :].bitcast(F32), ALU.subtract).then_inc(w_lo, 1)

            def counts_low(m, i):
                dve.wait_ge(c_hi, m * NB + i + 1)
                nc.vector.tensor_tensor(counts[m][1][:, i, :], cf[:, i % 2, :], counts[m][0][:, i, :].bitcast(F32), ALU.subtract).then_inc(c_lo, 1)

            def build_counts(m):
                half = counts[m][2]
                for i in range(NB + 1):
                    if i < NB:
                        c = i - half * HNB
                        loops = 0 <= c < HNB
                        if m * NB + i >= 2:
                            dve.wait_ge(c_lo, m * NB + i - 1)
                        nc.vector.tensor_copy(cf[:, i % 2, :], countT[:, i, half * HALF:(half + 1) * HALF]).then_inc(c_step if loops else c_f, 1)
                        if loops:
                            dve.wait_ge(c_step, m * HNB + c + 1)
                            nc.vector.tensor_tensor(cf[:, i % 2, c * P:(c + 1) * P], cf[:, i % 2, c * P:(c + 1) * P], ident[:, :], ALU.add).then_inc(c_f, 1)
                    if i >= 1:
                        counts_low(m, i - 1)

            for b in range(NB + 1):
                if b < NB:
                    if b >= 2:
                        dve.wait_ge(x_lo, b - 1)
                    nc.vector.tensor_scalar(rows[:, b % 2, :], x1[:, b, :], dinv[:, b:b + 1], None, ALU.mult).then_inc(x_f, 1)
                if b >= 1:
                    dve.wait_ge(x_hi, b)
                    nc.vector.tensor_tensor(xl[:, b - 1, :], rows[:, (b - 1) % 2, :], xh[:, b - 1, :].bitcast(F32), ALU.subtract).then_inc(x_lo, 1)
            build_counts(0)
            dve.wait_ge(dinv_in, 16)
            for half in range(2):
                hs = slice(half * HALF, (half + 1) * HALF)
                for f in range(FB + 1):
                    if f < PARTS:
                        chunk_low(half * CH + f)
                    if f < FB:
                        n = half * FB + f
                        dve.wait_ge(y_full, n + 1)
                        if n >= 2:
                            dve.wait_ge(y_lo, n - 1)
                        nc.vector.tensor_tensor(yf[:, f % 2, :], banks[f % 2][:, :], dinv_bc[:, hs], ALU.mult).then_inc(y_out, 1)
                    if f >= 1:
                        dve.wait_ge(y_hi, half * FB + f)
                        nc.vector.tensor_tensor(yl[:, f - 1, :], yf[:, (f - 1) % 2, :], yh[:, f - 1, :].bitcast(F32), ALU.subtract).then_inc(y_lo, 1)
                for k in range(FB):
                    dve.wait_ge(h_out, half * FB + k + 1)
                    nc.vector.tensor_tensor(hl[:, k, :], hf[:, k % 2, :], hh[:, k, :].bitcast(F32), ALU.subtract).then_inc(h_lo, 1)
                    if k + PARTS < CH:
                        chunk_low(half * CH + k + PARTS)
                if half == 0:
                    build_counts(1)
                for s in range(FB + PARTS, CH):
                    chunk_low(half * CH + s)
                dve.wait_ge(w_used, (half + 1) * CH)
                for c in range(HNB):
                    b = half * HNB + c
                    if b >= 2:
                        dve.wait_ge(rows_out[b % 2], 16 * (b // 2))
                    nc.vector.tensor_scalar(rows[:, b % 2, HC:D], banks[2 * c + 1][:, 0:HC], dinv[:, b:b + 1], None, ALU.mult).then_inc(row_done[1], 1)
            build_counts(2)
            for b in range(NB):
                dve.wait_ge(g_hi, b + 1)
                nc.vector.tensor_tensor(xl[:, b, :], rows[:, b % 2, :], xh[:, b, :].bitcast(F32), ALU.subtract).then_inc(g_lo, 1)
            for n in range(NB):
                b = (n + HNB) % NB
                dve.wait_ge(agg_full, n + 1)
                dve.wait_ge(xb, n + 1)
                for i in range(2):
                    cs = slice(i * HC, (i + 1) * HC)
                    nc.vector.scalar_tensor_tensor(out=x1[:, b, cs], in0=banks[2 * (n % 4) + i][:, 0:HC], scalar=dinv[:, b:b + 1], in1=x1[:, b, cs],
                                                   op0=ALU.mult, op1=ALU.add).then_inc(added, 1)
                normalise(nc, dve, x1[:, b, :], stats[:, b, :, :], moments[:, b, :], root[:, b:b + 1], n, added, norm_step, root_done)

        @block.tensor
        def _(pe):
            pe.wait_ge(x_lo, NB)
            for half in range(2):
                def emptied(bank):
                    if half:
                        pe.wait_ge(row_done[bank % 2], bank // 2 + 1)

                pe.wait_ge(c_lo, NB * (half + 1))
                for f in range(FB):
                    if f >= 2:
                        pe.wait_ge(y_out, half * FB + f - 1)
                    else:
                        emptied(f)
                    fs = slice(f * P, (f + 1) * P)
                    for b in range(NB):
                        last = split_products(nc, banks[f % 2][:, :], (xh[:, b, fs], xl[:, b, fs]), (ch[:, b, :], cl[:, b, :]), b == 0, b == NB - 1)
                    last.then_inc(y_full, 1)
                for k in range(FB):
                    g = half * CH + k
                    pe.wait_ge(w_lo, g + 1)
                    if k == 0:
                        pe.wait_ge(y_lo, half * FB + FB)
                    if k >= 2:
                        pe.wait_ge(h_out, half * FB + k - 1)
                    else:
                        emptied(2 + k)
                    for f in range(FB):
                        fs = slice(f * P, (f + 1) * P)
                        last = split_products(nc, banks[2 + k % 2][:, :], (wh[:, g % PARTS, fs], wl[:, g % PARTS, fs]), (yh[:, f, :], yl[:, f, :]),
                                              f == 0, f == FB - 1)
                    last.then_inc(w_used, 1)
                pe.wait_ge(h_lo, half * FB + FB)
                for i in range(2):
                    if half:
                        pe.wait_ge(row_done[i], HNB)
                for k in range(FB):
                    g = half * CH + FB + k
                    pe.wait_ge(w_lo, g + 1)
                    for c in range(HNB):
                        bs = slice(c * P, (c + 1) * P)
                        for i in range(2):
                            cs = slice(i * HC, (i + 1) * HC)
                            last = split_products(nc, banks[2 * c + i][:, 0:HC], (hh[:, k, bs], hl[:, k, bs]), (wh[:, g % PARTS, cs], wl[:, g % PARTS, cs]),
                                                  k == 0, k == FB - 1)
                    last.then_inc(w_used, 1)
            pe.wait_ge(g_lo, NB)
            for n in range(NB):
                m = 1 + n // HNB
                high, low, _ = counts[m]
                c = n % HNB
                if c == 0:
                    pe.wait_ge(c_lo, NB * (m + 1))
                if n >= 4:
                    pe.wait_ge(added, 2 * (n - 3))
                bs = slice(c * P, (c + 1) * P)
                for i in range(2):
                    cs = slice(i * HC, (i + 1) * HC)
                    for s in range(NB):
                        last = split_products(nc, banks[2 * (n % 4) + i][:, 0:HC], (high[:, s, bs], low[:, s, bs]), (xh[:, s, cs], xl[:, s, cs]),
                                              s == 0, s == NB - 1)
                last.then_inc(agg_full, 1)


_INS = ["x", "src", "dst", "L0_gnn_W1", "L0_gnn_a_src1", "L0_gnn_a_dst1", "L0_gnn_b1", "L0_gnn_W2", "L0_gnn_a_src2", "L0_gnn_a_dst2",
        "L0_gnn_b2", "L1_gnn_W1", "L1_gnn_b1", "L1_gnn_W2", "L1_gnn_b2"]


def kernel(**inputs):
    import numpy as _np
    import concourse.bacc as _bacc
    from concourse import mybir as _mybir
    from concourse.bass_utils import run_bass_kernel_spmd as _run

    nc = _bacc.Bacc("TRN2", target_bir_lowering=False, num_devices=1)
    arrays, args = {}, []
    for name in _INS:
        a = _np.ascontiguousarray(inputs[name])
        arrays[f"in_{name}"] = a
        args.append(nc.dram_tensor(f"in_{name}", a.shape, _mybir.dt.from_np(a.dtype), kind="ExternalInput").ap())
    out = nc.dram_tensor("out_0", (N, D), _mybir.dt.float32, kind="ExternalOutput").ap()
    gnn_resnorm(nc, *args, out)
    r = _run(nc, [arrays], core_ids=[0])
    return r.results[0]["out_0"]
```

```python
import concourse.bass as bass
from concourse import mybir
from contextlib import ExitStack

F32 = mybir.dt.float32
F32R = mybir.dt.float32r
BF16 = mybir.dt.bfloat16
F16 = mybir.dt.float16
I16 = mybir.dt.int16
I32 = mybir.dt.int32
ALU = mybir.AluOpType
ACT = mybir.ActivationFunctionType
AX = mybir.AxisListType

P = 128
N = 1024
NB = N // P
D = 768
FB = D // P
HC = D // 2
H = 8
E = 16384
ET = E // P
HALF = N // 2
HNB = HALF // P
LN_EPS = 1e-5
DEN_EPS = 1e-16
SLOPE = 0.2
EXACT_COUNT = 4096.0
NOT_LINKED = -1e30
LOWEST = -3.0e38

SBUF_FROM = 16512
SBUF_TO = 229344


def split_products(nc, out, stationary, moving, first, last, grouped=True):
    (sh, sl), (mh, ml) = stationary, moving
    nc.tensor.matmul(out, sh, mh, start=first, stop=False, skip_group_check=not grouped)
    nc.tensor.matmul(out, sh, ml, start=False, stop=False, skip_group_check=not grouped)
    return nc.tensor.matmul(out, sl, mh, start=False, stop=last, skip_group_check=not grouped)


def gnn_resnorm(nc, x, src, dst, gat_w1, gat_a_src1, gat_a_dst1, gat_b1, gat_w2, gat_a_src2, gat_a_dst2, gat_b2,
                gcn_w1, gcn_b1, gcn_w2, gcn_b2, out):
    ctx = ExitStack()
    held, stage = [], [0]

    def sem(name):
        held.append(nc.alloc_semaphore(name=f"{name}_{stage[0]}"))
        return held[-1]

    def end_of_stage():
        nc.clear_and_free_semaphores(held)
        held.clear()
        stage[0] += 1
        nc.all_engine_barrier()

    with ctx:
        place = [SBUF_FROM]

        def sb(name, shape, dt, at=place):
            size = 2 if dt in (BF16, F16, I16) else 4
            for n in shape[1:]:
                size *= n
            t = nc.alloc_sbuf_tensor_at(name, shape, dt, offset=at[0])
            at[0] += -(-size // 32) * 32
            assert at[0] <= SBUF_TO, (name, at[0])
            return t

        countT = sb("countT", [P, NB, N], I16)
        ident = sb("ident", [P, P], F32)
        ones = sb("ones", [P, P], F32)
        zero_r = sb("zero_r", [P, P], F32R)
        src_logit = sb("src_logit", [P, H, NB], F32)
        src_logit02 = sb("src_logit02", [P, H, NB], F32)
        bias1 = sb("bias1", [P, H * FB], F32)
        dst_logit = sb("dst_logit", [P, H, NB], F32)
        a2_cols = sb("a2_cols", [P, FB, 2], F32)
        many_i = sb("many_i", [1, 8], I32)
        dinv = sb("dinv", [P, NB], F32)
        gcn_bias1 = sb("gcn_bias1", [P, FB], F32)
        FREE = place[0]
        xh = sb("xh", [P, NB, D], F32R)
        xl = sb("xl", [P, NB, D], F32R)
        FREE_BESIDE_X = place[0]

        banks = [ctx.enter_context(nc.psum_tensor(f"bank{i}", [P, 512], F32)) for i in range(8)]

        logits_d = nc.dram_tensor("logits_scratch", [2 * H, N], F32, kind="Internal").ap()
        expo_d = nc.dram_tensor("expo_scratch", [2 * HNB, P], F32, kind="Internal").ap()
        logits2_d = nc.dram_tensor("logits2_scratch", [NB, P], F32, kind="Internal").ap()
        expo2_d = nc.dram_tensor("expo2_scratch", [2, NB, P], F32, kind="Internal").ap()
        dinv_d = nc.dram_tensor("dinv_scratch", [NB, P], F32, kind="Internal").ap()
        mask_d = nc.dram_tensor("mask_scratch", [P, NB * N], BF16, kind="Internal").ap()
        h2_d = nc.dram_tensor("h2_scratch", [N, D], F32, kind="Internal").ap()
        x1_d = nc.dram_tensor("x1_scratch", [N, D], F32, kind="Internal").ap()

        graph_and_logits(nc, sb, sem, FREE_BESIDE_X, banks, locals())
        end_of_stage()
        attention_heads(nc, sb, sem, FREE_BESIDE_X, banks, locals())
        hidden_to_rows(nc, ctx, sb, sem, FREE, banks, 1, locals())
        end_of_stage()
        at = [FREE]
        x1_at = at[0]
        x1 = sb("x1", [P, NB, D], F32, at)
        sx_at = at[0]
        sxh = sb("sxh", [P, NB, D], F32R, at)
        sxl = sb("sxl", [P, NB, D], F32R, at)
        counts_at = at[0]
        ch = sb("ch", [P, NB, HALF], F32R, at)
        cl = sb("cl", [P, NB, HALF], F32R, at)
        FREE_LATE = at[0]
        second_attention(nc, sb, sem, banks, locals())
        end_of_stage()
        graph_convolution(nc, sb, sem, banks, locals())


def graph_and_logits(nc, sb, sem, FREE, banks, t):
    x, countT, ident, ones, zero_r, xh, xl = t["x"], t["countT"], t["ident"], t["ones"], t["zero_r"], t["xh"], t["xl"]
    src_logit, src_logit02, dst_logit, bias1 = t["src_logit"], t["src_logit02"], t["dst_logit"], t["bias1"]
    dinv, gcn_bias1, many_i, a2_cols = t["dinv"], t["gcn_bias1"], t["many_i"], t["a2_cols"]
    logits_d, dinv_d, mask_d, gat_w1 = t["logits_d"], t["dinv_d"], t["mask_d"], t["gat_w1"]

    at = [FREE]
    xr = sb("pro_x", [P, NB, D], F32, at)
    xT = sb("pro_xT", [P, FB, N], F32, at)
    w = [sb(f"pro_w{i}", [P, FB, D], F32, at) for i in range(2)]
    a_bc = sb("a_bc", [P, 2, 2, D], F32, at)
    product = sb("product", [P, 2, D], F32, at)
    junk = sb("pro_junk", [P, 2, D], BF16, at)
    hot_src = [sb(f"hot_src{i}", [P, N], BF16, at) for i in range(4)]
    hot_dst = [sb(f"hot_dst{i}", [P, P], BF16, at) for i in range(4)]
    node_h = sb("node_h", [P, N], F16, at)
    node_i = nc.alloc_sbuf_tensor_at("node_i", [P, N], I32, offset=at[0])
    logitT = nc.alloc_sbuf_tensor_at("logitT", [2 * H, N], F32, offset=at[0])
    count = [sb(f"count{i}", [P, N], F32, at) for i in range(2)]
    mask = sb("mask", [P, 2, N], BF16, at)
    dinvT = nc.alloc_sbuf_tensor_at("dinvT", [NB, P], F32, offset=at[0])
    edge_i = sb("edge_i", [P, 2, P], I32, at)
    edge_f = sb("edge_f", [P, 2, P], F32, at)
    edgeT = sb("edgeT", [P, 2, 2 * P], F32, at)
    quad_i = sb("quad_i", [P, P], I32, at)
    quad = sb("quad", [P, P], F32, at)
    quad_end = sb("quad_end", [P, P], F32, at)
    block_i = sb("block_i", [P, NB], I32, at)
    block_f = sb("block_f", [P, NB], F32, at)
    span = sb("span", [P, 2], F32, at)
    touch = sb("touch", [P, 2, NB], F32, at)
    touchT = sb("touchT", [P, 2, P], F32, at)
    range_f = sb("range_f", [P, 4], F32, at)
    range_i = sb("range_i", [P, 2], I32, at)
    zero_b = sb("zero_b", [P, 512], BF16, at)
    rows_in = sb("rows_in", [H * FB, P], F32, at)
    small_in = sb("small_in", [FB, 3, P], F32, at)
    v = sb("v", [P, FB, 2 * H], F32, at)
    logit = sb("logit", [P, NB, 2 * H], F32, at)
    deg_parts = sb("deg_parts", [P, NB, 2], F32, at)
    deg = sb("deg", [P, NB], F32, at)
    many = sb("many", [P, NB + 1], F32, at)

    edges_in, small_rows_in = sem("edges_in"), sem("small_rows_in")
    x_in = sem("x_in")
    w_in = [sem(f"w_in{i}") for i in range(2)]
    a_in = [sem(f"a_in{i}") for i in range(2)]
    product_full, product_sum, v_sum = sem("product_full"), sem("product_sum"), sem("v_sum")
    const_g, const_v, edge_cast, edgeT_full, edgeT_done = (sem(n) for n in ("const_g", "const_v", "edge_cast", "edgeT_full", "edgeT_done"))
    span_done, span_full, range_done = sem("span_done"), sem("span_full"), sem("range_done")
    hot_ready = [sem(f"hot_ready{b}") for b in range(NB)]
    hot_free = [sem(f"hot_free{b}") for b in range(NB)]
    count_full, count_out, mask_done = sem("count_full"), sem("count_out"), sem("mask_done")
    turned, turned_out = sem("turned"), sem("turned_out")
    x_hi, x_lo = sem("x_hi"), sem("x_lo")
    cols_full, cols_done = sem("cols_full"), sem("cols_done")
    logitT_full, logitT_done, logit_full, logit_done, logits_out = (sem(n) for n in ("logitT_full", "logitT_done", "logit_full", "logit_done", "logits_out"))
    deg_step, root_done, dinv_done, dinvT_full, dinvT_done, dinv_out = (sem(n) for n in ("deg_step", "root_done", "dinv_done", "dinvT_full", "dinvT_done", "dinv_out"))
    mask_out = [sem(f"mask_out{i}") for i in range(2)]
    many_step, many_full, many_done = sem("many_step"), sem("many_full"), sem("many_done")

    XG, CG = 2 * FB, 2
    order = [[("x", g, 0) for g in range(2 * b, min(2 * b + 2, XG))] + [("count", b, i) for i in range(CG)] for b in range(NB)]
    group = {g: n for n, g in enumerate(g for of_block in order for g in of_block)}
    BY_VECTOR = 2

    with nc.Block() as block:
        @block.sync
        def _(sp):
            sp.dma_start(edge_i[:, 0, :], t["src"].rearrange("(t p) -> t p", p=P)).then_inc(edges_in, 16)
            sp.dma_start(edge_i[:, 1, :], t["dst"].rearrange("(t p) -> t p", p=P)).then_inc(edges_in, 16)
            sp.dma_start(xr[:, :, :], x.rearrange("(b p) f -> p b f", p=P)).then_inc(x_in, 16)
            sp.dma_start(rows_in[:, :], t["gat_b1"].rearrange("(k p) -> k p", p=P)).then_inc(small_rows_in, 16)
            for i, name in enumerate(("gat_a_src2", "gat_a_dst2")):
                sp.dma_start(small_in[:, i, :], t[name].rearrange("a (k p) -> (a k) p", p=P)).then_inc(small_rows_in, 16)
            sp.dma_start(small_in[:, 2, :], t["gcn_b1"].rearrange("(k p) -> k p", p=P)).then_inc(small_rows_in, 16)
            for h in range(NB + 1):
                if h < H:
                    if h >= 2:
                        sp.wait_ge(v_sum, (h - 1) * 2 * BY_VECTOR)
                        sp.wait_ge(product_sum, (h - 1) * 2 * (FB - BY_VECTOR))
                    for k, name in enumerate(("gat_a_src1", "gat_a_dst1")):
                        sp.dma_start(a_bc[:, h % 2, k, :], t[name][h, :].partition_broadcast(P)).then_inc(a_in[h % 2], 16)
                    sp.dma_start(w[h % 2][:, :, :], gat_w1[:, h * D:(h + 1) * D].rearrange("(f p) c -> p f c", p=P)).then_inc(w_in[h % 2], 16)
                if h >= 1:
                    b = h - 1
                    sp.wait_ge(mask_done, b + 1)
                    sp.dma_start(mask_d[:, b * N:(b + 1) * N], mask[:, b % 2, :]).then_inc(mask_out[b % 2], 16)
            sp.wait_ge(dinvT_done, 1)
            sp.dma_start(dinv_d, dinvT[:, :]).then_inc(dinv_out, 16)
            sp.wait_ge(logitT_done, 2)
            sp.dma_start(logits_d, logitT[:, :]).then_inc(logits_out, 16)
            for i in range(2):
                sp.wait_ge(mask_out[i], 16 * NB // 2)
            sp.wait_ge(dinv_out, 16)
            sp.wait_ge(logits_out, 16)

        @block.gpsimd
        def _(pool):
            nc.gpsimd.memset(ident[:, :], 0.0).then_inc(const_g, 1)
            nc.gpsimd.iota(node_i[:, :], pattern=[[1, N]], base=0, channel_multiplier=0).then_inc(const_g, 1)
            nc.gpsimd.iota(quad_i[:, :], pattern=[[1, ET // 4], [0, 4]], base=0, channel_multiplier=0).then_inc(const_g, 1)
            nc.gpsimd.iota(block_i[:, :], pattern=[[P, NB]], base=0, channel_multiplier=0).then_inc(const_g, 1)
            pool.wait_ge(const_g, 4)
            nc.gpsimd.affine_select(out=ident[:, :], in_=ident[:, :], compare_op=ALU.not_equal, fill=1.0, base=0,
                                    pattern=[[-1, P]], channel_multiplier=1).then_inc(const_g, 1)
            n = 0
            for h in range(H):
                pool.wait_ge(w_in[h % 2], 16 * (h // 2 + 1))
                pool.wait_ge(a_in[h % 2], 32 * (h // 2 + 1))
                for f in range(BY_VECTOR, FB):
                    for k in range(2):
                        if n >= 2:
                            pool.wait_ge(product_sum, n - 1)
                        nc.gpsimd.tensor_tensor(product[:, n % 2, :], w[h % 2][:, f, :], a_bc[:, h % 2, k, :], ALU.mult).then_inc(product_full, 1)
                        n += 1

        @block.vector
        def _(dve):
            nc.vector.memset(zero_b[:, :], 0.0).then_inc(const_v, 1)
            nc.vector.memset(ones[:, :], 1.0).then_inc(const_v, 1)
            dve.wait_ge(const_g, 5)
            nc.vector.tensor_copy(node_h[:, :], node_i[:, :]).then_inc(const_v, 1)
            nc.vector.tensor_copy(quad[:, :], quad_i[:, :]).then_inc(const_v, 1)
            nc.vector.tensor_copy(block_f[:, :], block_i[:, :]).then_inc(const_v, 1)
            dve.wait_ge(const_v, 5)
            nc.vector.tensor_scalar(quad_end[:, :], quad[:, :], -1.0, float(ET // 4), ALU.mult, ALU.add).then_inc(const_v, 1)
            nc.vector.tensor_scalar(zero_r[:, :], ones[:, :], 0.0, None, ALU.mult).then_inc(const_v, 1)
            dve.wait_ge(const_v, 7)
            nc.vector.tensor_scalar(quad[:, :], quad[:, :], 1.0, None, ALU.add).then_inc(const_v, 1)
            dve.wait_ge(edges_in, 32)
            nc.vector.tensor_copy(edge_f[:, :, :], edge_i[:, :, :]).then_inc(edge_cast, 1)
            dve.wait_ge(edge_cast, 1)
            nc.vector.tensor_reduce(span[:, 0:1], edge_f[:, 1, :], AX.X, ALU.min).then_inc(span_done, 1)
            nc.vector.tensor_reduce(span[:, 1:2], edge_f[:, 1, :], AX.X, ALU.max).then_inc(span_done, 1)
            dve.wait_ge(span_done, 2)
            nc.vector.tensor_scalar(touch[:, 0, :], block_f[:, :], span[:, 0:1], float(-P), ALU.subtract, ALU.is_gt).then_inc(span_done, 1)
            nc.vector.tensor_scalar(touch[:, 1, :], block_f[:, :], span[:, 1:2], None, ALU.is_le).then_inc(span_done, 1)
            dve.wait_ge(span_done, 4)
            nc.vector.tensor_tensor(touch[:, 0, :], touch[:, 0, :], touch[:, 1, :], ALU.mult).then_inc(span_done, 1)
            dve.wait_ge(edgeT_full, 2)
            nc.vector.tensor_copy(edgeT[:, 0, 0:P], banks[5][:, 0:P]).then_inc(edgeT_done, 1)
            nc.vector.tensor_copy(edgeT[:, 1, 0:P], banks[6][:, 0:P]).then_inc(edgeT_done, 1)
            dve.wait_ge(span_full, 1)
            dve.wait_ge(const_v, 8)
            nc.vector.tensor_tensor(touchT[0:NB, 0, :], banks[7][0:NB, 0:P], quad_end[0:NB, :], ALU.mult).then_inc(range_done, 1)
            nc.vector.tensor_tensor(touchT[0:NB, 1, :], banks[7][0:NB, 0:P], quad[0:NB, :], ALU.mult).then_inc(range_done, 1)
            dve.wait_ge(range_done, 2)
            nc.vector.tensor_reduce(range_f[0:NB, 0:1], touchT[0:NB, 0, :], AX.X, ALU.max).then_inc(range_done, 1)
            nc.vector.tensor_reduce(range_f[0:NB, 1:2], touchT[0:NB, 1, :], AX.X, ALU.max).then_inc(range_done, 1)
            dve.wait_ge(range_done, 4)
            nc.vector.tensor_scalar(range_f[0:NB, 0:1], range_f[0:NB, 0:1], 1.0, -1.0, ALU.max, ALU.mult).then_inc(range_done, 1)
            dve.wait_ge(range_done, 5)
            nc.vector.tensor_scalar(range_f[0:NB, 2:3], range_f[0:NB, 0:1], float(ET // 4), None, ALU.add).then_inc(range_done, 1)
            dve.wait_ge(range_done, 6)
            nc.vector.tensor_tensor(range_f[0:NB, 3:4], range_f[0:NB, 1:2], range_f[0:NB, 2:3], ALU.subtract).then_inc(range_done, 1)
            dve.wait_ge(range_done, 7)
            nc.vector.tensor_scalar(range_f[0:NB, 3:4], range_f[0:NB, 3:4], 1.0, None, ALU.max).then_inc(range_done, 1)
            dve.wait_ge(range_done, 8)
            nc.vector.tensor_copy(range_i[0:NB, :], range_f[0:NB, 2:4]).then_inc(range_done, 1)
            dve.wait_ge(range_done, 9)
            dve.wait_ge(edgeT_done, 2)

            def beside_block(b):
                dve.wait_ge(w_in[b % 2], 16 * (b // 2 + 1))
                dve.wait_ge(a_in[b % 2], 32 * (b // 2 + 1))
                for f in range(BY_VECTOR):
                    for k in range(2):
                        n = 2 * (b * BY_VECTOR + f) + k
                        if n >= 2:
                            dve.wait_ge(v_sum, n - 1)
                        nc.vector.tensor_tensor_reduce(out=junk[:, k, :], in0=w[b % 2][:, f, :], in1=a_bc[:, b % 2, k, :], scale=1.0, scalar=0.0,
                                                       op0=ALU.mult, op1=ALU.add, accum_out=v[:, f, 2 * b + k:2 * b + k + 1]).then_inc(v_sum, 1)
                dve.wait_ge(count_out, 2 * b + 2)
                if b >= 2:
                    dve.wait_ge(mask_out[b % 2], 16 * (b // 2))
                nc.vector.tensor_scalar(mask[:, b % 2, :], count[b % 2][:, :], 0.0, NOT_LINKED, ALU.is_equal, ALU.mult).then_inc(mask_done, 1)
                dve.wait_ge(x_hi, b + 1)
                nc.vector.tensor_tensor(xl[:, b, :], xr[:, b, :], xh[:, b, :].bitcast(F32), ALU.subtract).then_inc(x_lo, 1)

            for b in range(NB):
                first_quad = dve.value_load(range_i[b:b + 1, 0:1], min_val=0, max_val=ET // 4 - 1)
                quads = dve.value_load(range_i[b:b + 1, 1:2], min_val=1, max_val=ET // 4)
                with dve.Fori(0, quads) as q:
                    for j in range(4):
                        tile = (q + first_quad) * 4 + j
                        dve.wait_ge(hot_free[b], q * 4 + (j + 1))
                        nc.vector.tensor_scalar(hot_src[j][:, :], node_h[:, :], edgeT[:, 0, bass.ds(tile, 1)], None, ALU.is_equal)
                        nc.vector.tensor_scalar(hot_dst[j][:, :], node_h[:, b * P:(b + 1) * P], edgeT[:, 1, bass.ds(tile, 1)], None,
                                                ALU.is_equal).then_inc(hot_ready[b], 1)
                beside_block(b)
            nc.vector.tensor_tensor(deg[:, :], deg_parts[:, :, 0], deg_parts[:, :, 1], ALU.add).then_inc(deg_step, 1)
            dve.wait_ge(deg_step, 1)
            nc.vector.tensor_scalar(deg[:, :], deg[:, :], 1.0, None, ALU.add).then_inc(deg_step, 1)
            dve.wait_ge(deg_step, 2)
            nc.vector.tensor_scalar(many[:, 0:NB], deg[:, :], EXACT_COUNT, None, ALU.is_gt).then_inc(many_step, 1)
            dve.wait_ge(many_step, 1)
            nc.vector.tensor_reduce(many[:, NB:NB + 1], many[:, 0:NB], AX.X, ALU.add).then_inc(many_step, 1)
            dve.wait_ge(root_done, 1)
            nc.vector.reciprocal(dinv[:, :], deg[:, :]).then_inc(dinv_done, 1)
            dve.wait_ge(many_full, 1)
            nc.vector.tensor_copy(many_i[0:1, 0:1], banks[5][0:1, 0:1]).then_inc(many_done, 1)
            dve.wait_ge(logit_full, 1)
            nc.vector.tensor_copy(logit[:, :, :], banks[6][:, 0:NB * 2 * H].rearrange("p (b r) -> p b r", b=NB)).then_inc(logit_done, 1)
            dve.wait_ge(logit_done, 1)
            by_head = logit[:, :, :].rearrange("p b (h k) -> p k h b", k=2)
            nc.vector.tensor_copy(src_logit[:, :, :], by_head[:, 0, :, :]).then_inc(logit_done, 1)
            nc.vector.tensor_scalar(src_logit02[:, :, :], by_head[:, 0, :, :], SLOPE, None, ALU.mult).then_inc(logit_done, 1)
            nc.vector.tensor_copy(dst_logit[:, :, :], by_head[:, 1, :, :]).then_inc(logit_done, 1)

        @block.scalar
        def _(act):
            def group_out(g):
                kind, n, i = g
                bank = banks[5 + group[g] % 3]
                act.wait_ge(turned, group[g] + 1)
                if kind == "x":
                    to, frm = xT[:, n // 2, (n % 2) * 512:(n % 2 + 1) * 512], bank[:, :]
                else:
                    to, frm = countT[:, 4 * i:4 * i + 4, n * P:(n + 1) * P], bank[:, :].rearrange("p (s d) -> p s d", s=4)
                nc.scalar.copy(to, frm).then_inc(turned_out, 1)

            def sum_products(h, fs):
                for f in fs:
                    for k in range(2):
                        n = 2 * (h * (FB - BY_VECTOR) + f - BY_VECTOR) + k
                        act.wait_ge(product_full, n + 1)
                        nc.scalar.activation(product[:, n % 2, :], product[:, n % 2, :], ACT.Copy,
                                             accum_out=v[:, f, 2 * h + k:2 * h + k + 1]).then_inc(product_sum, 1)

            act.wait_ge(cols_full, 1)
            nc.scalar.copy(bias1[:, :], banks[4][:, 0:H * FB]).then_inc(cols_done, 1)
            nc.scalar.copy(a2_cols[:, :, :], banks[4][:, 256:256 + 2 * FB].rearrange("p (k c) -> p c k", k=2)).then_inc(cols_done, 1)
            nc.scalar.copy(gcn_bias1[:, :], banks[4][:, 256 + 2 * FB:256 + 3 * FB]).then_inc(cols_done, 1)
            act.wait_ge(x_in, 16)
            for b in range(NB):
                nc.scalar.copy(xh[:, b, :], xr[:, b, :]).then_inc(x_hi, 1)
                sum_products(b, range(BY_VECTOR, BY_VECTOR + 2))
                act.wait_ge(count_full, b + 1)
                if b >= 2:
                    act.wait_ge(turned, group[("count", b - 2, 1)] + 1)
                    act.wait_ge(mask_done, b - 1)
                for i in range(2):
                    nc.scalar.activation(count[b % 2][:, i * 512:(i + 1) * 512], banks[2 * (b % 2) + i][:, :], ACT.Copy,
                                         accum_out=deg_parts[:, b, i:i + 1]).then_inc(count_out, 1)
                for g in order[b]:
                    group_out(g)
                sum_products(b, range(BY_VECTOR + 2, FB))
            act.wait_ge(many_step, 2)
            nc.scalar.activation(deg[:, :], deg[:, :], ACT.Sqrt).then_inc(root_done, 1)
            act.wait_ge(dinvT_full, 1)
            nc.scalar.copy(dinvT[:, :], banks[7][0:NB, 0:P]).then_inc(dinvT_done, 1)
            for i in range(2):
                act.wait_ge(logitT_full, i + 1)
                nc.scalar.copy(logitT[:, i * 512:(i + 1) * 512], banks[i][0:2 * H, :]).then_inc(logitT_done, 1)

        @block.tensor
        def _(pe):
            pe.wait_ge(const_g, 5)
            pe.wait_ge(edge_cast, 1)
            for i in range(2):
                nc.tensor.transpose(banks[5 + i][:, 0:P], edge_f[:, i, :], ident[:, :]).then_inc(edgeT_full, 1)
            pe.wait_ge(span_done, 5)
            nc.tensor.transpose(banks[7][0:NB, 0:P], touch[:, 0, :], ident[:, :]).then_inc(span_full, 1)
            pe.wait_ge(small_rows_in, 64)
            K = H * FB
            nc.tensor.transpose(banks[4][:, 0:K], rows_in[:, :], ident[0:K, 0:K])
            for i in range(3):
                last = nc.tensor.transpose(banks[4][:, 256 + i * FB:256 + (i + 1) * FB], small_in[:, i, :], ident[0:FB, 0:FB])
            last.then_inc(cols_full, 1)

            def turn(g):
                kind, n, i = g
                at = group[g]
                if at >= 3:
                    pe.wait_ge(turned_out, at - 2)
                bank = banks[5 + at % 3]
                if kind == "x":
                    parts = [xr[:, 4 * (n % 2) + j, (n // 2) * P:(n // 2 + 1) * P] for j in range(4)]
                else:
                    parts = [count[n % 2][:, (4 * i + j) * P:(4 * i + j + 1) * P] for j in range(4)]
                for j, part in enumerate(parts):
                    last = nc.tensor.transpose(bank[:, j * P:(j + 1) * P], part, ident[:, :])
                last.then_inc(turned, 1)

            pe.wait_ge(x_in, 16)
            pe.wait_ge(range_done, 9)
            for b in range(NB):
                quads = pe.value_load(range_i[b:b + 1, 1:2], min_val=1, max_val=ET // 4)
                pair = banks[2 * (b % 2)], banks[2 * (b % 2) + 1]
                if b >= 2:
                    pe.wait_ge(count_out, 2 * (b - 1))
                for i in range(2):
                    last = nc.tensor.matmul(pair[i][:, :], zero_b[:, 0:P], zero_b[:, :], start=True, stop=False, skip_group_check=True)
                last.then_inc(hot_free[b], 4)
                with pe.Fori(0, quads) as q:
                    for j in range(4):
                        pe.wait_ge(hot_ready[b], q * 4 + (j + 1))
                        for i in range(2):
                            last = nc.tensor.matmul(pair[i][:, :], hot_dst[j][:, :], hot_src[j][:, i * 512:(i + 1) * 512],
                                                    start=False, stop=False, skip_group_check=True)
                        last.then_inc(hot_free[b], 1)
                for i in range(2):
                    last = nc.tensor.matmul(pair[i][:, :], zero_b[:, 0:P], zero_b[:, :], start=False, stop=True, skip_group_check=True)
                last.then_inc(count_full, 1)
                for g in order[b]:
                    if g == ("count", b, 0):
                        pe.wait_ge(count_out, 2 * b + 2)
                    turn(g)
            pe.wait_ge(turned_out, len(group))
            pe.wait_ge(dinv_done, 1)
            nc.tensor.transpose(banks[7][0:NB, 0:P], dinv[:, :], ident[:, :]).then_inc(dinvT_full, 1)
            nc.tensor.matmul(banks[5][0:1, 0:1], many[:, NB:NB + 1], ones[:, 0:1], start=True, stop=True).then_inc(many_full, 1)
            pe.wait_ge(v_sum, 2 * H * BY_VECTOR)
            pe.wait_ge(product_sum, 2 * H * (FB - BY_VECTOR))
            for i in range(2):
                for f in range(FB):
                    last = nc.tensor.matmul(banks[i][0:2 * H, :], v[:, f, :], xT[:, f, i * 512:(i + 1) * 512], start=(f == 0), stop=(f == FB - 1))
                last.then_inc(logitT_full, 1)
            for b in range(NB):
                if b % 4 == 0:
                    pe.wait_ge(logitT_done, b // 4 + 1)
                last = nc.tensor.transpose(banks[6][:, b * 2 * H:(b + 1) * 2 * H], logitT[:, b * P:(b + 1) * P], ident[0:2 * H, 0:2 * H])
            last.then_inc(logit_full, 1)


STEPS = [("B", 0), ("B", 1)] + [s for k in range(2, FB) for s in (("C", k - 2), ("B", k))] + [("C", FB - 2), ("C", FB - 1)]
AT = {s: n for n, s in enumerate(STEPS)}
NS = len(STEPS)
RAW, PARTS = 3, 4


def attention_heads(nc, sb, sem, FREE, banks, t):
    countT, ident, ones, zero_r, xh, xl = t["countT"], t["ident"], t["ones"], t["zero_r"], t["xh"], t["xl"]
    src_logit, src_logit02, dst_logit, bias1 = t["src_logit"], t["src_logit02"], t["dst_logit"], t["bias1"]
    logits_d, expo_d, mask_d, h2_d = t["logits_d"], t["expo_d"], t["mask_d"], t["h2_d"]
    gat_w1, gat_w2 = t["gat_w1"], t["gat_w2"]
    at = [FREE]
    ph = sb("ph", [P, NB, HALF], F32R, at)
    pl = sb("pl", [P, NB, HALF], F32R, at)
    yh = sb("yh", [P, FB, HALF], F32R, at)
    yl = sb("yl", [P, FB, HALF], F32R, at)
    h_at = at[0]
    hh = sb("hh", [P, 3, HALF], F32R, at)
    hl = sb("hl", [P, 3, HALF], F32R, at)
    wh = sb("wh", [P, PARTS, D], F32R, at)
    wl = sb("wl", [P, PARTS, D], F32R, at)
    wr = sb("wr", [P, RAW, D], F32, at)
    expo_bc = sb("expo_bc", [P, 2, HALF], F32, at)
    psum_rows = sb("psum_rows", [P, HALF], F32, at)
    rden = sb("rden", [P, HALF], F32, at)
    pf = sb("pf", [P, 2, HALF], F32, at)
    e_at = at[0]
    e1 = sb("e1", [P, 2, HALF], F32, at)
    e2 = sb("e2", [P, 2, HALF], F32, at)
    r_at = at[0]
    he = sb("he", [P, 2, HALF], F32, at)
    hr = sb("hr", [P, 2, HALF], F32, at)
    mask = sb("mask_half", [P, HNB, N], BF16, at)
    top = sb("top", [P, HNB], F32, at)
    expo = sb("expo", [P, 2, HNB], F32, at)
    expoT = sb("expoT", [2 * HNB, P], F32, at)
    row_bc = nc.alloc_sbuf_tensor_at("row_bc", [P, N], F32, offset=e_at)
    yf = nc.alloc_sbuf_tensor_at("yf", [P, 2, HALF], F32, offset=e_at + 4 * N)
    junk = nc.alloc_sbuf_tensor_at("junk", [P, HNB, N], BF16, offset=r_at)
    rows = nc.alloc_sbuf_tensor_at("rows", [P, 2, D], F32, offset=r_at)
    cols = nc.alloc_sbuf_tensor_at("cols", [P, FB, HALF], F32, offset=h_at)

    U = 2 * H
    w_in = [sem(f"w_in{i}") for i in range(RAW)]
    w_hi = sem("w_hi")
    w_lo = sem("w_lo")
    w_used = sem("w_used")
    row_in, mask_in, top_sum, expo_step = sem("row_in"), sem("mask_in"), sem("top_sum"), sem("expo_step")
    expoT_full, expoT_out, expo_saved, expo_in = sem("expoT_full"), sem("expoT_out"), sem("expo_saved"), sem("expo_in")
    e_done, e_max, p_hi = sem("e_done"), sem("e_max"), sem("p_hi")
    p_full = sem("p_full")
    p_lo = sem("p_lo")
    p_sum = sem("p_sum")
    den_full, den_out, rden_done = sem("den_full"), sem("den_out"), sem("rden_done")
    y_full, y_hi = sem("y_full"), sem("y_hi")
    y_out = sem("y_out")
    y_lo = sem("y_lo")
    h_out = sem("h_out")
    h_sum, h_hi = sem("h_sum"), sem("h_hi")
    h_lo = sem("h_lo")
    cols_done, rows_turned, rows_done, cols_saved = sem("cols_done"), sem("rows_turned"), sem("rows_done"), sem("cols_saved")
    rows_saved = [sem(f"rows_saved{i}") for i in range(2)]

    def units(engine, unit):
        with engine.Fori(0, H - 1) as h:
            unit(h, 0, h, (0, h + 1), False)
        unit(H - 1, 0, H - 1, (1, 0), False)
        unit(H, 1, 0, (1, 1), True)
        with engine.Fori(1, H - 1) as h:
            unit(h + H, 1, h, (1, h + 1), False)
        unit(U - 1, 1, H - 1, None, False)

    def work_bank(kind, k=0):
        at = {"sums": 0, "A": 1 + k + (k >= 3), "exponents": 4, "B": 8 + k}[kind]
        return banks[6 + at % 2]

    with nc.Block() as block:
        @block.sync
        def _(sp):
            def load_row(h):
                sp.dma_start(row_bc[:, :], logits_d[bass.ds(h * 2, 1), :].rearrange("a n -> (a n)").partition_broadcast(P)).then_inc(row_in, 16)

            def load_mask(half):
                sp.dma_start(mask[:, :, :].rearrange("p b n -> p (b n)"), mask_d[:, half * HNB * N:(half + 1) * HNB * N]).then_inc(mask_in, 16)

            def exponents_to_all(v):
                sp.wait_ge(expoT_out, v + 1)
                sp.dma_start(expo_d, expoT[:, :]).then_inc(expo_saved, 16)
                sp.wait_ge(expo_saved, v * 16 + 16)
                sp.dma_start(expo_bc[:, :, :].rearrange("p k n -> p (k n)"), expo_d.rearrange("k p -> (k p)").partition_broadcast(P)).then_inc(expo_in, 16)

            def load_chunk(u, h, s):
                kind, k = STEPS[s]
                i = s % RAW
                sp.wait_ge(w_lo, u * NS + (s + 1))
                if kind == "B":
                    sp.dma_start(wr[:, i, :].rearrange("p (f c) -> p f c", f=FB),
                                 gat_w1[:, bass.ds(h * D + k * P, P)].rearrange("(f p) c -> p f c", p=P)).then_inc(w_in[i], 16)
                else:
                    sp.dma_start(wr[:, i, :], gat_w2[bass.ds(h * D + k * P, P), :]).then_inc(w_in[i], 16)

            def unit(u, half, h, following, leaving):
                if following:
                    sp.wait_ge(p_lo, u * NB + (NB + 2))
                    load_row(following[1])
                    if following[0] != half:
                        sp.wait_ge(top_sum, (u + 1) * HNB)
                        load_mask(following[0])
                for s in range(NS):
                    load_chunk(u, h, s)
                    if s == 5 and following:
                        exponents_to_all(u + 1)
                    if s == 5 and leaving:
                        for b in range(HNB):
                            sp.wait_ge(rows_done, 2 * b + 2)
                            sp.dma_start(h2_d[b * P:(b + 1) * P, :], rows[:, b % 2, :]).then_inc(rows_saved[b % 2], 16)

            load_row(0)
            load_mask(0)
            exponents_to_all(0)
            units(sp, unit)
            for i in range(2):
                sp.wait_ge(rows_saved[i], 16 * HNB // 2)

        @block.gpsimd
        def _(pool):
            def sum_rows(v):
                for i in range(1, NB):
                    pool.wait_ge(p_full, v * NB + (i + 3))
                    if i >= 2:
                        pool.wait_ge(p_sum, v * 7 + (i + 1))
                    before = pf[:, 0, :] if i == 1 else psum_rows[:, :]
                    nc.gpsimd.tensor_tensor(psum_rows[:, :], before, pf[:, i % 2, :], ALU.add).then_inc(p_sum, 1)

            def unit(u, half, h, following, leaving):
                if following:
                    pool.wait_ge(den_full, u + 1)
                    sum_rows(u + 1)

            pool.sem_inc(p_sum, 2)
            sum_rows(0)
            units(pool, unit)

        @block.scalar
        def _(act):
            def exponents_out(v):
                act.wait_ge(expoT_full, v + 1)
                nc.scalar.copy(expoT[:, :], work_bank("exponents")[0:2 * HNB, 0:P]).then_inc(expoT_out, 1)

            def exponentials(v, h, i):
                act.wait_ge(p_full, v * NB + (i + 1))
                nc.scalar.activation(e1[:, i % 2, :], expo_bc[:, 0, :], ACT.Exp, bias=src_logit[:, bass.ds(h, 1), i])
                nc.scalar.activation(e2[:, i % 2, :], expo_bc[:, 1, :], ACT.Exp, bias=src_logit02[:, bass.ds(h, 1), i]).then_inc(e_done, 1)

            def weight_high(v, i):
                act.wait_ge(p_full, v * NB + (i + 3))
                nc.scalar.copy(ph[:, i, :], pf[:, i % 2, :]).then_inc(p_hi, 1)

            def chunk_high(u, s):
                act.wait_ge(w_in[s % RAW], u * (NS // RAW * 16) + (s // RAW + 1) * 16)
                act.wait_ge(w_used, u * NS + (s + 1))
                nc.scalar.copy(wh[:, s % PARTS, :], wr[:, s % RAW, :]).then_inc(w_hi, 1)

            def unit(u, half, h, following, leaving):
                if leaving:
                    act.wait_ge(w_used, u * NS + PARTS)
                    for f in range(FB):
                        nc.scalar.copy(cols[:, f, :], banks[f][:, :]).then_inc(cols_done, 1)
                for f in range(FB):
                    if f < PARTS:
                        chunk_high(u, f)
                    act.wait_ge(y_out, u * FB + (f + 2))
                    nc.scalar.copy(yh[:, f, :], yf[:, f % 2, :]).then_inc(y_hi, 1)
                    if f == 2 and following:
                        exponents_out(u + 1)
                if following:
                    act.wait_ge(expo_in, u * 16 + 32)
                act.wait_ge(y_lo, u * FB + (FB + 2))
                for s, (kind, k) in enumerate(STEPS):
                    if following and s < NB:
                        exponentials(u + 1, following[1], s)
                    if kind == "B":
                        act.wait_ge(w_used, u * NS + (s + 1 + PARTS))
                        if leaving and k == 0:
                            for i in range(2):
                                act.wait_ge(rows_saved[i], 16 * HNB // 2)
                        act.wait_ge(h_lo, u * FB + (k + 2))
                        b = bias1[:, bass.ds(h * FB + k, 1)]
                        nc.scalar.activation(he[:, k % 2, :], work_bank("B", k)[:, :], ACT.Exp, bias=b)
                        nc.scalar.activation(hr[:, k % 2, :], work_bank("B", k)[:, :], ACT.Relu, bias=b).then_inc(h_out, 1)
                    if following and 1 <= s < NB + 1:
                        weight_high(u + 1, s - 1)
                    if s + PARTS < NS:
                        chunk_high(u, s + PARTS)

            act.sem_inc(h_out, 2)
            exponents_out(0)
            act.wait_ge(expo_in, 16)
            for i in range(NB + 1):
                if i < NB:
                    exponentials(0, 0, i)
                if i >= 1:
                    weight_high(0, i - 1)
            units(act, unit)

        @block.vector
        def _(dve):
            def exponents(v, half, h, ready=None):
                if ready:
                    ready()
                for c in range(HNB):
                    nc.vector.tensor_tensor_reduce(out=junk[:, c, :], in0=mask[:, c, :], in1=row_bc[:, :], scale=1.0, scalar=LOWEST,
                                                   op0=ALU.add, op1=ALU.max, accum_out=top[:, c:c + 1]).then_inc(top_sum, 1)
                dve.wait_ge(top_sum, v * HNB + HNB)
                ad = dst_logit[:, bass.ds(h, 1), half * HNB:(half + 1) * HNB].rearrange("p a c -> p (a c)")
                nc.vector.tensor_tensor(top[:, :], top[:, :], ad, ALU.add).then_inc(expo_step, 1)
                dve.wait_ge(expo_step, v * 4 + 1)
                nc.vector.scalar_tensor_tensor(out=top[:, :], in0=top[:, :], scalar=SLOPE, in1=top[:, :], op0=ALU.mult, op1=ALU.max).then_inc(expo_step, 1)
                dve.wait_ge(expo_step, v * 4 + 2)
                nc.vector.tensor_tensor(expo[:, 0, :], ad, top[:, :], ALU.subtract).then_inc(expo_step, 1)
                nc.vector.scalar_tensor_tensor(out=expo[:, 1, :], in0=ad, scalar=SLOPE, in1=top[:, :], op0=ALU.mult, op1=ALU.subtract).then_inc(expo_step, 1)

            def weight_products(v, half, i):
                dve.wait_ge(e_done, v * NB + (i + 1))
                nc.vector.tensor_tensor(e1[:, i % 2, :], e1[:, i % 2, :], e2[:, i % 2, :], ALU.max).then_inc(e_max, 1)
                dve.wait_ge(e_max, v * NB + (i + 1))
                dve.wait_ge(p_sum, v * 7 + (i + 1 if i < 2 else max(i - 2, 1) + 2))
                dve.wait_ge(p_lo, v * NB + (i + 1))
                nc.vector.scalar_tensor_tensor(out=pf[:, i % 2, :], in0=e1[:, i % 2, :], scalar=1.0,
                                               in1=countT[:, i, half * HALF:(half + 1) * HALF], op0=ALU.min, op1=ALU.mult).then_inc(p_full, 1)

            def weight_low(v, i):
                dve.wait_ge(p_hi, v * NB + (i + 1))
                nc.vector.tensor_tensor(pl[:, i, :], pf[:, i % 2, :], ph[:, i, :].bitcast(F32), ALU.subtract).then_inc(p_lo, 1)

            def chunk_low(u, s):
                dve.wait_ge(w_hi, u * NS + (s + 1))
                nc.vector.tensor_tensor(wl[:, s % PARTS, :], wr[:, s % RAW, :], wh[:, s % PARTS, :].bitcast(F32), ALU.subtract).then_inc(w_lo, 1)

            def unit(u, half, h, following, leaving):
                dve.wait_ge(den_full, u + 1)
                dve.wait_ge(y_out, u * FB + 1)
                nc.vector.tensor_scalar(rden[:, :], work_bank("sums")[:, :], DEN_EPS, None, ALU.add).then_inc(den_out, 1)
                dve.wait_ge(den_out, u + 1)
                nc.vector.reciprocal(rden[:, :], rden[:, :]).then_inc(rden_done, 1)
                if following:
                    def ready():
                        dve.wait_ge(h_lo, u * FB + 3)
                        dve.wait_ge(expo_step, u * 4 + 4)
                        dve.wait_ge(row_in, u * 16 + 32)
                        chunk_low(u, 0)
                        if following[0] != half:
                            dve.wait_ge(mask_in, 32)

                    exponents(u + 1, *following, ready)
                else:
                    chunk_low(u, 0)
                dve.wait_ge(rden_done, u + 1)
                for f in range(FB + 1):
                    if f == 3 and leaving:
                        dve.wait_ge(top_sum, (u + 2) * HNB)
                        for b in range(HNB):
                            if b >= 2:
                                dve.wait_ge(rows_saved[b % 2], 16)
                            for i in range(2):
                                dve.wait_ge(rows_turned, 2 * b + i + 1)
                                nc.vector.tensor_copy(rows[:, b % 2, i * HC:(i + 1) * HC], banks[(2 * b + i) % FB][:, 0:HC]).then_inc(rows_done, 1)
                    if f < FB:
                        dve.wait_ge(y_full, u * FB + (f + 1))
                        dve.wait_ge(y_lo, u * FB + (f + 1))
                        nc.vector.tensor_tensor(yf[:, f % 2, :], work_bank("A", f)[:, :], rden[:, :], ALU.mult).then_inc(y_out, 1)
                    if 1 <= f < PARTS:
                        chunk_low(u, f)
                    if f >= 1:
                        dve.wait_ge(y_hi, u * FB + f)
                        nc.vector.tensor_tensor(yl[:, f - 1, :], yf[:, (f - 1) % 2, :], yh[:, f - 1, :].bitcast(F32), ALU.subtract).then_inc(y_lo, 1)
                for s, (kind, k) in enumerate(STEPS):
                    if following and s < NB:
                        weight_products(u + 1, following[0], s)
                    if kind == "B":
                        dve.wait_ge(h_out, u * FB + (k + 3))
                        nc.vector.scalar_tensor_tensor(out=he[:, k % 2, :], in0=he[:, k % 2, :], scalar=1.0, in1=hr[:, k % 2, :],
                                                       op0=ALU.min, op1=ALU.add).then_inc(h_sum, 1)
                        dve.wait_ge(h_sum, u * FB + (k + 1))
                        dve.wait_ge(h_lo, u * FB + (k + 1))
                        nc.vector.tensor_scalar(hh[:, k % 3, :], he[:, k % 2, :], 1.0, None, ALU.subtract).then_inc(h_hi, 1)
                        dve.wait_ge(h_hi, u * FB + (k + 1))
                        nc.vector.scalar_tensor_tensor(out=hl[:, k % 3, :], in0=he[:, k % 2, :], scalar=1.0, in1=hh[:, k % 3, :].bitcast(F32),
                                                       op0=ALU.subtract, op1=ALU.subtract).then_inc(h_lo, 1)
                    if following and 1 <= s < NB + 1:
                        weight_low(u + 1, s - 1)
                    if s + PARTS < NS:
                        chunk_low(u, s + PARTS)

            dve.sem_inc(w_lo, RAW)
            dve.sem_inc(p_full, 2)
            dve.sem_inc(p_lo, 2)
            dve.sem_inc(y_lo, 2)
            dve.sem_inc(h_lo, 3)
            dve.sem_inc(y_out, 1)
            dve.wait_ge(row_in, 16)
            dve.wait_ge(mask_in, 16)
            exponents(0, 0, 0)
            for i in range(NB + 1):
                if i < NB:
                    weight_products(0, 0, i)
                if i >= 1:
                    weight_low(0, i - 1)
            units(dve, unit)

        @block.tensor
        def _(pe):
            def exponents_turned(v):
                pe.wait_ge(expo_step, v * 4 + 4)
                nc.tensor.transpose(work_bank("exponents")[0:2 * HNB, 0:P], expo[:, :, :].rearrange("p k c -> p (k c)"), ident[:, :]).then_inc(expoT_full, 1)

            def open_banks():
                for f in range(FB):
                    nc.tensor.matmul(banks[f][:, :], zero_r[:, :], xl[:, 0, 0:HALF], start=True, stop=False, skip_group_check=True)

            def close_banks():
                for f in range(FB):
                    last = nc.tensor.matmul(banks[f][:, :], zero_r[:, :], xl[:, 0, 0:HALF], start=False, stop=True, skip_group_check=True)
                return last

            def unit(u, half, h, following, leaving):
                pe.wait_ge(p_sum, u * 7 + 9)
                pe.wait_ge(h_out, u * FB + 2)
                nc.tensor.matmul(work_bank("sums")[:, :], ones[:, :], psum_rows[:, :], start=True, stop=True).then_inc(den_full, 1)
                pe.wait_ge(p_lo, u * NB + (NB + 2))
                for f in range(FB):
                    if f == 1:
                        pe.wait_ge(den_out, u + 1)
                    elif f == 4 and following:
                        pe.wait_ge(expoT_out, u + 2)
                    elif f >= 2:
                        pe.wait_ge(y_out, u * FB + (f if f != 3 else f + 1))
                    fs = slice(f * P, (f + 1) * P)
                    for b in range(NB):
                        last = split_products(nc, work_bank("A", f)[:, :], (xh[:, b, fs], xl[:, b, fs]), (ph[:, b, :], pl[:, b, :]),
                                              b == 0, b == NB - 1)
                    last.then_inc(y_full, 1)
                    if f == 2 and following:
                        pe.wait_ge(y_out, u * FB + 3)
                        exponents_turned(u + 1)
                    if f == 2 and leaving:
                        pe.wait_ge(cols_done, FB)
                        for b in range(HNB):
                            for i in range(2):
                                n = 2 * b + i
                                if n >= FB:
                                    pe.wait_ge(rows_done, n - FB + 1)
                                for j in range(3):
                                    last = nc.tensor.transpose(banks[n % FB][:, j * P:(j + 1) * P], cols[:, 3 * i + j, b * P:(b + 1) * P], ident[:, :])
                                last.then_inc(rows_turned, 1)
                if leaving:
                    pe.wait_ge(rows_done, 2 * HNB)
                    open_banks()
                for s, (kind, k) in enumerate(STEPS):
                    i = s % PARTS
                    pe.wait_ge(w_lo, u * NS + (s + 1 + RAW))
                    if kind == "B":
                        if k == 0:
                            pe.wait_ge(y_out, u * FB + FB)
                        if k >= 2:
                            pe.wait_ge(h_out, u * FB + (k + 1))
                        for f in range(FB):
                            if k == 0:
                                pe.wait_ge(y_lo, u * FB + (f + 3))
                            fs = slice(f * P, (f + 1) * P)
                            last = split_products(nc, work_bank("B", k)[:, :], (wh[:, i, fs], wl[:, i, fs]), (yh[:, f, :], yl[:, f, :]),
                                                  f == 0, f == FB - 1)
                    else:
                        pe.wait_ge(h_lo, u * FB + (k + 4))
                        for f in range(FB):
                            fs = slice(f * P, (f + 1) * P)
                            last = split_products(nc, banks[f][:, :], (wh[:, i, fs], wl[:, i, fs]), (hh[:, k % 3, :], hl[:, k % 3, :]),
                                                  False, False, grouped=False)
                    if s == NS - 1 and following and following[0] != half:
                        last = close_banks()
                    last.then_inc(w_used, 1)

            open_banks()
            pe.sem_inc(w_used, PARTS)
            exponents_turned(0)
            units(pe, unit)
            close_banks()


def hidden_to_rows(nc, ctx, sb, sem, FREE, banks, half, t):
    ident, h2_d = t["ident"], t["h2_d"]
    n = f"_{half}"
    at = [FREE]
    cols = sb("h2_cols" + n, [P, FB, HALF], F32, at)
    rows = sb("h2_rows" + n, [P, HNB, D], F32, at)
    cols_done, turned, rows_done, rows_out = (sem(s + n) for s in ("cols_done", "turned", "rows_done", "rows_out"))
    with nc.Block() as block:
        @block.scalar
        def _(act):
            for f in range(FB):
                nc.scalar.copy(cols[:, f, :], banks[f][:, :]).then_inc(cols_done, 1)

        @block.tensor
        def _(pe):
            pe.wait_ge(cols_done, FB)
            for b in range(HNB):
                pair = 2 * (b % 2)
                if b >= 2:
                    pe.wait_ge(rows_done, 2 * (b - 1))
                for i in range(2):
                    for j in range(3):
                        f = 3 * i + j
                        last = nc.tensor.transpose(banks[pair + i][:, j * P:(j + 1) * P], cols[:, f, b * P:(b + 1) * P], ident[:, :])
                    last.then_inc(turned, 1)

        @block.vector
        def _(dve):
            for b in range(HNB):
                for i in range(2):
                    dve.wait_ge(turned, 2 * b + i + 1)
                    nc.vector.tensor_copy(rows[:, b, i * HC:(i + 1) * HC], banks[2 * (b % 2) + i][:, 0:HC]).then_inc(rows_done, 1)

        @block.sync
        def _(sp):
            for b in range(HNB):
                sp.wait_ge(rows_done, 2 * b + 2)
                sp.dma_start(h2_d[half * HALF + b * P:half * HALF + (b + 1) * P, :], rows[:, b, :]).then_inc(rows_out, 16)
            sp.wait_ge(rows_out, 16 * HNB)


NORM_STEPS, NORM_ROOT = 6, 4


def normalise(nc, dve, row, stats, moments, root, n, added, step, root_done):
    dve.wait_ge(added, 2 * n + 2)
    for i in range(2):
        nc.vector.bn_stats(stats[:, i, :], row[:, i * HC:(i + 1) * HC]).then_inc(step, 1)
    dve.wait_ge(step, NORM_STEPS * n + 2)
    nc.vector.bn_aggr(moments, stats.rearrange("p i s -> p (i s)")).then_inc(step, 1)
    dve.wait_ge(step, NORM_STEPS * n + 3)
    nc.vector.tensor_scalar(root, moments[:, 1:2], LN_EPS, None, ALU.add).then_inc(step, 1)
    dve.wait_ge(root_done, n + 1)
    nc.vector.reciprocal(root, root).then_inc(step, 1)
    dve.wait_ge(step, NORM_STEPS * n + 5)
    nc.vector.tensor_scalar(row, row, moments[:, 0:1], root, ALU.subtract, ALU.mult).then_inc(step, 1)


class SplitCounts:

    def __init__(self, nc, countT, ident, high, low, half, number, hi, loops, lo):
        self.nc, self.countT, self.ident, self.high, self.low, self.half = nc, countT, ident, high, low, half
        self.number, self.hi, self.loops, self.lo = number, hi, loops, lo

    def scalar_part(self, i):
        hs = slice(self.half * HALF, (self.half + 1) * HALF)
        self.nc.scalar.copy(self.high[:, i, :], self.countT[:, i, hs]).then_inc(self.hi, 1)

    def vector_part(self, dve, i):
        hs = slice(self.half * HALF, (self.half + 1) * HALF)
        c = i - self.half * HNB
        tile = slice(c * P, (c + 1) * P)
        dve.wait_ge(self.hi, self.number * NB + i + 1)
        if not 0 <= c < HNB:
            self.nc.vector.tensor_tensor(self.low[:, i, :], self.countT[:, i, hs], self.high[:, i, :].bitcast(F32), ALU.subtract).then_inc(self.lo, 1)
            return
        at = 2 * (self.number * HNB + c)
        self.nc.vector.tensor_tensor(self.high[:, i, tile], self.countT[:, i, i * P:(i + 1) * P], self.ident[:, :], ALU.add).then_inc(self.loops, 1)
        dve.wait_ge(self.loops, at + 1)
        self.nc.vector.tensor_tensor(self.low[:, i, :], self.countT[:, i, hs], self.high[:, i, :].bitcast(F32), ALU.subtract).then_inc(self.loops, 1)
        dve.wait_ge(self.loops, at + 2)
        self.nc.vector.tensor_tensor(self.low[:, i, tile], self.low[:, i, tile].bitcast(F32), self.ident[:, :], ALU.add).then_inc(self.lo, 1)


def second_attention(nc, sb, sem, banks, t):
    x, countT, ident, dinv = t["x"], t["countT"], t["ident"], t["dinv"]
    h2_d, mask_d, logits2_d, expo2_d, x1_d = t["h2_d"], t["mask_d"], t["logits2_d"], t["expo2_d"], t["x1_d"]
    x1, sxh, sxl, ch, cl = t["x1"], t["sxh"], t["sxl"], t["ch"], t["cl"]
    DX = D + 2
    at = [t["counts_at"]]
    ph = [sb("p2h0", [P, NB, HALF], F32R, at)]
    pl = [sb("p2l0", [P, NB, HALF], F32R, at)]
    assert at[0] == t["FREE_LATE"]
    ph += [sb("p2h1", [P, NB, HALF], F32R, at)]
    mask = nc.alloc_sbuf_tensor_at("mask2", [P, NB, N], BF16, offset=at[0])
    pl += [sb("p2l1", [P, NB, HALF], F32R, at)]
    gh = sb("gh", [P, NB, DX], F32R, at)
    gl = sb("gl", [P, NB, DX], F32R, at)
    b2_bc = sb("b2_bc", [P, D], F32, at)
    logit2 = sb("logit2", [P, 2, NB], F32, at)
    logit02 = sb("logit2_02", [P, NB], F32, at)
    top = sb("top2", [P, NB], F32, at)
    expo = sb("expo2", [P, 2, NB], F32, at)
    rden = sb("rden2", [P, NB], F32, at)
    stats = sb("stats1", [P, NB, 2, 6], F32, at)
    moments = sb("moments1", [P, NB, 2], F32, at)
    root = sb("root1", [P, NB], F32, at)
    at = [t["sx_at"]]
    a2_bc = sb("a2_bc", [P, 2, D], F32, at)
    h2 = sb("h2", [P, 4, D], F32, at)
    logit2T = sb("logit2T", [NB, P], F32, at)
    expoT = sb("expo2T", [2 * NB, P], F32, at)
    expo_bc = sb("expo2_bc", [P, 2, N], F32, at)
    e1 = sb("e1_2", [P, 2, HALF], F32, at)
    e2 = sb("e2_2", [P, 2, HALF], F32, at)
    pf = sb("pf_2", [P, 2, HALF], F32, at)
    row_bc = sb("row2_bc", [P, N], F32, at)
    junk = [sb(f"junk2{i}", [P, N], BF16, at) for i in range(2)]
    assert at[0] <= t["counts_at"]
    in_sem = {k: sem("in2_" + k) for k in ("x", "b", "a", "mask", "row", "expo")}
    h2_in = [sem(f"h2_in{i}") for i in range(4)]
    logit_sum, g_hi, g_lo, g_one = sem("logit2_sum"), sem("g_hi"), sem("g_lo"), sem("g_one")
    xb_done, turned, turned_out, logits_out, small = (sem(n) for n in ("xb_done", "turned2", "turned2_out", "logits2_out", "small2"))
    top_sum, e_done, e_max, p_full, p_hi, p_lo = (sem(n) for n in ("top2_sum", "e2_done", "e2_max", "p2_full", "p2_hi", "p2_lo"))
    agg_full, bank_free, agg_step, norm_step, root_sem = (sem(n) for n in ("agg2_full", "agg2_free", "agg2_step", "norm1_step", "root1_done"))

    sx_hi, sx_lo, c_hi, c_loops, c_lo, x1_out = (sem(n) for n in ("sx_hi", "sx_lo", "c_hi", "c_loops", "c_lo", "x1_out"))
    counts = SplitCounts(nc, countT, ident, ch, cl, 0, 0, c_hi, c_loops, c_lo)

    def counts_beside(b):
        return range(2 * (b - HNB), 2 * (b - HNB) + 2) if b >= HNB else ()

    with nc.Block() as block:
        @block.sync
        def _(sp):
            for b in range(NB):
                if b >= 4:
                    sp.wait_ge(g_lo, b - 3)
                    sp.wait_ge(logit_sum, 2 * (b - 3))
                sp.dma_start(h2[:, b % 4, :], h2_d[b * P:(b + 1) * P, :]).then_inc(h2_in[b % 4], 16)
                if b == 0:
                    sp.dma_start(a2_bc[:, 0, :], t["gat_a_src2"].rearrange("a c -> (a c)").partition_broadcast(P)).then_inc(in_sem["a"], 16)
                    sp.dma_start(a2_bc[:, 1, :], t["gat_a_dst2"].rearrange("a c -> (a c)").partition_broadcast(P)).then_inc(in_sem["a"], 16)
                if b == 3:
                    sp.dma_start(mask[:, :, :].rearrange("p b n -> p (b n)"), mask_d).then_inc(in_sem["mask"], 16)
                    sp.dma_start(x1[:, :, :], x.rearrange("(b p) f -> p b f", p=P)).then_inc(in_sem["x"], 16)
                    sp.dma_start(b2_bc[:, :], t["gat_b2"].partition_broadcast(P)).then_inc(in_sem["b"], 16)
            sp.wait_ge(turned_out, 1)
            sp.dma_start(logits2_d, logit2T[:, :]).then_inc(logits_out, 16)
            sp.wait_ge(logits_out, 16)
            sp.dma_start(row_bc[:, :], logits2_d.rearrange("b p -> (b p)").partition_broadcast(P)).then_inc(in_sem["row"], 16)
            sp.wait_ge(turned_out, 2)
            sp.dma_start(expo2_d.rearrange("k b p -> (k b) p"), expoT[:, :]).then_inc(logits_out, 16)
            sp.wait_ge(logits_out, 32)
            sp.dma_start(expo_bc[:, :, :].rearrange("p k n -> p (k n)"), expo2_d.rearrange("k b p -> (k b p)").partition_broadcast(P)).then_inc(in_sem["expo"], 16)
            for b in range(NB):
                sp.wait_ge(norm_step, NORM_STEPS * (b + 1))
                sp.dma_start(x1_d[b * P:(b + 1) * P, :], x1[:, b, :]).then_inc(x1_out, 16)
            sp.wait_ge(x1_out, 16 * NB)

        @block.scalar
        def _(act):
            for b in range(NB):
                act.wait_ge(h2_in[b % 4], 16 * (b // 4 + 1))
                nc.scalar.copy(gh[:, b, 0:D], h2[:, b % 4, :]).then_inc(g_hi, 1)
            act.wait_ge(turned, 1)
            nc.scalar.copy(logit2T[:, :], banks[0][0:NB, 0:P]).then_inc(turned_out, 1)
            act.wait_ge(turned, 2)
            nc.scalar.copy(expoT[:, :], banks[1][0:2 * NB, 0:P]).then_inc(turned_out, 1)
            act.wait_ge(in_sem["expo"], 16)
            for half in range(2):
                for i in range(NB + 1):
                    c = half * NB + i
                    if i < NB:
                        if c >= 2:
                            act.wait_ge(p_full, c - 1)
                        hs = slice(half * HALF, (half + 1) * HALF)
                        nc.scalar.activation(e1[:, i % 2, :], expo_bc[:, 0, hs], ACT.Exp, bias=logit2[:, 0, i:i + 1])
                        nc.scalar.activation(e2[:, i % 2, :], expo_bc[:, 1, hs], ACT.Exp, bias=logit02[:, i:i + 1]).then_inc(e_done, 1)
                    if i >= 1:
                        act.wait_ge(p_full, c)
                        nc.scalar.copy(ph[half][:, i - 1, :], pf[:, (i - 1) % 2, :]).then_inc(p_hi, 1)
            for b in range(NB):
                for i in counts_beside(b):
                    if i == 0:
                        act.wait_ge(agg_full, HNB)
                    counts.scalar_part(i)
                act.wait_ge(norm_step, NORM_STEPS * b + NORM_ROOT)
                nc.scalar.activation(root[:, b:b + 1], root[:, b:b + 1], ACT.Sqrt).then_inc(root_sem, 1)
                act.wait_ge(norm_step, NORM_STEPS * (b + 1))
                nc.scalar.activation(sxh[:, b, :], x1[:, b, :], ACT.Copy, scale=dinv[:, b:b + 1]).then_inc(sx_hi, 1)

        @block.vector
        def _(dve):
            nc.vector.tensor_scalar(gh[:, :, D:DX], ident[:, 0:2 * NB].rearrange("p (b c) -> p b c", c=2), 0.0, 1.0, ALU.mult, ALU.add).then_inc(g_one, 1)
            nc.vector.tensor_scalar(gl[:, :, D:DX], ident[:, 0:2 * NB].rearrange("p (b c) -> p b c", c=2), 0.0, None, ALU.mult).then_inc(g_one, 1)
            dve.wait_ge(in_sem["a"], 32)
            for b in range(NB):
                dve.wait_ge(h2_in[b % 4], 16 * (b // 4 + 1))
                for k in range(2):
                    if b >= 1:
                        dve.wait_ge(logit_sum, 2 * b + k - 1)
                    nc.vector.tensor_tensor_reduce(out=junk[k][:, 0:D], in0=h2[:, b % 4, :], in1=a2_bc[:, k, :], scale=1.0, scalar=0.0,
                                                   op0=ALU.mult, op1=ALU.add, accum_out=logit2[:, k, b:b + 1]).then_inc(logit_sum, 1)
                dve.wait_ge(g_hi, b + 1)
                nc.vector.tensor_tensor(gl[:, b, 0:D], h2[:, b % 4, :], gh[:, b, 0:D].bitcast(F32), ALU.subtract).then_inc(g_lo, 1)
            dve.wait_ge(logit_sum, 2 * NB)
            nc.vector.tensor_scalar(logit02[:, :], logit2[:, 0, :], SLOPE, None, ALU.mult).then_inc(small, 1)
            dve.wait_ge(in_sem["x"], 16)
            dve.wait_ge(in_sem["b"], 16)
            for b in range(NB):
                nc.vector.tensor_tensor(x1[:, b, :], x1[:, b, :], b2_bc[:, :], ALU.add).then_inc(xb_done, 1)
            dve.wait_ge(in_sem["row"], 16)
            dve.wait_ge(in_sem["mask"], 16)
            for b in range(NB):
                if b >= 2:
                    dve.wait_ge(top_sum, b - 1)
                nc.vector.tensor_tensor_reduce(out=junk[b % 2][:, :], in0=mask[:, b, :], in1=row_bc[:, :], scale=1.0, scalar=LOWEST,
                                               op0=ALU.add, op1=ALU.max, accum_out=top[:, b:b + 1]).then_inc(top_sum, 1)
            dve.wait_ge(top_sum, NB)
            nc.vector.tensor_tensor(top[:, :], top[:, :], logit2[:, 1, :], ALU.add).then_inc(small, 1)
            dve.wait_ge(small, 2)
            nc.vector.scalar_tensor_tensor(out=top[:, :], in0=top[:, :], scalar=SLOPE, in1=top[:, :], op0=ALU.mult, op1=ALU.max).then_inc(small, 1)
            dve.wait_ge(small, 3)
            nc.vector.tensor_tensor(expo[:, 0, :], logit2[:, 1, :], top[:, :], ALU.subtract).then_inc(small, 1)
            nc.vector.scalar_tensor_tensor(out=expo[:, 1, :], in0=logit2[:, 1, :], scalar=SLOPE, in1=top[:, :], op0=ALU.mult, op1=ALU.subtract).then_inc(small, 1)
            for half in range(2):
                for i in range(NB + 1):
                    c = half * NB + i
                    if i < NB:
                        dve.wait_ge(e_done, c + 1)
                        nc.vector.tensor_tensor(e1[:, i % 2, :], e1[:, i % 2, :], e2[:, i % 2, :], ALU.max).then_inc(e_max, 1)
                        dve.wait_ge(e_max, c + 1)
                        if c >= 2:
                            dve.wait_ge(p_lo, c - 1)
                        nc.vector.scalar_tensor_tensor(out=pf[:, i % 2, :], in0=e1[:, i % 2, :], scalar=1.0,
                                                       in1=countT[:, i, half * HALF:(half + 1) * HALF], op0=ALU.min, op1=ALU.mult).then_inc(p_full, 1)
                    if i >= 1:
                        dve.wait_ge(p_hi, c)
                        nc.vector.tensor_tensor(pl[half][:, i - 1, :], pf[:, (i - 1) % 2, :], ph[half][:, i - 1, :].bitcast(F32), ALU.subtract).then_inc(p_lo, 1)
            def scaled_low(b):
                dve.wait_ge(sx_hi, b + 1)
                nc.vector.scalar_tensor_tensor(out=sxl[:, b, :], in0=x1[:, b, :], scalar=dinv[:, b:b + 1], in1=sxh[:, b, :].bitcast(F32),
                                               op0=ALU.mult, op1=ALU.subtract).then_inc(sx_lo, 1)

            for b in range(NB):
                left, right = banks[2 * (b % 4)], banks[2 * (b % 4) + 1]
                dve.wait_ge(agg_full, b + 1)
                nc.vector.tensor_scalar(rden[:, b:b + 1], right[:, HC:HC + 1], DEN_EPS, None, ALU.add).then_inc(agg_step, 1)
                dve.wait_ge(agg_step, 2 * b + 1)
                nc.vector.reciprocal(rden[:, b:b + 1], rden[:, b:b + 1]).then_inc(agg_step, 1)
                dve.wait_ge(agg_step, 2 * b + 2)
                dve.wait_ge(xb_done, NB)
                for i, bank in enumerate((left, right)):
                    cs = slice(i * HC, (i + 1) * HC)
                    nc.vector.scalar_tensor_tensor(out=x1[:, b, cs], in0=bank[:, 0:HC], scalar=rden[:, b:b + 1], in1=x1[:, b, cs],
                                                   op0=ALU.mult, op1=ALU.add).then_inc(bank_free, 1)
                normalise(nc, dve, x1[:, b, :], stats[:, b, :, :], moments[:, b, :], root[:, b:b + 1], b, bank_free, norm_step, root_sem)
                if b >= 1:
                    scaled_low(b - 1)
                for i in counts_beside(b):
                    counts.vector_part(dve, i)
            scaled_low(NB - 1)

        @block.tensor
        def _(pe):
            pe.wait_ge(logit_sum, 2 * NB)
            nc.tensor.transpose(banks[0][0:NB, 0:P], logit2[:, 0, :], ident[:, :]).then_inc(turned, 1)
            pe.wait_ge(small, 5)
            nc.tensor.transpose(banks[1][0:2 * NB, 0:P], expo[:, :, :].rearrange("p k b -> p (k b)"), ident[:, :]).then_inc(turned, 1)
            pe.wait_ge(turned_out, 2)
            pe.wait_ge(g_lo, NB)
            pe.wait_ge(g_one, 2)
            for b in range(NB):
                half, c = b // HNB, b % HNB
                pe.wait_ge(p_lo, NB * (half + 1))
                if b >= 4:
                    pe.wait_ge(bank_free, 2 * (b - 3))
                for i in range(2):
                    cs = slice(i * HC, (i + 1) * HC + 2 * i)
                    for s in range(NB):
                        bs = slice(c * P, (c + 1) * P)
                        last = split_products(nc, banks[2 * (b % 4) + i][:, 0:HC + 2 * i], (ph[half][:, s, bs], pl[half][:, s, bs]),
                                              (gh[:, s, cs], gl[:, s, cs]), s == 0, s == NB - 1)
                last.then_inc(agg_full, 1)


def graph_convolution(nc, sb, sem, banks, t):
    countT, ident, dinv, gcn_bias1, many_i = t["countT"], t["ident"], t["dinv"], t["gcn_bias1"], t["many_i"]
    dinv_d, x1_d, gcn_w1, gcn_w2, out = t["dinv_d"], t["x1_d"], t["gcn_w1"], t["gcn_w2"], t["out"]
    x1, xh, xl, ch, cl = t["x1"], t["sxh"], t["sxl"], t["ch"], t["cl"]
    at = [t["x1_at"]]
    wh = sb("gwh", [P, PARTS, D], F32R, at)
    wl = sb("gwl", [P, PARTS, D], F32R, at)
    assert at[0] <= t["sx_at"]
    at = [t["FREE_LATE"]]
    y_at = at[0]
    yh = sb("gyh", [P, FB, HALF], F32R, at)
    yl = sb("gyl", [P, FB, HALF], F32R, at)
    hh = sb("ghh", [P, FB, HALF], F32R, at)
    hl = sb("ghl", [P, FB, HALF], F32R, at)
    wr = sb("gwr", [P, RAW, D], F32, at)
    dinv_bc = sb("gdinv_bc", [P, N], F32, at)
    yf = sb("gyf", [P, 2, HALF], F32, at)
    hf = sb("ghf", [P, 2, HALF], F32, at)
    rows = sb("grows", [P, HNB, D], F32, at)
    stats = sb("gstats", [P, NB, 2, 6], F32, at)
    moments = sb("gmoments", [P, NB, 2], F32, at)
    root = sb("groot", [P, NB], F32, at)
    ch2 = nc.alloc_sbuf_tensor_at("gch2", [P, NB, HALF], F32R, offset=y_at)
    cl2 = nc.alloc_sbuf_tensor_at("gcl2", [P, NB, HALF], F32R, offset=y_at + 4 * NB * HALF)
    b2_bc = nc.alloc_sbuf_tensor_at("gb2_bc", [P, D], F32, offset=y_at + 4 * NB * HALF * 2)

    dinv_in, x1_in, b2_in = (sem(n) for n in ("gdinv_in", "gx1_in", "gb2_in"))
    w_in = [sem(f"gw_in{i}") for i in range(RAW)]
    w_hi, w_lo, w_used = sem("gw_hi"), sem("gw_lo"), sem("gw_used")
    c_hi, c_loops, c_lo = sem("gc_hi"), sem("gc_loops"), sem("gc_lo")
    y_full, y_out, y_hi, y_lo = (sem(n) for n in ("gy_full", "gy_out", "gy_hi", "gy_lo"))
    h_out, h_lo = sem("gh_out"), sem("gh_lo")
    rows_full, rows_hi, rows_lo = sem("grows_full"), sem("grows_hi"), sem("grows_lo")
    row_done = [sem("grow_s"), sem("grow_v")]
    xb = sem("gxb")
    agg_full, added, norm_step, root_done, out_done = (sem(n) for n in ("gagg_full", "gadded", "gnorm_step", "groot_done", "gout_done"))
    CH = 2 * FB

    def row_full(engine, half, c):
        if c < HNB - 1:
            engine.wait_ge(rows_full, half * (HNB - 1) + c + 1)
        else:
            engine.wait_ge(w_used, (half + 1) * CH)

    counts1 = SplitCounts(nc, countT, ident, ch, cl, 1, 0, c_hi, c_loops, c_lo)
    counts2 = SplitCounts(nc, countT, ident, ch2, cl2, 0, 1, c_hi, c_loops, c_lo)

    with nc.Block() as block:
        @block.sync
        def _(sp):
            for half in range(2):
                for s in range(CH):
                    g, k = half * CH + s, s % FB
                    if g >= RAW:
                        sp.wait_ge(w_lo, g - RAW + 1)
                    if s < FB:
                        sp.dma_start(wr[:, g % RAW, :].rearrange("p (f c) -> p f c", f=FB),
                                     gcn_w1[:, k * P:(k + 1) * P].rearrange("(f p) c -> p f c", p=P)).then_inc(w_in[g % RAW], 16)
                    else:
                        sp.dma_start(wr[:, g % RAW, :], gcn_w2[k * P:(k + 1) * P, :]).then_inc(w_in[g % RAW], 16)
                    if g == 0:
                        sp.dma_start(dinv_bc[:, :], dinv_d.rearrange("b p -> (b p)").partition_broadcast(P)).then_inc(dinv_in, 16)
            sp.wait_ge(w_used, 2 * CH)
            sp.dma_start(x1[:, :, :], x1_d.rearrange("(b p) f -> p b f", p=P)).then_inc(x1_in, 16)
            sp.dma_start(b2_bc[:, :], t["gcn_b2"].partition_broadcast(P)).then_inc(b2_in, 16)
            for n in range(NB):
                b = (n + HNB) % NB
                sp.wait_ge(norm_step, NORM_STEPS * (n + 1))
                sp.dma_start(out[b * P:(b + 1) * P, :], x1[:, b, :]).then_inc(out_done, 16)
            sp.wait_ge(out_done, 16 * NB)

        @block.gpsimd
        def _(pool):
            pool.wait_ge(x1_in, 16)
            pool.wait_ge(b2_in, 16)
            for n in range(NB):
                b = (n + HNB) % NB
                nc.gpsimd.tensor_tensor(x1[:, b, :], x1[:, b, :], b2_bc[:, :], ALU.add).then_inc(xb, 1)

        @block.scalar
        def _(act):
            def chunk_high(g):
                act.wait_ge(w_in[g % RAW], 16 * (g // RAW + 1))
                if g >= PARTS:
                    act.wait_ge(w_used, g - PARTS + 1)
                nc.scalar.copy(wh[:, g % PARTS, :], wr[:, g % RAW, :]).then_inc(w_hi, 1)

            for half in range(2):
                for f in range(FB):
                    if f < PARTS:
                        chunk_high(half * CH + f)
                    act.wait_ge(y_out, half * FB + f + 1)
                    nc.scalar.copy(yh[:, f, :], yf[:, f % 2, :]).then_inc(y_hi, 1)
                for k in range(FB):
                    n = half * FB + k
                    act.wait_ge(w_used, half * CH + k + 1)
                    if n >= 2:
                        act.wait_ge(h_lo, n - 1)
                    nc.scalar.activation(hh[:, k, :], banks[2 + k % 2][:, :], ACT.Relu, bias=gcn_bias1[:, k:k + 1])
                    nc.scalar.activation(hf[:, k % 2, :], banks[2 + k % 2][:, :], ACT.Relu, bias=gcn_bias1[:, k:k + 1]).then_inc(h_out, 1)
                    if k + PARTS < CH:
                        chunk_high(half * CH + k + PARTS)
                if half == 0:
                    for i in range(NB):
                        counts1.scalar_part(i)
                for s in range(FB + PARTS, CH):
                    chunk_high(half * CH + s)
                if half == 1:
                    act.wait_ge(row_done[0], HNB)
                    act.wait_ge(row_done[1], HNB)
                    for b in range(HNB):
                        nc.scalar.copy(xh[:, b, :], rows[:, b, :]).then_inc(rows_hi, 1)
                for c in range(HNB):
                    row_full(act, half, c)
                    if half == 0:
                        nc.scalar.activation(rows[:, c, 0:HC], banks[2 * c][:, 0:HC], ACT.Copy, scale=dinv[:, c:c + 1]).then_inc(row_done[0], 1)
                    else:
                        for i in range(2):
                            nc.scalar.activation(xh[:, HNB + c, i * HC:(i + 1) * HC], banks[2 * c + i][:, 0:HC], ACT.Copy,
                                                 scale=dinv[:, HNB + c:HNB + c + 1]).then_inc(rows_hi, 1)
            for i in range(NB):
                counts2.scalar_part(i)
            for n in range(NB):
                b = (n + HNB) % NB
                act.wait_ge(norm_step, NORM_STEPS * n + NORM_ROOT)
                nc.scalar.activation(root[:, b:b + 1], root[:, b:b + 1], ACT.Sqrt).then_inc(root_done, 1)

        @block.vector
        def _(dve):
            def chunk_low(g):
                dve.wait_ge(w_hi, g + 1)
                nc.vector.tensor_tensor(wl[:, g % PARTS, :], wr[:, g % RAW, :], wh[:, g % PARTS, :].bitcast(F32), ALU.subtract).then_inc(w_lo, 1)

            for half in range(2):
                hs = slice(half * HALF, (half + 1) * HALF)
                for f in range(FB + 1):
                    if f < PARTS:
                        chunk_low(half * CH + f)
                    if f == 0 and half == 0:
                        dve.wait_ge(dinv_in, 16)
                    if f < FB:
                        n = half * FB + f
                        dve.wait_ge(y_full, n + 1)
                        if n >= 2:
                            dve.wait_ge(y_lo, n - 1)
                        nc.vector.tensor_tensor(yf[:, f % 2, :], banks[f % 2][:, :], dinv_bc[:, hs], ALU.mult).then_inc(y_out, 1)
                    if f >= 1:
                        dve.wait_ge(y_hi, half * FB + f)
                        nc.vector.tensor_tensor(yl[:, f - 1, :], yf[:, (f - 1) % 2, :], yh[:, f - 1, :].bitcast(F32), ALU.subtract).then_inc(y_lo, 1)
                for k in range(FB):
                    dve.wait_ge(h_out, half * FB + k + 1)
                    nc.vector.tensor_tensor(hl[:, k, :], hf[:, k % 2, :], hh[:, k, :].bitcast(F32), ALU.subtract).then_inc(h_lo, 1)
                    if k + PARTS < CH:
                        chunk_low(half * CH + k + PARTS)
                if half == 0:
                    for i in range(NB):
                        counts1.vector_part(dve, i)
                for s in range(FB + PARTS, CH):
                    chunk_low(half * CH + s)
                if half == 1:
                    for b in range(HNB):
                        dve.wait_ge(rows_hi, b + 1)
                        nc.vector.tensor_tensor(xl[:, b, :], rows[:, b, :], xh[:, b, :].bitcast(F32), ALU.subtract).then_inc(rows_lo, 1)
                for c in range(HNB):
                    if half == 0:
                        row_full(dve, half, c)
                        nc.vector.tensor_scalar(rows[:, c, HC:D], banks[2 * c + 1][:, 0:HC], dinv[:, c:c + 1], None, ALU.mult).then_inc(row_done[1], 1)
                    else:
                        for i in range(2):
                            cs = slice(i * HC, (i + 1) * HC)
                            dve.wait_ge(rows_hi, HNB + 2 * c + i + 1)
                            nc.vector.scalar_tensor_tensor(out=xl[:, HNB + c, cs], in0=banks[2 * c + i][:, 0:HC], scalar=dinv[:, HNB + c:HNB + c + 1],
                                                           in1=xh[:, HNB + c, cs].bitcast(F32), op0=ALU.mult, op1=ALU.subtract).then_inc(rows_lo, 1)
            for i in range(NB):
                counts2.vector_part(dve, i)
            for n in range(NB):
                b = (n + HNB) % NB
                dve.wait_ge(agg_full, n + 1)
                dve.wait_ge(xb, n + 1)
                for i in range(2):
                    cs = slice(i * HC, (i + 1) * HC)
                    nc.vector.scalar_tensor_tensor(out=x1[:, b, cs], in0=banks[2 * (n % 4) + i][:, 0:HC], scalar=dinv[:, b:b + 1], in1=x1[:, b, cs],
                                                   op0=ALU.mult, op1=ALU.add).then_inc(added, 1)
                normalise(nc, dve, x1[:, b, :], stats[:, b, :, :], moments[:, b, :], root[:, b:b + 1], n, added, norm_step, root_done)

        @block.tensor
        def _(pe):
            many = pe.value_load(many_i[0:1, 0:1], min_val=0, max_val=N * NB)

            for half in range(2):
                if half:
                    pe.wait_ge(c_lo, NB)
                for f in range(FB):
                    bank = banks[f % 2]
                    if f >= 2:
                        pe.wait_ge(y_out, half * FB + f - 1)
                    elif half:
                        pe.wait_ge(row_done[f], 1)
                    fs = slice(f * P, (f + 1) * P)
                    for b in range(NB):
                        nc.tensor.matmul(bank[:, :], xh[:, b, fs], ch[:, b, :], start=(b == 0), stop=False)
                    with pe.If(many > 0):
                        for b in range(NB):
                            nc.tensor.matmul(bank[:, :], xh[:, b, fs], cl[:, b, :], start=False, stop=False)
                    for b in range(NB):
                        last = nc.tensor.matmul(bank[:, :], xl[:, b, fs], ch[:, b, :], start=False, stop=(b == NB - 1))
                    last.then_inc(y_full, 1)
                for k in range(FB):
                    g = half * CH + k
                    pe.wait_ge(w_lo, g + 1)
                    if k >= 2:
                        pe.wait_ge(h_out, half * FB + k - 1)
                    elif half:
                        pe.wait_ge(row_done[k], 2)
                    for f in range(FB):
                        if k == 0:
                            pe.wait_ge(y_lo, half * FB + f + 1)
                        fs = slice(f * P, (f + 1) * P)
                        last = split_products(nc, banks[2 + k % 2][:, :], (wh[:, g % PARTS, fs], wl[:, g % PARTS, fs]), (yh[:, f, :], yl[:, f, :]),
                                              f == 0, f == FB - 1)
                    last.then_inc(w_used, 1)
                for k in range(FB):
                    g = half * CH + FB + k
                    pe.wait_ge(w_lo, g + 1)
                    pe.wait_ge(h_lo, half * FB + k + 1)
                    for c in (0, 2, 3, 1) if k == 0 else range(HNB):
                        if k == 0 and c == 1:
                            pe.wait_ge(h_out, half * FB + FB)
                        elif k == 0 and half:
                            for i in range(2):
                                pe.wait_ge(row_done[i], HNB)
                        bs = slice(c * P, (c + 1) * P)
                        for i in range(2):
                            cs = slice(i * HC, (i + 1) * HC)
                            last = split_products(nc, banks[2 * c + i][:, 0:HC], (hh[:, k, bs], hl[:, k, bs]), (wh[:, g % PARTS, cs], wl[:, g % PARTS, cs]),
                                                  k == 0, k == FB - 1)
                        if k == FB - 1 and c < HNB - 1:
                            last.then_inc(rows_full, 1)
                    last.then_inc(w_used, 1)
            for n in range(NB):
                high, low = ((ch, cl), (ch2, cl2))[n // HNB]
                c = n % HNB
                if n == HNB:
                    pe.wait_ge(c_lo, 2 * NB)
                pair = banks[2 * (n % 4)], banks[2 * (n % 4) + 1]
                if n >= 4:
                    pe.wait_ge(added, 2 * (n - 3))
                else:
                    pe.wait_ge(rows_lo, HNB + 2 * n + 2)
                bs = slice(c * P, (c + 1) * P)
                for i, bank in enumerate(pair):
                    cs = slice(i * HC, (i + 1) * HC)
                    for s in range(NB):
                        if n == 0:
                            pe.wait_ge(rows_hi, s + 1 if s < HNB else HNB + 2 * (s - HNB) + 2)
                        nc.tensor.matmul(bank[:, 0:HC], high[:, s, bs], xh[:, s, cs], start=(s == 0), stop=False)
                    with pe.If(many > 0):
                        for s in range(NB):
                            nc.tensor.matmul(bank[:, 0:HC], low[:, s, bs], xh[:, s, cs], start=False, stop=False)
                    for s in range(NB):
                        if n == 0:
                            pe.wait_ge(rows_lo, s + 1 if s < HNB else HNB + 2 * (s - HNB) + 2)
                        last = nc.tensor.matmul(bank[:, 0:HC], high[:, s, bs], xl[:, s, cs], start=False, stop=(s == NB - 1))
                last.then_inc(agg_full, 1)


_INS = ["x", "src", "dst", "L0_gnn_W1", "L0_gnn_a_src1", "L0_gnn_a_dst1", "L0_gnn_b1", "L0_gnn_W2", "L0_gnn_a_src2", "L0_gnn_a_dst2",
        "L0_gnn_b2", "L1_gnn_W1", "L1_gnn_b1", "L1_gnn_W2", "L1_gnn_b2"]


def kernel(**inputs):
    import numpy as _np
    import concourse.bacc as _bacc
    from concourse import mybir as _mybir
    from concourse.bass_utils import run_bass_kernel_spmd as _run

    nc = _bacc.Bacc("TRN2", target_bir_lowering=False, num_devices=1)
    arrays, args = {}, []
    for name in _INS:
        a = _np.ascontiguousarray(inputs[name])
        arrays[f"in_{name}"] = a
        args.append(nc.dram_tensor(f"in_{name}", a.shape, _mybir.dt.from_np(a.dtype), kind="ExternalInput").ap())
    out = nc.dram_tensor("out_0", (N, D), _mybir.dt.float32, kind="ExternalOutput").ap()
    gnn_resnorm(nc, *args, out)
    r = _run(nc, [arrays], core_ids=[0])
    return r.results[0]["out_0"]
```

```python
import concourse.bass as bass
from concourse import mybir
from contextlib import ExitStack

F32 = mybir.dt.float32
F32R = mybir.dt.float32r
BF16 = mybir.dt.bfloat16
F16 = mybir.dt.float16
I16 = mybir.dt.int16
I32 = mybir.dt.int32
ALU = mybir.AluOpType
ACT = mybir.ActivationFunctionType
AX = mybir.AxisListType

P = 128
N = 1024
NB = N // P
D = 768
FB = D // P
HC = D // 2
H = 8
E = 16384
ET = E // P
HALF = N // 2
HNB = HALF // P
LN_EPS = 1e-5
DEN_EPS = 1e-16
SLOPE = 0.2
EXACT_COUNT = 4096.0
NOT_LINKED = -1e30
LOWEST = -3.0e38

SBUF_FROM = 16512
SBUF_TO = 229344


def split_products(nc, out, stationary, moving, first, last, grouped=True):
    (sh, sl), (mh, ml) = stationary, moving
    nc.tensor.matmul(out, sh, mh, start=first, stop=False, skip_group_check=not grouped)
    nc.tensor.matmul(out, sh, ml, start=False, stop=False, skip_group_check=not grouped)
    return nc.tensor.matmul(out, sl, mh, start=False, stop=last, skip_group_check=not grouped)


def gnn_resnorm(nc, x, src, dst, gat_w1, gat_a_src1, gat_a_dst1, gat_b1, gat_w2, gat_a_src2, gat_a_dst2, gat_b2,
                gcn_w1, gcn_b1, gcn_w2, gcn_b2, out):
    ctx = ExitStack()
    held, stage = [], [0]

    def sem(name):
        held.append(nc.alloc_semaphore(name=f"{name}_{stage[0]}"))
        return held[-1]

    def end_of_stage():
        nc.clear_and_free_semaphores(held)
        held.clear()
        stage[0] += 1
        nc.all_engine_barrier()

    with ctx:
        place = [SBUF_FROM]

        def sb(name, shape, dt, at=place):
            size = 2 if dt in (BF16, F16, I16) else 4
            for n in shape[1:]:
                size *= n
            t = nc.alloc_sbuf_tensor_at(name, shape, dt, offset=at[0])
            at[0] += -(-size // 32) * 32
            assert at[0] <= SBUF_TO, (name, at[0])
            return t

        countT = sb("countT", [P, NB, N], I16)
        ident = sb("ident", [P, P], F32)
        ones = sb("ones", [P, P], F32)
        zero_r = sb("zero_r", [P, P], F32R)
        src_logit = sb("src_logit", [P, H, NB], F32)
        src_logit02 = sb("src_logit02", [P, H, NB], F32)
        bias1 = sb("bias1", [P, H * FB], F32)
        dst_logit = sb("dst_logit", [P, H, NB], F32)
        a2_cols = sb("a2_cols", [P, FB, 2], F32)
        many_i = sb("many_i", [1, 8], I32)
        dinv = sb("dinv", [P, NB], F32)
        gcn_bias1 = sb("gcn_bias1", [P, FB], F32)
        FREE = place[0]
        xh = sb("xh", [P, NB, D], F32R)
        xl = sb("xl", [P, NB, D], F32R)
        mask_half = sb("mask_half", [P, HNB, N], BF16)
        FREE_BESIDE_X = place[0]

        banks = [ctx.enter_context(nc.psum_tensor(f"bank{i}", [P, 512], F32)) for i in range(8)]

        logits_d = nc.dram_tensor("logits_scratch", [2 * H, N], F32, kind="Internal").ap()
        expo_d = nc.dram_tensor("expo_scratch", [2 * HNB, P], F32, kind="Internal").ap()
        dinv_d = nc.dram_tensor("dinv_scratch", [NB, P], F32, kind="Internal").ap()
        mask_d = nc.dram_tensor("mask_scratch", [P, NB * N], BF16, kind="Internal").ap()
        h2_d = nc.dram_tensor("h2_scratch", [N, D], F32, kind="Internal").ap()
        x1_d = nc.dram_tensor("x1_scratch", [N, D], F32, kind="Internal").ap()

        graph_and_logits(nc, sb, sem, FREE_BESIDE_X, banks, locals())
        end_of_stage()
        attention_heads(nc, sb, sem, FREE_BESIDE_X, banks, locals())
        end_of_stage()
        at = [FREE]
        x1_at = at[0]
        x1 = sb("x1", [P, NB, D], F32, at)
        sx_at = at[0]
        sxh = sb("sxh", [P, NB, D], F32R, at)
        sxl = sb("sxl", [P, NB, D], F32R, at)
        counts_at = at[0]
        ch = sb("ch", [P, NB, HALF], F32R, at)
        cl = sb("cl", [P, NB, HALF], F32R, at)
        FREE_LATE = at[0]
        second_attention(nc, sb, sem, banks, locals())
        end_of_stage()
        graph_convolution(nc, sb, sem, banks, locals())


def graph_and_logits(nc, sb, sem, FREE, banks, t):
    x, countT, ident, ones, zero_r, xh, xl = t["x"], t["countT"], t["ident"], t["ones"], t["zero_r"], t["xh"], t["xl"]
    src_logit, src_logit02, dst_logit, bias1 = t["src_logit"], t["src_logit02"], t["dst_logit"], t["bias1"]
    dinv, gcn_bias1, many_i, a2_cols = t["dinv"], t["gcn_bias1"], t["many_i"], t["a2_cols"]
    mask_half = t["mask_half"]
    logits_d, dinv_d, mask_d, gat_w1 = t["logits_d"], t["dinv_d"], t["mask_d"], t["gat_w1"]

    at = [FREE]
    xr = sb("pro_x", [P, NB, D], F32, at)
    xT = sb("pro_xT", [P, FB, N], F32, at)
    w = [sb(f"pro_w{i}", [P, FB, D], F32, at) for i in range(2)]
    a_bc = sb("a_bc", [P, 2, 2, D], F32, at)
    early = [at[0]]
    product = sb("product", [P, 2, D], F32, at)
    edge_i = sb("edge_i", [P, 2, P], I32, early)
    edge_f = sb("edge_f", [P, 2, P], F32, early)
    quad_i = sb("quad_i", [P, P], I32, early)
    quad = sb("quad", [P, P], F32, early)
    quad_end = sb("quad_end", [P, P], F32, early)
    touch = sb("touch", [P, 2, NB], F32, early)
    touchT = sb("touchT", [P, 2, P], F32, early)
    assert early[0] <= at[0]
    small_in = nc.alloc_sbuf_tensor_at("small_in", [FB, 3, P], F32, offset=at[0])
    junk = sb("pro_junk", [P, 2, D], BF16, at)
    hot_src = [sb(f"hot_src{i}", [P, N], BF16, at) for i in range(4)]
    hot_dst = [sb(f"hot_dst{i}", [P, P], BF16, at) for i in range(4)]
    node_h = sb("node_h", [P, N], F16, at)
    node_i = nc.alloc_sbuf_tensor_at("node_i", [P, N], I32, offset=at[0])
    logitT = nc.alloc_sbuf_tensor_at("logitT", [2 * H, N], F32, offset=at[0])
    dinvT = nc.alloc_sbuf_tensor_at("dinvT", [NB, P], F32, offset=at[0] + 4 * N)
    count = [sb(f"count{i}", [P, N], F32, at) for i in range(2)]
    mask_late = sb("mask_late", [P, 2, N], BF16, at)
    edgeT = sb("edgeT", [P, 2, 2 * P], F32, at)
    block_i = sb("block_i", [P, NB], I32, at)
    block_f = sb("block_f", [P, NB], F32, at)
    span = sb("span", [P, 2], F32, at)
    range_f = sb("range_f", [P, 4], F32, at)
    range_i = sb("range_i", [P, 2], I32, at)
    zero_b = sb("zero_b", [P, 512], BF16, at)
    rows_in = sb("rows_in", [H * FB, P], F32, at)
    v = sb("v", [P, FB, 2 * H], F32, at)
    logit = sb("logit", [P, NB, 2 * H], F32, at)
    deg_parts = sb("deg_parts", [P, NB, 2], F32, at)
    deg = sb("deg", [P, NB], F32, at)
    many = sb("many", [P, NB + 1], F32, at)

    edges_in, small_rows_in = sem("edges_in"), sem("small_rows_in")
    x_in = sem("x_in")
    w_in = [sem(f"w_in{i}") for i in range(2)]
    a_in = [sem(f"a_in{i}") for i in range(2)]
    product_full, product_sum, v_sum = sem("product_full"), sem("product_sum"), sem("v_sum")
    const_g, const_v, edge_cast, edgeT_full, edgeT_done = (sem(n) for n in ("const_g", "const_v", "edge_cast", "edgeT_full", "edgeT_done"))
    span_done, span_full, range_done = sem("span_done"), sem("span_full"), sem("range_done")
    hot_ready = [sem(f"hot_ready{b}") for b in range(NB)]
    hot_free = [sem(f"hot_free{b}") for b in range(NB)]
    count_full, count_out, mask_done = sem("count_full"), sem("count_out"), sem("mask_done")
    turned, turned_out = sem("turned"), sem("turned_out")
    x_hi, x_lo = sem("x_hi"), sem("x_lo")
    cols_full, cols_done = sem("cols_full"), sem("cols_done")
    logitT_full, logitT_done, logit_full, logit_done, logits_out = (sem(n) for n in ("logitT_full", "logitT_done", "logit_full", "logit_done", "logits_out"))
    deg_step, root_done, dinv_done, dinvT_full, dinvT_done, dinv_out = (sem(n) for n in ("deg_step", "root_done", "dinv_done", "dinvT_full", "dinvT_done", "dinv_out"))
    mask_out = [sem(f"mask_out{i}") for i in range(2)]
    many_step, many_full, many_done = sem("many_step"), sem("many_full"), sem("many_done")

    XG, CG = 2 * FB, 2
    order = [[("x", g, 0) for g in range(2 * b, min(2 * b + 2, XG))] + [("count", b, i) for i in range(CG)] for b in range(NB)]
    group = {g: n for n, g in enumerate(g for of_block in order for g in of_block)}
    BY_VECTOR = 2

    def mask_of(b):
        return mask_half[:, b, :] if b < HNB else mask_late[:, b % 2, :]

    with nc.Block() as block:
        @block.sync
        def _(sp):
            sp.dma_start(edge_i[:, 0, :], t["src"].rearrange("(t p) -> t p", p=P)).then_inc(edges_in, 16)
            sp.dma_start(edge_i[:, 1, :], t["dst"].rearrange("(t p) -> t p", p=P)).then_inc(edges_in, 16)
            sp.dma_start(xr[:, :, :], x.rearrange("(b p) f -> p b f", p=P)).then_inc(x_in, 16)
            sp.dma_start(rows_in[:, :], t["gat_b1"].rearrange("(k p) -> k p", p=P)).then_inc(small_rows_in, 16)
            for i, name in enumerate(("gat_a_src2", "gat_a_dst2")):
                sp.dma_start(small_in[:, i, :], t[name].rearrange("a (k p) -> (a k) p", p=P)).then_inc(small_rows_in, 16)
            sp.dma_start(small_in[:, 2, :], t["gcn_b1"].rearrange("(k p) -> k p", p=P)).then_inc(small_rows_in, 16)
            for h in range(NB + 1):
                if h < H:
                    if h >= 2:
                        sp.wait_ge(v_sum, (h - 1) * 2 * BY_VECTOR)
                        sp.wait_ge(product_sum, (h - 1) * 2 * (FB - BY_VECTOR))
                    for k, name in enumerate(("gat_a_src1", "gat_a_dst1")):
                        sp.dma_start(a_bc[:, h % 2, k, :], t[name][h, :].partition_broadcast(P)).then_inc(a_in[h % 2], 16)
                    sp.dma_start(w[h % 2][:, :, :], gat_w1[:, h * D:(h + 1) * D].rearrange("(f p) c -> p f c", p=P)).then_inc(w_in[h % 2], 16)
                if h >= 1:
                    b = h - 1
                    sp.wait_ge(mask_done, b + 1)
                    sp.dma_start(mask_d[:, b * N:(b + 1) * N], mask_of(b)).then_inc(mask_out[b % 2], 16)
            sp.wait_ge(logitT_done, 2)
            sp.dma_start(logits_d, logitT[:, :]).then_inc(logits_out, 16)
            sp.wait_ge(dinvT_done, 1)
            sp.dma_start(dinv_d, dinvT[:, :]).then_inc(dinv_out, 16)
            for i in range(2):
                sp.wait_ge(mask_out[i], 16 * NB // 2)
            sp.wait_ge(dinv_out, 16)
            sp.wait_ge(logits_out, 16)

        @block.gpsimd
        def _(pool):
            nc.gpsimd.memset(ident[:, :], 0.0).then_inc(const_g, 1)
            nc.gpsimd.iota(node_i[:, :], pattern=[[1, N]], base=0, channel_multiplier=0).then_inc(const_g, 1)
            nc.gpsimd.iota(quad_i[:, :], pattern=[[1, ET // 4], [0, 4]], base=0, channel_multiplier=0).then_inc(const_g, 1)
            nc.gpsimd.iota(block_i[:, :], pattern=[[P, NB]], base=0, channel_multiplier=0).then_inc(const_g, 1)
            pool.wait_ge(const_g, 4)
            nc.gpsimd.affine_select(out=ident[:, :], in_=ident[:, :], compare_op=ALU.not_equal, fill=1.0, base=0,
                                    pattern=[[-1, P]], channel_multiplier=1).then_inc(const_g, 1)
            n = 0
            pool.wait_ge(range_done, 9)
            for h in range(H):
                pool.wait_ge(w_in[h % 2], 16 * (h // 2 + 1))
                pool.wait_ge(a_in[h % 2], 32 * (h // 2 + 1))
                for f in range(BY_VECTOR, FB):
                    for k in range(2):
                        if n >= 2:
                            pool.wait_ge(product_sum, n - 1)
                        nc.gpsimd.tensor_tensor(product[:, n % 2, :], w[h % 2][:, f, :], a_bc[:, h % 2, k, :], ALU.mult).then_inc(product_full, 1)
                        n += 1

        @block.vector
        def _(dve):
            nc.vector.memset(zero_b[:, :], 0.0).then_inc(const_v, 1)
            nc.vector.memset(ones[:, :], 1.0).then_inc(const_v, 1)
            dve.wait_ge(const_g, 5)
            nc.vector.tensor_copy(node_h[:, :], node_i[:, :]).then_inc(const_v, 1)
            nc.vector.tensor_copy(quad[:, :], quad_i[:, :]).then_inc(const_v, 1)
            nc.vector.tensor_copy(block_f[:, :], block_i[:, :]).then_inc(const_v, 1)
            dve.wait_ge(const_v, 5)
            nc.vector.tensor_scalar(quad_end[:, :], quad[:, :], -1.0, float(ET // 4), ALU.mult, ALU.add).then_inc(const_v, 1)
            nc.vector.tensor_scalar(zero_r[:, :], ones[:, :], 0.0, None, ALU.mult).then_inc(const_v, 1)
            dve.wait_ge(const_v, 7)
            nc.vector.tensor_scalar(quad[:, :], quad[:, :], 1.0, None, ALU.add).then_inc(const_v, 1)
            dve.wait_ge(edges_in, 32)
            nc.vector.tensor_copy(edge_f[:, :, :], edge_i[:, :, :]).then_inc(edge_cast, 1)
            dve.wait_ge(edge_cast, 1)
            nc.vector.tensor_reduce(span[:, 0:1], edge_f[:, 1, :], AX.X, ALU.min).then_inc(span_done, 1)
            nc.vector.tensor_reduce(span[:, 1:2], edge_f[:, 1, :], AX.X, ALU.max).then_inc(span_done, 1)
            dve.wait_ge(span_done, 2)
            nc.vector.tensor_scalar(touch[:, 0, :], block_f[:, :], span[:, 0:1], float(-P), ALU.subtract, ALU.is_gt).then_inc(span_done, 1)
            nc.vector.tensor_scalar(touch[:, 1, :], block_f[:, :], span[:, 1:2], None, ALU.is_le).then_inc(span_done, 1)
            dve.wait_ge(span_done, 4)
            nc.vector.tensor_tensor(touch[:, 0, :], touch[:, 0, :], touch[:, 1, :], ALU.mult).then_inc(span_done, 1)
            dve.wait_ge(edgeT_full, 2)
            nc.vector.tensor_copy(edgeT[:, 0, 0:P], banks[5][:, 0:P]).then_inc(edgeT_done, 1)
            nc.vector.tensor_copy(edgeT[:, 1, 0:P], banks[6][:, 0:P]).then_inc(edgeT_done, 1)
            dve.wait_ge(span_full, 1)
            dve.wait_ge(const_v, 8)
            nc.vector.tensor_tensor(touchT[0:NB, 0, :], banks[7][0:NB, 0:P], quad_end[0:NB, :], ALU.mult).then_inc(range_done, 1)
            nc.vector.tensor_tensor(touchT[0:NB, 1, :], banks[7][0:NB, 0:P], quad[0:NB, :], ALU.mult).then_inc(range_done, 1)
            dve.wait_ge(range_done, 2)
            nc.vector.tensor_reduce(range_f[0:NB, 0:1], touchT[0:NB, 0, :], AX.X, ALU.max).then_inc(range_done, 1)
            nc.vector.tensor_reduce(range_f[0:NB, 1:2], touchT[0:NB, 1, :], AX.X, ALU.max).then_inc(range_done, 1)
            dve.wait_ge(range_done, 4)
            nc.vector.tensor_scalar(range_f[0:NB, 0:1], range_f[0:NB, 0:1], 1.0, -1.0, ALU.max, ALU.mult).then_inc(range_done, 1)
            dve.wait_ge(range_done, 5)
            nc.vector.tensor_scalar(range_f[0:NB, 2:3], range_f[0:NB, 0:1], float(ET // 4), None, ALU.add).then_inc(range_done, 1)
            dve.wait_ge(range_done, 6)
            nc.vector.tensor_tensor(range_f[0:NB, 3:4], range_f[0:NB, 1:2], range_f[0:NB, 2:3], ALU.subtract).then_inc(range_done, 1)
            dve.wait_ge(range_done, 7)
            nc.vector.tensor_scalar(range_f[0:NB, 3:4], range_f[0:NB, 3:4], 1.0, None, ALU.max).then_inc(range_done, 1)
            dve.wait_ge(range_done, 8)
            nc.vector.tensor_copy(range_i[0:NB, :], range_f[0:NB, 2:4]).then_inc(range_done, 1)
            dve.wait_ge(range_done, 9)
            dve.wait_ge(edgeT_done, 2)

            dve.wait_ge(cols_full, 1)

            def beside_block(b):
                dve.wait_ge(w_in[b % 2], 16 * (b // 2 + 1))
                dve.wait_ge(a_in[b % 2], 32 * (b // 2 + 1))
                for f in range(BY_VECTOR):
                    for k in range(2):
                        n = 2 * (b * BY_VECTOR + f) + k
                        if n >= 2:
                            dve.wait_ge(v_sum, n - 1)
                        nc.vector.tensor_tensor_reduce(out=junk[:, k, :], in0=w[b % 2][:, f, :], in1=a_bc[:, b % 2, k, :], scale=1.0, scalar=0.0,
                                                       op0=ALU.mult, op1=ALU.add, accum_out=v[:, f, 2 * b + k:2 * b + k + 1]).then_inc(v_sum, 1)
                dve.wait_ge(count_out, 2 * b + 2)
                if b >= HNB + 2:
                    dve.wait_ge(mask_out[b % 2], 16 * (b // 2))
                nc.vector.tensor_scalar(mask_of(b), count[b % 2][:, :], 0.0, NOT_LINKED, ALU.is_equal, ALU.mult).then_inc(mask_done, 1)
                dve.wait_ge(x_hi, b + 1)
                nc.vector.tensor_tensor(xl[:, b, :], xr[:, b, :], xh[:, b, :].bitcast(F32), ALU.subtract).then_inc(x_lo, 1)

            for b in range(NB):
                first_quad = dve.value_load(range_i[b:b + 1, 0:1], min_val=0, max_val=ET // 4 - 1)
                quads = dve.value_load(range_i[b:b + 1, 1:2], min_val=1, max_val=ET // 4)
                with dve.Fori(0, quads) as q:
                    for j in range(4):
                        tile = (q + first_quad) * 4 + j
                        dve.wait_ge(hot_free[b], q * 4 + (j + 1))
                        nc.vector.tensor_scalar(hot_src[j][:, :], node_h[:, :], edgeT[:, 0, bass.ds(tile, 1)], None, ALU.is_equal)
                        nc.vector.tensor_scalar(hot_dst[j][:, :], node_h[:, b * P:(b + 1) * P], edgeT[:, 1, bass.ds(tile, 1)], None,
                                                ALU.is_equal).then_inc(hot_ready[b], 1)
                beside_block(b)
            nc.vector.tensor_tensor(deg[:, :], deg_parts[:, :, 0], deg_parts[:, :, 1], ALU.add).then_inc(deg_step, 1)
            dve.wait_ge(deg_step, 1)
            nc.vector.tensor_scalar(deg[:, :], deg[:, :], 1.0, None, ALU.add).then_inc(deg_step, 1)
            dve.wait_ge(deg_step, 2)
            nc.vector.tensor_scalar(many[:, 0:NB], deg[:, :], EXACT_COUNT, None, ALU.is_gt).then_inc(many_step, 1)
            dve.wait_ge(many_step, 1)
            nc.vector.tensor_reduce(many[:, NB:NB + 1], many[:, 0:NB], AX.X, ALU.add).then_inc(many_step, 1)
            dve.wait_ge(root_done, 1)
            nc.vector.reciprocal(dinv[:, :], deg[:, :]).then_inc(dinv_done, 1)
            dve.wait_ge(logit_full, 1)
            nc.vector.tensor_copy(logit[:, :, :], banks[6][:, 0:NB * 2 * H].rearrange("p (b r) -> p b r", b=NB)).then_inc(logit_done, 1)
            dve.wait_ge(logit_done, 1)
            by_head = logit[:, :, :].rearrange("p b (h k) -> p k h b", k=2)
            nc.vector.tensor_copy(src_logit[:, :, :], by_head[:, 0, :, :]).then_inc(logit_done, 1)
            nc.vector.tensor_scalar(src_logit02[:, :, :], by_head[:, 0, :, :], SLOPE, None, ALU.mult).then_inc(logit_done, 1)
            nc.vector.tensor_copy(dst_logit[:, :, :], by_head[:, 1, :, :]).then_inc(logit_done, 1)
            dve.wait_ge(many_full, 1)
            nc.vector.tensor_copy(many_i[0:1, 0:1], banks[5][0:1, 0:1]).then_inc(many_done, 1)

        @block.scalar
        def _(act):
            def group_out(g):
                kind, n, i = g
                bank = banks[5 + group[g] % 3]
                act.wait_ge(turned, group[g] + 1)
                if kind == "x":
                    to, frm = xT[:, n // 2, (n % 2) * 512:(n % 2 + 1) * 512], bank[:, :]
                else:
                    to, frm = countT[:, 4 * i:4 * i + 4, n * P:(n + 1) * P], bank[:, :].rearrange("p (s d) -> p s d", s=4)
                nc.scalar.copy(to, frm).then_inc(turned_out, 1)

            def sum_products(h, fs):
                for f in fs:
                    for k in range(2):
                        n = 2 * (h * (FB - BY_VECTOR) + f - BY_VECTOR) + k
                        act.wait_ge(product_full, n + 1)
                        nc.scalar.activation(product[:, n % 2, :], product[:, n % 2, :], ACT.Copy,
                                             accum_out=v[:, f, 2 * h + k:2 * h + k + 1]).then_inc(product_sum, 1)

            act.wait_ge(cols_full, 1)
            nc.scalar.copy(bias1[:, :], banks[4][:, 0:H * FB]).then_inc(cols_done, 1)
            nc.scalar.copy(a2_cols[:, :, :], banks[4][:, 256:256 + 2 * FB].rearrange("p (k c) -> p c k", k=2)).then_inc(cols_done, 1)
            nc.scalar.copy(gcn_bias1[:, :], banks[4][:, 256 + 2 * FB:256 + 3 * FB]).then_inc(cols_done, 1)
            act.wait_ge(x_in, 16)
            for b in range(NB):
                nc.scalar.copy(xh[:, b, :], xr[:, b, :]).then_inc(x_hi, 1)
                sum_products(b, range(BY_VECTOR, BY_VECTOR + 2))
                act.wait_ge(count_full, b + 1)
                if b >= 2:
                    act.wait_ge(turned, group[("count", b - 2, 1)] + 1)
                    act.wait_ge(mask_done, b - 1)
                for i in range(2):
                    nc.scalar.activation(count[b % 2][:, i * 512:(i + 1) * 512], banks[2 * (b % 2) + i][:, :], ACT.Copy,
                                         accum_out=deg_parts[:, b, i:i + 1]).then_inc(count_out, 1)
                for g in order[b]:
                    group_out(g)
                sum_products(b, range(BY_VECTOR + 2, FB))
            act.wait_ge(many_step, 2)
            nc.scalar.activation(deg[:, :], deg[:, :], ACT.Sqrt).then_inc(root_done, 1)
            for i in range(2):
                act.wait_ge(logitT_full, i + 1)
                nc.scalar.copy(logitT[:, i * 512:(i + 1) * 512], banks[i][0:2 * H, :]).then_inc(logitT_done, 1)
            act.wait_ge(dinvT_full, 1)
            nc.scalar.copy(dinvT[:, :], banks[7][0:NB, 0:P]).then_inc(dinvT_done, 1)

        @block.tensor
        def _(pe):
            pe.wait_ge(const_g, 5)
            pe.wait_ge(edge_cast, 1)
            for i in range(2):
                nc.tensor.transpose(banks[5 + i][:, 0:P], edge_f[:, i, :], ident[:, :]).then_inc(edgeT_full, 1)
            pe.wait_ge(span_done, 5)
            nc.tensor.transpose(banks[7][0:NB, 0:P], touch[:, 0, :], ident[:, :]).then_inc(span_full, 1)
            pe.wait_ge(small_rows_in, 64)
            K = H * FB
            nc.tensor.transpose(banks[4][:, 0:K], rows_in[:, :], ident[0:K, 0:K])
            for i in range(3):
                last = nc.tensor.transpose(banks[4][:, 256 + i * FB:256 + (i + 1) * FB], small_in[:, i, :], ident[0:FB, 0:FB])
            last.then_inc(cols_full, 1)

            def turn(g):
                kind, n, i = g
                at = group[g]
                if at >= 3:
                    pe.wait_ge(turned_out, at - 2)
                bank = banks[5 + at % 3]
                if kind == "x":
                    parts = [xr[:, 4 * (n % 2) + j, (n // 2) * P:(n // 2 + 1) * P] for j in range(4)]
                else:
                    parts = [count[n % 2][:, (4 * i + j) * P:(4 * i + j + 1) * P] for j in range(4)]
                for j, part in enumerate(parts):
                    last = nc.tensor.transpose(bank[:, j * P:(j + 1) * P], part, ident[:, :])
                last.then_inc(turned, 1)

            pe.wait_ge(x_in, 16)
            pe.wait_ge(range_done, 9)
            for b in range(NB):
                quads = pe.value_load(range_i[b:b + 1, 1:2], min_val=1, max_val=ET // 4)
                pair = banks[2 * (b % 2)], banks[2 * (b % 2) + 1]
                if b >= 2:
                    pe.wait_ge(count_out, 2 * (b - 1))
                for i in range(2):
                    last = nc.tensor.matmul(pair[i][:, :], zero_b[:, 0:P], zero_b[:, :], start=True, stop=False, skip_group_check=True)
                last.then_inc(hot_free[b], 4)
                with pe.Fori(0, quads) as q:
                    for j in range(4):
                        pe.wait_ge(hot_ready[b], q * 4 + (j + 1))
                        for i in range(2):
                            last = nc.tensor.matmul(pair[i][:, :], hot_dst[j][:, :], hot_src[j][:, i * 512:(i + 1) * 512],
                                                    start=False, stop=False, skip_group_check=True)
                        last.then_inc(hot_free[b], 1)
                for i in range(2):
                    last = nc.tensor.matmul(pair[i][:, :], zero_b[:, 0:P], zero_b[:, :], start=False, stop=True, skip_group_check=True)
                last.then_inc(count_full, 1)
                for g in order[b]:
                    if g == ("count", b, 0):
                        pe.wait_ge(count_out, 2 * b + 2)
                    turn(g)
            pe.wait_ge(turned_out, len(group))
            pe.wait_ge(v_sum, 2 * H * BY_VECTOR)
            pe.wait_ge(product_sum, 2 * H * (FB - BY_VECTOR))
            for i in range(2):
                for f in range(FB):
                    last = nc.tensor.matmul(banks[i][0:2 * H, :], v[:, f, :], xT[:, f, i * 512:(i + 1) * 512], start=(f == 0), stop=(f == FB - 1))
                last.then_inc(logitT_full, 1)
            for b in range(NB):
                if b % 4 == 0:
                    pe.wait_ge(logitT_done, b // 4 + 1)
                last = nc.tensor.transpose(banks[6][:, b * 2 * H:(b + 1) * 2 * H], logitT[:, b * P:(b + 1) * P], ident[0:2 * H, 0:2 * H])
            last.then_inc(logit_full, 1)
            pe.wait_ge(dinv_done, 1)
            nc.tensor.transpose(banks[7][0:NB, 0:P], dinv[:, :], ident[:, :]).then_inc(dinvT_full, 1)
            nc.tensor.matmul(banks[5][0:1, 0:1], many[:, NB:NB + 1], ones[:, 0:1], start=True, stop=True).then_inc(many_full, 1)


STEPS = [("B", 0), ("B", 1)] + [s for k in range(2, FB) for s in (("C", k - 2), ("B", k))] + [("C", FB - 2), ("C", FB - 1)]
NS = len(STEPS)
RAW, PARTS = 3, 4


def attention_heads(nc, sb, sem, FREE, banks, t):
    countT, ident, ones, zero_r, xh, xl = t["countT"], t["ident"], t["ones"], t["zero_r"], t["xh"], t["xl"]
    src_logit, src_logit02, dst_logit, bias1 = t["src_logit"], t["src_logit02"], t["dst_logit"], t["bias1"]
    logits_d, expo_d, mask_d, h2_d = t["logits_d"], t["expo_d"], t["mask_d"], t["h2_d"]
    gat_w1, gat_w2 = t["gat_w1"], t["gat_w2"]
    at = [FREE]
    ph = sb("ph", [P, NB, HALF], F32R, at)
    pl = sb("pl", [P, NB, HALF], F32R, at)
    yh = sb("yh", [P, FB, HALF], F32R, at)
    yl = sb("yl", [P, FB, HALF], F32R, at)
    h_at = at[0]
    hh = sb("hh", [P, 3, HALF], F32R, at)
    hl = sb("hl", [P, 3, HALF], F32R, at)
    wh = sb("wh", [P, PARTS, D], F32R, at)
    wl = sb("wl", [P, PARTS, D], F32R, at)
    wr = sb("wr", [P, RAW, D], F32, at)
    expo_bc = sb("expo_bc", [P, 2, HALF], F32, at)
    psum_rows = sb("psum_rows", [P, HALF], F32, at)
    rden = sb("rden", [P, HALF], F32, at)
    pf = sb("pf", [P, 2, HALF], F32, at)
    e_at = at[0]
    e1 = sb("e1", [P, 2, HALF], F32, at)
    e2 = sb("e2", [P, 2, HALF], F32, at)
    r_at = at[0]
    he = sb("he", [P, 2, HALF], F32, at)
    hr = sb("hr", [P, 2, HALF], F32, at)
    mask = t["mask_half"]
    top = sb("top", [P, HNB], F32, at)
    expo = sb("expo", [P, 2, HNB], F32, at)
    row_bc = nc.alloc_sbuf_tensor_at("row_bc", [P, N], F32, offset=e_at)
    yf = nc.alloc_sbuf_tensor_at("yf", [P, 2, HALF], F32, offset=e_at + 4 * N)
    junk = nc.alloc_sbuf_tensor_at("junk", [P, HNB, N], BF16, offset=r_at)
    rows = nc.alloc_sbuf_tensor_at("rows", [P, 2, D], F32, offset=r_at)
    cols = nc.alloc_sbuf_tensor_at("cols", [P, FB, HALF], F32, offset=h_at)

    U = 2 * H
    w_in = [sem(f"w_in{i}") for i in range(RAW)]
    w_hi = sem("w_hi")
    w_lo = sem("w_lo")
    w_used = sem("w_used")
    row_in, mask_in, top_sum, expo_step = sem("row_in"), sem("mask_in"), sem("top_sum"), sem("expo_step")
    expo_saved, expo_in = sem("expo_saved"), sem("expo_in")
    e_done, e_max, p_hi = sem("e_done"), sem("e_max"), sem("p_hi")
    p_full = sem("p_full")
    p_lo = sem("p_lo")
    p_sum = sem("p_sum")
    den_full, den_out, rden_done = sem("den_full"), sem("den_out"), sem("rden_done")
    y_full, y_hi = sem("y_full"), sem("y_hi")
    y_out = sem("y_out")
    y_lo = sem("y_lo")
    h_out = sem("h_out")
    h_sum, h_hi = sem("h_sum"), sem("h_hi")
    h_lo = sem("h_lo")
    cols_done, rows_turned, rows_done, cols_saved = sem("cols_done"), sem("rows_turned"), sem("rows_done"), sem("cols_saved")
    rows_saved = [sem(f"rows_saved{i}") for i in range(2)]

    def units(engine, unit):
        unit(0, 0, 0, (0, 1), False, True)
        with engine.Fori(1, H - 1) as h:
            unit(h, 0, h, (0, h + 1), False)
        unit(H - 1, 0, H - 1, (1, 0), False)
        unit(H, 1, 0, (1, 1), True)
        with engine.Fori(1, H - 1) as h:
            unit(h + H, 1, h, (1, h + 1), False)
        unit(U - 1, 1, H - 1, None, False)

    def y_bank(f, first):
        return banks[f] if first else work_bank("A", f)

    def work_bank(kind, k=0):
        at = {"sums": 0, "A": 1 + k, "B": 1 + FB + k}[kind]
        return banks[6 + at % 2]

    with nc.Block() as block:
        @block.sync
        def _(sp):
            def load_row(h):
                sp.dma_start(row_bc[:, :], logits_d[bass.ds(h * 2, 1), :].rearrange("a n -> (a n)").partition_broadcast(P)).then_inc(row_in, 16)

            def load_mask(half):
                sp.dma_start(mask[:, :, :].rearrange("p b n -> p (b n)"), mask_d[:, half * HNB * N:(half + 1) * HNB * N]).then_inc(mask_in, 16)

            def exponents_to_all(v):
                sp.wait_ge(expo_step, v * 4 + 4)
                sp.dma_start(expo_d.rearrange("k p -> p k"), expo[:, :, :].rearrange("p k c -> p (k c)"), allow_slow_non_contiguous=True).then_inc(expo_saved, 16)
                sp.wait_ge(expo_saved, v * 16 + 16)
                sp.dma_start(expo_bc[:, :, :].rearrange("p k n -> p (k n)"), expo_d.rearrange("k p -> (k p)").partition_broadcast(P)).then_inc(expo_in, 16)

            def load_chunk(u, h, s):
                kind, k = STEPS[s]
                i = s % RAW
                sp.wait_ge(w_lo, u * NS + (s + 1))
                if kind == "B":
                    sp.dma_start(wr[:, i, :].rearrange("p (f c) -> p f c", f=FB),
                                 gat_w1[:, bass.ds(h * D + k * P, P)].rearrange("(f p) c -> p f c", p=P)).then_inc(w_in[i], 16)
                else:
                    sp.dma_start(wr[:, i, :], gat_w2[bass.ds(h * D + k * P, P), :]).then_inc(w_in[i], 16)

            def unit(u, half, h, following, leaving, first=False):
                if following:
                    sp.wait_ge(p_lo, u * NB + (NB + 2))
                    load_row(following[1])
                    if following[0] != half:
                        sp.wait_ge(top_sum, (u + 1) * HNB)
                        load_mask(following[0])
                for s in range(NS):
                    load_chunk(u, h, s)
                    if s == RAW and following:
                        exponents_to_all(u + 1)
                    if s == 5 and leaving:
                        for b in range(HNB):
                            sp.wait_ge(rows_done, 2 * b + 2)
                            sp.dma_start(h2_d[b * P:(b + 1) * P, :], rows[:, b % 2, :]).then_inc(rows_saved[b % 2], 16)

            load_row(0)
            exponents_to_all(0)
            units(sp, unit)
            for i in range(2):
                sp.wait_ge(rows_saved[i], 16 * HNB // 2)

        @block.gpsimd
        def _(pool):
            def sum_rows(v):
                for i in range(1, NB):
                    pool.wait_ge(p_full, v * NB + (i + 3))
                    if i >= 2:
                        pool.wait_ge(p_sum, v * (NB - 1) + (i + 1))
                    before = pf[:, 0, :] if i == 1 else psum_rows[:, :]
                    nc.gpsimd.tensor_tensor(psum_rows[:, :], before, pf[:, i % 2, :], ALU.add).then_inc(p_sum, 1)

            def unit(u, half, h, following, leaving, first=False):
                if following:
                    pool.wait_ge(den_full, u + 1)
                    sum_rows(u + 1)

            pool.sem_inc(p_sum, 2)
            sum_rows(0)
            units(pool, unit)

        @block.scalar
        def _(act):
            def exponentials(v, h, i):
                act.wait_ge(p_full, v * NB + (i + 1))
                nc.scalar.activation(e1[:, i % 2, :], expo_bc[:, 0, :], ACT.Exp, bias=src_logit[:, bass.ds(h, 1), i])
                nc.scalar.activation(e2[:, i % 2, :], expo_bc[:, 1, :], ACT.Exp, bias=src_logit02[:, bass.ds(h, 1), i]).then_inc(e_done, 1)

            def weight_high(v, i):
                act.wait_ge(p_full, v * NB + (i + 3))
                nc.scalar.copy(ph[:, i, :], pf[:, i % 2, :]).then_inc(p_hi, 1)

            def chunk_high(u, s):
                act.wait_ge(w_in[s % RAW], u * (NS // RAW * 16) + (s // RAW + 1) * 16)
                act.wait_ge(w_used, u * NS + (s + 1))
                nc.scalar.copy(wh[:, s % PARTS, :], wr[:, s % RAW, :]).then_inc(w_hi, 1)

            def unit(u, half, h, following, leaving, first=False):
                if leaving:
                    act.wait_ge(w_used, u * NS + PARTS)
                    for f in range(FB):
                        nc.scalar.copy(cols[:, f, :], banks[f][:, :]).then_inc(cols_done, 1)
                for f in range(FB):
                    if f < PARTS:
                        chunk_high(u, f)
                    act.wait_ge(y_out, u * FB + (f + 2))
                    nc.scalar.copy(yh[:, f, :], yf[:, f % 2, :]).then_inc(y_hi, 1)
                if following:
                    act.wait_ge(expo_in, u * 16 + 32)
                act.wait_ge(y_lo, u * FB + (FB + 2))
                for s, (kind, k) in enumerate(STEPS):
                    if following and s < NB:
                        exponentials(u + 1, following[1], s)
                    if kind == "B":
                        act.wait_ge(w_used, u * NS + (s + 1 + PARTS))
                        if leaving and k == 0:
                            for i in range(2):
                                act.wait_ge(rows_saved[i], 16 * HNB // 2)
                        act.wait_ge(h_lo, u * FB + (k + 2))
                        b = bias1[:, bass.ds(h * FB + k, 1)]
                        nc.scalar.activation(he[:, k % 2, :], work_bank("B", k)[:, :], ACT.Exp, bias=b)
                        nc.scalar.activation(hr[:, k % 2, :], work_bank("B", k)[:, :], ACT.Relu, bias=b).then_inc(h_out, 1)
                    if following and 1 <= s < NB + 1:
                        weight_high(u + 1, s - 1)
                    if s + PARTS < NS:
                        chunk_high(u, s + PARTS)

            act.sem_inc(h_out, 2)
            act.wait_ge(expo_in, 16)
            for i in range(NB + 1):
                if i < NB:
                    exponentials(0, 0, i)
                if i >= 1:
                    weight_high(0, i - 1)
            units(act, unit)

        @block.vector
        def _(dve):
            def exponents(v, half, h, ready=None):
                if ready:
                    ready()
                for c in range(HNB):
                    nc.vector.tensor_tensor_reduce(out=junk[:, c, :], in0=mask[:, c, :], in1=row_bc[:, :], scale=1.0, scalar=LOWEST,
                                                   op0=ALU.add, op1=ALU.max, accum_out=top[:, c:c + 1]).then_inc(top_sum, 1)
                dve.wait_ge(top_sum, v * HNB + HNB)
                ad = dst_logit[:, bass.ds(h, 1), half * HNB:(half + 1) * HNB].rearrange("p a c -> p (a c)")
                nc.vector.tensor_tensor(top[:, :], top[:, :], ad, ALU.add).then_inc(expo_step, 1)
                dve.wait_ge(expo_step, v * 4 + 1)
                nc.vector.scalar_tensor_tensor(out=top[:, :], in0=top[:, :], scalar=SLOPE, in1=top[:, :], op0=ALU.mult, op1=ALU.max).then_inc(expo_step, 1)
                dve.wait_ge(expo_step, v * 4 + 2)
                nc.vector.tensor_tensor(expo[:, 0, :], ad, top[:, :], ALU.subtract).then_inc(expo_step, 1)
                nc.vector.scalar_tensor_tensor(out=expo[:, 1, :], in0=ad, scalar=SLOPE, in1=top[:, :], op0=ALU.mult, op1=ALU.subtract).then_inc(expo_step, 1)

            def weight_products(v, half, i):
                dve.wait_ge(e_done, v * NB + (i + 1))
                nc.vector.tensor_tensor(e1[:, i % 2, :], e1[:, i % 2, :], e2[:, i % 2, :], ALU.max).then_inc(e_max, 1)
                dve.wait_ge(e_max, v * NB + (i + 1))
                dve.wait_ge(p_sum, v * (NB - 1) + (i + 1 if i < 2 else max(i - 2, 1) + 2))
                dve.wait_ge(p_lo, v * NB + (i + 1))
                nc.vector.scalar_tensor_tensor(out=pf[:, i % 2, :], in0=e1[:, i % 2, :], scalar=1.0,
                                               in1=countT[:, i, half * HALF:(half + 1) * HALF], op0=ALU.min, op1=ALU.mult).then_inc(p_full, 1)

            def weight_low(v, i):
                dve.wait_ge(p_hi, v * NB + (i + 1))
                nc.vector.tensor_tensor(pl[:, i, :], pf[:, i % 2, :], ph[:, i, :].bitcast(F32), ALU.subtract).then_inc(p_lo, 1)

            def chunk_low(u, s):
                dve.wait_ge(w_hi, u * NS + (s + 1))
                nc.vector.tensor_tensor(wl[:, s % PARTS, :], wr[:, s % RAW, :], wh[:, s % PARTS, :].bitcast(F32), ALU.subtract).then_inc(w_lo, 1)

            def unit(u, half, h, following, leaving, first=False):
                def prepare():
                    if not following:
                        chunk_low(u, 0)
                        return

                    def ready():
                        dve.wait_ge(expo_saved, u * 16 + 16)
                        dve.wait_ge(h_lo, u * FB + 3)
                        dve.wait_ge(expo_step, u * 4 + 4)
                        dve.wait_ge(row_in, u * 16 + 32)
                        chunk_low(u, 0)
                        if following[0] != half:
                            dve.wait_ge(mask_in, 16)

                    exponents(u + 1, *following, ready)

                if first:
                    prepare()
                dve.wait_ge(den_full, u + 1)
                dve.wait_ge(y_out, u * FB + 1)
                nc.vector.tensor_scalar(rden[:, :], work_bank("sums")[:, :], DEN_EPS, None, ALU.add).then_inc(den_out, 1)
                dve.wait_ge(den_out, u + 1)
                nc.vector.reciprocal(rden[:, :], rden[:, :]).then_inc(rden_done, 1)
                dve.wait_ge(rden_done, u + 1)
                for f in range(FB + 1):
                    if f == 1 and not first:
                        prepare()
                    if f == 3 and leaving:
                        dve.wait_ge(top_sum, (u + 2) * HNB)
                        for b in range(HNB):
                            if b >= 2:
                                dve.wait_ge(rows_saved[b % 2], 16)
                            for i in range(2):
                                dve.wait_ge(rows_turned, 2 * b + i + 1)
                                nc.vector.tensor_copy(rows[:, b % 2, i * HC:(i + 1) * HC], banks[(2 * b + i) % FB][:, 0:HC]).then_inc(rows_done, 1)
                    if f < FB:
                        dve.wait_ge(y_full, u * FB + (f + 1))
                        dve.wait_ge(y_lo, u * FB + (f + 1))
                        nc.vector.tensor_tensor(yf[:, f % 2, :], y_bank(f, first)[:, :], rden[:, :], ALU.mult).then_inc(y_out, 1)
                    if 1 <= f < PARTS:
                        chunk_low(u, f)
                    if f >= 1:
                        dve.wait_ge(y_hi, u * FB + f)
                        nc.vector.tensor_tensor(yl[:, f - 1, :], yf[:, (f - 1) % 2, :], yh[:, f - 1, :].bitcast(F32), ALU.subtract).then_inc(y_lo, 1)
                for s, (kind, k) in enumerate(STEPS):
                    if following and s < NB:
                        weight_products(u + 1, following[0], s)
                    if kind == "B":
                        dve.wait_ge(h_out, u * FB + (k + 3))
                        nc.vector.scalar_tensor_tensor(out=he[:, k % 2, :], in0=he[:, k % 2, :], scalar=1.0, in1=hr[:, k % 2, :],
                                                       op0=ALU.min, op1=ALU.add).then_inc(h_sum, 1)
                        dve.wait_ge(h_sum, u * FB + (k + 1))
                        dve.wait_ge(h_lo, u * FB + (k + 1))
                        nc.vector.tensor_scalar(hh[:, k % 3, :], he[:, k % 2, :], 1.0, None, ALU.subtract).then_inc(h_hi, 1)
                        dve.wait_ge(h_hi, u * FB + (k + 1))
                        nc.vector.scalar_tensor_tensor(out=hl[:, k % 3, :], in0=he[:, k % 2, :], scalar=1.0, in1=hh[:, k % 3, :].bitcast(F32),
                                                       op0=ALU.subtract, op1=ALU.subtract).then_inc(h_lo, 1)
                    if following and 1 <= s < NB + 1:
                        weight_low(u + 1, s - 1)
                    if s + PARTS < NS:
                        chunk_low(u, s + PARTS)

            dve.sem_inc(w_lo, RAW)
            dve.sem_inc(p_full, 2)
            dve.sem_inc(p_lo, 2)
            dve.sem_inc(y_lo, 2)
            dve.sem_inc(h_lo, 3)
            dve.sem_inc(y_out, 1)
            dve.wait_ge(row_in, 16)
            exponents(0, 0, 0)
            for i in range(NB + 1):
                if i < NB:
                    weight_products(0, 0, i)
                if i >= 1:
                    weight_low(0, i - 1)
            units(dve, unit)

        @block.tensor
        def _(pe):
            def open_banks():
                for f in range(FB):
                    nc.tensor.matmul(banks[f][:, :], zero_r[:, :], xl[:, 0, 0:HALF], start=True, stop=False, skip_group_check=True)

            def close_banks():
                for f in range(FB):
                    last = nc.tensor.matmul(banks[f][:, :], zero_r[:, :], xl[:, 0, 0:HALF], start=False, stop=True, skip_group_check=True)
                return last

            def unit(u, half, h, following, leaving, first=False):
                def sum_weights():
                    pe.wait_ge(p_sum, u * (NB - 1) + (NB + 1))
                    pe.wait_ge(h_out, u * FB + 2)
                    nc.tensor.matmul(work_bank("sums")[:, :], ones[:, :], psum_rows[:, :], start=True, stop=True).then_inc(den_full, 1)

                if first:
                    for b in range(NB):
                        if b == NB - 2:
                            sum_weights()
                        pe.wait_ge(p_lo, u * NB + (b + 3))
                        for f in range(FB):
                            fs = slice(f * P, (f + 1) * P)
                            last = split_products(nc, y_bank(f, first)[:, :], (xh[:, b, fs], xl[:, b, fs]), (ph[:, b, :], pl[:, b, :]),
                                                  b == 0, b == NB - 1)
                            if b == NB - 1:
                                last.then_inc(y_full, 1)
                else:
                    sum_weights()
                    pe.wait_ge(p_lo, u * NB + (NB + 2))
                for f in () if first else range(FB):
                    if f == 1:
                        pe.wait_ge(den_out, u + 1)
                    elif f >= 2:
                        pe.wait_ge(y_out, u * FB + f)
                    fs = slice(f * P, (f + 1) * P)
                    for b in range(NB):
                        last = split_products(nc, work_bank("A", f)[:, :], (xh[:, b, fs], xl[:, b, fs]), (ph[:, b, :], pl[:, b, :]),
                                              b == 0, b == NB - 1)
                    last.then_inc(y_full, 1)
                    if f == 2 and leaving:
                        pe.wait_ge(cols_done, FB)
                        for b in range(HNB):
                            for i in range(2):
                                n = 2 * b + i
                                if n >= FB:
                                    pe.wait_ge(rows_done, n - FB + 1)
                                for j in range(3):
                                    last = nc.tensor.transpose(banks[n % FB][:, j * P:(j + 1) * P], cols[:, 3 * i + j, b * P:(b + 1) * P], ident[:, :])
                                last.then_inc(rows_turned, 1)
                if leaving:
                    pe.wait_ge(rows_done, 2 * HNB)
                    open_banks()
                for s, (kind, k) in enumerate(STEPS):
                    if first and s == 2:
                        pe.wait_ge(y_out, FB + 1)
                        open_banks()
                    i = s % PARTS
                    pe.wait_ge(w_lo, u * NS + (s + 1 + RAW))
                    if kind == "B":
                        if k == 0 and not first:
                            pe.wait_ge(y_out, u * FB + FB)
                        if k >= 2:
                            pe.wait_ge(h_out, u * FB + (k + 1))
                        for f in range(FB):
                            if k == 0:
                                pe.wait_ge(y_lo, u * FB + (f + 3))
                            fs = slice(f * P, (f + 1) * P)
                            last = split_products(nc, work_bank("B", k)[:, :], (wh[:, i, fs], wl[:, i, fs]), (yh[:, f, :], yl[:, f, :]),
                                                  f == 0, f == FB - 1)
                    else:
                        pe.wait_ge(h_lo, u * FB + (k + 4))
                        for f in range(FB):
                            fs = slice(f * P, (f + 1) * P)
                            last = split_products(nc, banks[f][:, :], (wh[:, i, fs], wl[:, i, fs]), (hh[:, k % 3, :], hl[:, k % 3, :]),
                                                  False, False, grouped=False)
                    if s == NS - 1 and following and following[0] != half:
                        last = close_banks()
                    last.then_inc(w_used, 1)

            pe.sem_inc(w_used, PARTS)
            units(pe, unit)
            close_banks()


NORM_STEPS, NORM_ROOT = 6, 4


def normalise(nc, dve, row, stats, moments, root, n, added, step, root_done):
    dve.wait_ge(added, 2 * n + 2)
    for i in range(2):
        nc.vector.bn_stats(stats[:, i, :], row[:, i * HC:(i + 1) * HC]).then_inc(step, 1)
    dve.wait_ge(step, NORM_STEPS * n + 2)
    nc.vector.bn_aggr(moments, stats.rearrange("p i s -> p (i s)")).then_inc(step, 1)
    dve.wait_ge(step, NORM_STEPS * n + 3)
    nc.vector.tensor_scalar(root, moments[:, 1:2], LN_EPS, None, ALU.add).then_inc(step, 1)
    dve.wait_ge(root_done, n + 1)
    nc.vector.reciprocal(root, root).then_inc(step, 1)
    dve.wait_ge(step, NORM_STEPS * n + 5)
    nc.vector.tensor_scalar(row, row, moments[:, 0:1], root, ALU.subtract, ALU.mult).then_inc(step, 1)


def counts_high(nc, high, countT, half, i):
    return nc.scalar.copy(high[:, i, :], countT[:, i, half * HALF:(half + 1) * HALF])


def loops_high(nc, high, countT, ident, half, c):
    i = half * HNB + c
    return nc.vector.tensor_tensor(high[:, i, c * P:(c + 1) * P], countT[:, i, i * P:(i + 1) * P], ident[:, :], ALU.add)


def counts_low(nc, dve, low, high, countT, ident, half, number, step, done):
    for i in range(NB):
        c = i - half * HNB
        loops = 0 <= c < HNB
        nc.vector.tensor_tensor(low[:, i, :], countT[:, i, half * HALF:(half + 1) * HALF], high[:, i, :].bitcast(F32),
                                ALU.subtract).then_inc(step if loops else done, 1)
        if loops:
            tile = slice(c * P, (c + 1) * P)
            dve.wait_ge(step, number * HNB + c + 1)
            nc.vector.tensor_tensor(low[:, i, tile], low[:, i, tile].bitcast(F32), ident[:, :], ALU.add).then_inc(done, 1)


def second_attention(nc, sb, sem, banks, t):
    x, countT, ident, dinv, ones, a2_cols = t["x"], t["countT"], t["ident"], t["dinv"], t["ones"], t["a2_cols"]
    h2_d, mask_d, x1_d = t["h2_d"], t["mask_d"], t["x1_d"]
    x1, sxh, sxl, ch, cl = t["x1"], t["sxh"], t["sxl"], t["ch"], t["cl"]
    DX = D + 2
    h2 = nc.alloc_sbuf_tensor_at("h2", [P, NB, D], F32, offset=t["x1_at"])
    at = [t["counts_at"]]
    ph = [sb("p2h0", [P, NB, HALF], F32R, at)]
    pl = [sb("p2l0", [P, NB, HALF], F32R, at)]
    assert at[0] == t["FREE_LATE"]
    early = [at[0]]
    ph += [sb("p2h1", [P, NB, HALF], F32R, at)]
    pl += [sb("p2l1", [P, NB, HALF], F32R, at)]
    mask = sb("mask2", [P, NB, N], BF16, early)
    cols = sb("cols2", [P, FB, HALF], F32, early)
    diag = sb("diag2", [P, 2, HNB, P], F32, early)
    assert early[0] <= at[0]
    gh = sb("gh", [P, NB, DX], F32R, at)
    gl = sb("gl", [P, NB, DX], F32R, at)
    sx = nc.alloc_sbuf_tensor_at("sx", [P, D], F32, offset=at[0])
    b2_bc = sb("b2_bc", [P, D], F32, at)
    logit2 = sb("logit2", [P, 2, NB], F32, at)
    logit02 = sb("logit2_02", [P, NB], F32, at)
    top = sb("top2", [P, NB], F32, at)
    expo = sb("expo2", [P, 2, NB], F32, at)
    rden = sb("rden2", [P, NB], F32, at)
    stats = sb("stats1", [P, NB, 2, 6], F32, at)
    moments = sb("moments1", [P, NB, 2], F32, at)
    root = sb("root1", [P, NB], F32, at)
    at = [t["sx_at"]]
    a2_bc = sb("a2_bc", [P, 2, D], F32, at)
    expo_bc = sb("expo2_bc", [P, 2, N], F32, at)
    e1 = sb("e1_2", [P, 2, HALF], F32, at)
    e2 = sb("e2_2", [P, 2, HALF], F32, at)
    pf = sb("pf_2", [P, 2, HALF], F32, at)
    row_bc = sb("row2_bc", [P, N], F32, at)
    junk = [sb(f"junk2{i}", [P, N], BF16, at) for i in range(2)]
    assert at[0] <= t["counts_at"]

    a_in, b_in = sem("a2_in"), sem("b2_in")
    mask_in = [sem(f"mask2_in{i}") for i in range(2)]
    h2_in = [sem(f"h2_in{b}") for b in range(HNB)]
    x_in = [sem(f"x2_in{i}") for i in range(2)]
    cols_s, cols_v = sem("cols_s"), sem("cols_v")
    turned, turned_out = sem("turned"), sem("turned_out")
    logit_sum, logit_full, logit_done = sem("logit_sum"), sem("logit_full"), sem("logit_done")
    diag_done, spread, spread_out = sem("diag_done"), sem("spread"), sem("spread_out")
    g_hi, g_lo, g_lo_p, g_one, xb, small = (sem(n) for n in ("g_hi", "g_lo", "g_lo_p", "g_one", "xb", "small"))
    top_sum, e_done, e_max, p_full, p_hi, p_lo = (sem(n) for n in ("top_sum", "e_done", "e_max", "p_full", "p_hi", "p_lo"))
    agg_full, bank_free, agg_step, norm_step, root_done = (sem(n) for n in ("agg_full", "bank_free", "agg_step", "norm_step", "root_done"))
    sx_lo_v, sx_hi, sx_lo, c_hi, c_loops, x1_out = (sem(n) for n in ("sx_lo_v", "sx_hi", "sx_lo", "c_hi", "c_loops", "x1_out"))

    LAST = 2
    BY_VECTOR = (0, 4)

    def row_split(engine, b):
        of_vector = sum(i <= b for i in BY_VECTOR)
        engine.wait_ge(g_lo, of_vector)
        if b + 1 > of_vector:
            engine.wait_ge(g_lo_p, b + 1 - of_vector)

    PIECES = [(logit2[:, 0, :], row_bc[:, :], half) for half in range(2)] + \
             [(expo[:, k, :], expo_bc[:, k, :], half) for half in range(2) for k in range(2)]

    with nc.Block() as block:
        @block.sync
        def _(sp):
            for k, name in enumerate(("gat_a_src2", "gat_a_dst2")):
                sp.dma_start(a2_bc[:, k, :], t[name].rearrange("a c -> (a c)").partition_broadcast(P)).then_inc(a_in, 16)
            for b in range(HNB):
                sp.dma_start(h2[:, b, :], h2_d[b * P:(b + 1) * P, :]).then_inc(h2_in[b], 16)
            for i in range(2):
                sp.dma_start(mask[:, i * HNB:(i + 1) * HNB, :].rearrange("p b n -> p (b n)"), mask_d[:, i * HNB * N:(i + 1) * HNB * N]).then_inc(mask_in[i], 16)
            sp.dma_start(b2_bc[:, :], t["gat_b2"].partition_broadcast(P)).then_inc(b_in, 16)
            for b in range(NB):
                row_split(sp, b)
                sp.dma_start(x1[:, b, :], x[b * P:(b + 1) * P, :]).then_inc(x_in[b % 2], 16)
                if b >= 1:
                    sp.wait_ge(x_in[(b - 1) % 2], 16 * ((b - 1) // 2 + 1))
            for b in range(NB):
                sp.wait_ge(norm_step, NORM_STEPS * (b + 1))
                sp.dma_start(x1_d[b * P:(b + 1) * P, :], x1[:, b, :]).then_inc(x1_out, 16)
            sp.wait_ge(x1_out, 16 * NB)

        @block.gpsimd
        def _(pool):
            for b in range(NB):
                if b not in BY_VECTOR:
                    pool.wait_ge(g_hi, b + 1)
                    nc.gpsimd.tensor_tensor(gl[:, b, 0:D], h2[:, b, :], gh[:, b, 0:D].bitcast(F32), ALU.subtract).then_inc(g_lo_p, 1)
            pool.wait_ge(b_in, 16)
            for b in range(NB):
                pool.wait_ge(x_in[b % 2], 16 * (b // 2 + 1))
                nc.gpsimd.tensor_tensor(x1[:, b, :], x1[:, b, :], b2_bc[:, :], ALU.add).then_inc(xb, 1)
            for b in range(NB - LAST):
                pool.wait_ge(sx_hi, b + 1)
                nc.gpsimd.tensor_tensor(sxl[:, b, :], sx[:, :], sxh[:, b, :].bitcast(F32), ALU.subtract).then_inc(sx_lo, 1)

        @block.scalar
        def _(act):
            def row_high(b):
                nc.scalar.copy(gh[:, b, 0:D], h2[:, b, :]).then_inc(g_hi, 1)

            def spread_to_sbuf(n):
                _, to, half = PIECES[n]
                act.wait_ge(spread, n + 1)
                nc.scalar.copy(to[:, half * HALF:(half + 1) * HALF], banks[6 + n % 2][:, :]).then_inc(spread_out, 1)

            def exponentials(half, i):
                c = half * NB + i
                if c >= 2:
                    act.wait_ge(p_full, c - 1)
                hs = slice(half * HALF, (half + 1) * HALF)
                nc.scalar.activation(e1[:, i % 2, :], expo_bc[:, 0, hs], ACT.Exp, bias=logit2[:, 0, i:i + 1])
                nc.scalar.activation(e2[:, i % 2, :], expo_bc[:, 1, hs], ACT.Exp, bias=logit02[:, i:i + 1]).then_inc(e_done, 1)

            for f in range(0, FB, 2):
                nc.scalar.copy(cols[:, f, :], banks[f][:, :]).then_inc(cols_s, 1)
            for b in range(HNB):
                act.wait_ge(h2_in[b], 16)
                row_high(b)
            for n in range(2):
                spread_to_sbuf(n)
            for b in range(HNB):
                for i in range(2):
                    act.wait_ge(turned, 2 * b + i + 1)
                    nc.scalar.copy(h2[:, HNB + b, i * HC:(i + 1) * HC], banks[(2 * b + i) % FB][:, 0:HC]).then_inc(turned_out, 1)
            act.wait_ge(turned_out, 2 * HNB)
            for b in range(HNB, NB):
                row_high(b)
            for n in range(2, 4):
                spread_to_sbuf(n)
            act.wait_ge(spread_out, 4)
            for half in range(2):
                for i in range(NB + 1):
                    if i < NB:
                        if half == 1 and i == 0:
                            act.wait_ge(spread_out, 6)
                        exponentials(half, i)
                    if half == 0 and i == 0:
                        for n in range(4, 6):
                            spread_to_sbuf(n)
                    if half == 1 and i == NB:
                        act.wait_ge(agg_full, HNB)
                        for j in range(NB):
                            counts_high(nc, ch, countT, 0, j).then_inc(c_hi, 1)
                    if i >= 1:
                        act.wait_ge(p_full, half * NB + i)
                        nc.scalar.copy(ph[half][:, i - 1, :], pf[:, (i - 1) % 2, :]).then_inc(p_hi, 1)
            for b in range(NB):
                act.wait_ge(norm_step, NORM_STEPS * b + NORM_ROOT)
                nc.scalar.activation(root[:, b:b + 1], root[:, b:b + 1], ACT.Sqrt).then_inc(root_done, 1)
                act.wait_ge(norm_step, NORM_STEPS * (b + 1))
                if b < NB - LAST:
                    act.wait_ge(xb, NB)
                    if b >= 1:
                        act.wait_ge(sx_lo, b)
                    nc.scalar.activation(sx[:, :], x1[:, b, :], ACT.Copy, scale=dinv[:, b:b + 1])
                nc.scalar.activation(sxh[:, b, :], x1[:, b, :], ACT.Copy, scale=dinv[:, b:b + 1]).then_inc(sx_hi, 1)

        @block.vector
        def _(dve):
            def diagonals(n):
                frm, _, half = PIECES[n]
                if n >= 2:
                    dve.wait_ge(spread, n - 1)
                for c in range(HNB):
                    b = half * HNB + c
                    nc.vector.tensor_scalar(diag[:, n % 2, c, :], ident[:, :], frm[:, b:b + 1], None, ALU.mult).then_inc(diag_done, 1)

            def row_low(b):
                dve.wait_ge(g_hi, b + 1)
                nc.vector.tensor_tensor(gl[:, b, 0:D], h2[:, b, :], gh[:, b, 0:D].bitcast(F32), ALU.subtract).then_inc(g_lo, 1)

            def bank_out(b):
                left, right = banks[2 * (b % 4)], banks[2 * (b % 4) + 1]
                dve.wait_ge(agg_full, b + 1)
                nc.vector.tensor_scalar(rden[:, b:b + 1], right[:, HC:HC + 1], DEN_EPS, None, ALU.add).then_inc(agg_step, 1)
                dve.wait_ge(agg_step, 2 * b + 1)
                nc.vector.reciprocal(rden[:, b:b + 1], rden[:, b:b + 1]).then_inc(agg_step, 1)
                dve.wait_ge(agg_step, 2 * b + 2)
                dve.wait_ge(xb, b + 1)
                for i, bank in enumerate((left, right)):
                    cs = slice(i * HC, (i + 1) * HC)
                    nc.vector.scalar_tensor_tensor(out=x1[:, b, cs], in0=bank[:, 0:HC], scalar=rden[:, b:b + 1], in1=x1[:, b, cs],
                                                   op0=ALU.mult, op1=ALU.add).then_inc(bank_free, 1)

            for f in range(1, FB, 2):
                nc.vector.tensor_copy(cols[:, f, :], banks[f][:, :]).then_inc(cols_v, 1)
            zeros = ident[:, 0:2 * NB].rearrange("p (b c) -> p b c", c=2)
            nc.vector.tensor_scalar(gh[:, :, D:DX], zeros, 0.0, 1.0, ALU.mult, ALU.add).then_inc(g_one, 1)
            nc.vector.tensor_scalar(gl[:, :, D:DX], zeros, 0.0, None, ALU.mult).then_inc(g_one, 1)
            dve.wait_ge(a_in, 32)
            for b in range(HNB):
                dve.wait_ge(h2_in[b], 16)
                for k in range(2):
                    if b >= 1:
                        dve.wait_ge(logit_sum, 2 * b + k - 1)
                    nc.vector.tensor_tensor_reduce(out=junk[k][:, 0:D], in0=h2[:, b, :], in1=a2_bc[:, k, :], scale=1.0, scalar=0.0,
                                                   op0=ALU.mult, op1=ALU.add, accum_out=logit2[:, k, b:b + 1]).then_inc(logit_sum, 1)
            dve.wait_ge(logit_full, 1)
            nc.vector.tensor_copy(logit2[:, :, HNB:NB], banks[6][:, 0:2 * HNB].rearrange("p (b k) -> p k b", k=2)).then_inc(logit_done, 1)
            dve.wait_ge(logit_sum, 2 * HNB)
            dve.wait_ge(logit_done, 1)
            for n in range(2):
                diagonals(n)
            nc.vector.tensor_scalar(logit02[:, :], logit2[:, 0, :], SLOPE, None, ALU.mult).then_inc(small, 1)
            dve.wait_ge(spread_out, 2)
            for b in range(NB):
                if b % HNB == 0:
                    dve.wait_ge(mask_in[b // HNB], 16)
                if b >= 2:
                    dve.wait_ge(top_sum, b - 1)
                nc.vector.tensor_tensor_reduce(out=junk[b % 2][:, :], in0=mask[:, b, :], in1=row_bc[:, :], scale=1.0, scalar=LOWEST,
                                               op0=ALU.add, op1=ALU.max, accum_out=top[:, b:b + 1]).then_inc(top_sum, 1)
            dve.wait_ge(top_sum, NB)
            nc.vector.tensor_tensor(top[:, :], top[:, :], logit2[:, 1, :], ALU.add).then_inc(small, 1)
            dve.wait_ge(small, 2)
            nc.vector.scalar_tensor_tensor(out=top[:, :], in0=top[:, :], scalar=SLOPE, in1=top[:, :], op0=ALU.mult, op1=ALU.max).then_inc(small, 1)
            dve.wait_ge(small, 3)
            nc.vector.tensor_tensor(expo[:, 0, :], logit2[:, 1, :], top[:, :], ALU.subtract).then_inc(small, 1)
            nc.vector.scalar_tensor_tensor(out=expo[:, 1, :], in0=logit2[:, 1, :], scalar=SLOPE, in1=top[:, :], op0=ALU.mult, op1=ALU.subtract).then_inc(small, 1)
            dve.wait_ge(small, 5)
            for n in range(2, 6):
                diagonals(n)
            for half in range(2):
                for i in range(NB + 1):
                    c = half * NB + i
                    if i < NB:
                        dve.wait_ge(e_done, c + 1)
                        nc.vector.tensor_tensor(e1[:, i % 2, :], e1[:, i % 2, :], e2[:, i % 2, :], ALU.max).then_inc(e_max, 1)
                        dve.wait_ge(e_max, c + 1)
                        if c >= 2:
                            dve.wait_ge(p_lo, c - 1)
                        nc.vector.scalar_tensor_tensor(out=pf[:, i % 2, :], in0=e1[:, i % 2, :], scalar=1.0,
                                                       in1=countT[:, i, half * HALF:(half + 1) * HALF], op0=ALU.min, op1=ALU.mult).then_inc(p_full, 1)
                    if i >= 1:
                        dve.wait_ge(p_hi, c)
                        nc.vector.tensor_tensor(pl[half][:, i - 1, :], pf[:, (i - 1) % 2, :], ph[half][:, i - 1, :].bitcast(F32), ALU.subtract).then_inc(p_lo, 1)
                        if half == 0 and i - 1 in BY_VECTOR:
                            row_low(i - 1)
                    if half == 1 and i == 6:
                        for b in range(HNB):
                            bank_out(b)
            dve.wait_ge(c_hi, HNB)
            for c in range(HNB):
                loops_high(nc, ch, countT, ident, 0, c).then_inc(c_loops, 1)
            for b in range(NB):
                if b >= HNB:
                    bank_out(b)
                normalise(nc, dve, x1[:, b, :], stats[:, b, :, :], moments[:, b, :], root[:, b:b + 1], b, bank_free, norm_step, root_done)
                if b >= NB - LAST:
                    dve.wait_ge(sx_hi, b + 1)
                    nc.vector.scalar_tensor_tensor(out=sxl[:, b, :], in0=x1[:, b, :], scalar=dinv[:, b:b + 1], in1=sxh[:, b, :].bitcast(F32),
                                                   op0=ALU.mult, op1=ALU.subtract).then_inc(sx_lo_v, 1)

        @block.tensor
        def _(pe):
            def spread_piece(n):
                pe.wait_ge(diag_done, HNB * (n + 1))
                if n >= 2:
                    pe.wait_ge(spread_out, n - 1)
                nc.tensor.matmul(banks[6 + n % 2][:, :], ones[:, :], diag[:, n % 2, :, :].rearrange("p c n -> p (c n)"),
                                 start=True, stop=True).then_inc(spread, 1)

            def add_source(half, s, c):
                bs = slice(c * P, (c + 1) * P)
                for i in range(2):
                    cs = slice(i * HC, (i + 1) * HC + 2 * i)
                    last = split_products(nc, banks[2 * c + i][:, 0:HC + 2 * i], (ph[half][:, s, bs], pl[half][:, s, bs]),
                                          (gh[:, s, cs], gl[:, s, cs]), s == 0, s == NB - 1)
                return last

            pe.wait_ge(cols_s, FB // 2)
            pe.wait_ge(cols_v, FB // 2)
            for b in range(HNB):
                for f in range(FB):
                    last = nc.tensor.matmul(banks[6][:, 2 * b:2 * b + 2], cols[:, f, b * P:(b + 1) * P], a2_cols[:, f, :], start=(f == 0), stop=(f == FB - 1))
            last.then_inc(logit_full, 1)
            for n in range(2):
                spread_piece(n)
            for b in range(HNB):
                for i in range(2):
                    n = 2 * b + i
                    if n >= FB:
                        pe.wait_ge(turned_out, n - FB + 1)
                    for j in range(3):
                        last = nc.tensor.transpose(banks[n % FB][:, j * P:(j + 1) * P], cols[:, 3 * i + j, b * P:(b + 1) * P], ident[:, :])
                    last.then_inc(turned, 1)
            for n in range(2, 6):
                spread_piece(n)
            pe.wait_ge(turned_out, 2 * HNB)
            pe.wait_ge(g_one, 2)
            for s in range(NB):
                pe.wait_ge(p_lo, s + 1)
                row_split(pe, s)
                for c in range(HNB):
                    if s == 0 and c == HNB - 1:
                        pe.wait_ge(spread_out, 6)
                    last = add_source(0, s, c)
                    if s == NB - 1:
                        last.then_inc(agg_full, 1)
            for group in ((0, 1), (2,), (3,)):
                for s in range(NB):
                    pe.wait_ge(p_lo, NB + s + 1)
                    for c in group:
                        if s == 0:
                            pe.wait_ge(bank_free, 2 * (c + 1))
                        last = add_source(1, s, c)
                        if s == NB - 1:
                            last.then_inc(agg_full, 1)


def graph_convolution(nc, sb, sem, banks, t):
    countT, ident, dinv, gcn_bias1, many_i = t["countT"], t["ident"], t["dinv"], t["gcn_bias1"], t["many_i"]
    dinv_d, x1_d, gcn_w1, gcn_w2, out = t["dinv_d"], t["x1_d"], t["gcn_w1"], t["gcn_w2"], t["out"]
    x1, xh, xl, ch, cl = t["x1"], t["sxh"], t["sxl"], t["ch"], t["cl"]
    at = [t["x1_at"]]
    wh = sb("gwh", [P, PARTS, D], F32R, at)
    wl = sb("gwl", [P, PARTS, D], F32R, at)
    assert at[0] <= t["sx_at"]
    at = [t["FREE_LATE"]]
    y_at = at[0]
    yh = sb("gyh", [P, FB, HALF], F32R, at)
    yl = sb("gyl", [P, FB, HALF], F32R, at)
    hh = sb("ghh", [P, FB, HALF], F32R, at)
    hl = sb("ghl", [P, FB, HALF], F32R, at)
    wr = sb("gwr", [P, RAW, D], F32, at)
    dinv_bc = sb("gdinv_bc", [P, N], F32, at)
    yf = sb("gyf", [P, 2, HALF], F32, at)
    hf = sb("ghf", [P, 2, HALF], F32, at)
    rows = sb("grows", [P, HNB, D], F32, at)
    stats = sb("gstats", [P, NB, 2, 6], F32, at)
    moments = sb("gmoments", [P, NB, 2], F32, at)
    root = sb("groot", [P, NB], F32, at)
    ch2 = nc.alloc_sbuf_tensor_at("gch2", [P, NB, HALF], F32R, offset=y_at)
    cl2 = nc.alloc_sbuf_tensor_at("gcl2", [P, NB, HALF], F32R, offset=y_at + 4 * NB * HALF)
    b2_bc = nc.alloc_sbuf_tensor_at("gb2_bc", [P, D], F32, offset=y_at + 4 * NB * HALF * 2)

    dinv_in, x1_in, b2_in = (sem(n) for n in ("gdinv_in", "gx1_in", "gb2_in"))
    w_in = [sem(f"gw_in{i}") for i in range(RAW)]
    w_hi, w_lo, w_used = sem("gw_hi"), sem("gw_lo"), sem("gw_used")
    c_hi, c_loops, c_step, c_lo = sem("gc_hi"), sem("gc_loops"), sem("gc_step"), sem("gc_lo")
    y_full, y_out, y_hi, y_lo = (sem(n) for n in ("gy_full", "gy_out", "gy_hi", "gy_lo"))
    h_out, h_lo = sem("gh_out"), sem("gh_lo")
    rows_full, rows_hi, rows_lo = sem("grows_full"), sem("grows_hi"), sem("grows_lo")
    row_done = [sem("grow_s"), sem("grow_v")]
    xb = sem("gxb")
    agg_full, added, norm_step, root_done, out_done = (sem(n) for n in ("gagg_full", "gadded", "gnorm_step", "groot_done", "gout_done"))
    CH = 2 * FB

    def row_full(engine, half, c):
        if c < HNB - 1:
            engine.wait_ge(rows_full, half * (HNB - 1) + c + 1)
        else:
            engine.wait_ge(w_used, (half + 1) * CH)


    with nc.Block() as block:
        @block.sync
        def _(sp):
            for half in range(2):
                for s in range(CH):
                    g, k = half * CH + s, s % FB
                    if g >= RAW:
                        sp.wait_ge(w_lo, g - RAW + 1)
                    if s < FB:
                        sp.dma_start(wr[:, g % RAW, :].rearrange("p (f c) -> p f c", f=FB),
                                     gcn_w1[:, k * P:(k + 1) * P].rearrange("(f p) c -> p f c", p=P)).then_inc(w_in[g % RAW], 16)
                    else:
                        sp.dma_start(wr[:, g % RAW, :], gcn_w2[k * P:(k + 1) * P, :]).then_inc(w_in[g % RAW], 16)
                    if g == 0:
                        sp.dma_start(dinv_bc[:, :], dinv_d.rearrange("b p -> (b p)").partition_broadcast(P)).then_inc(dinv_in, 16)
            sp.wait_ge(w_used, 2 * CH)
            sp.dma_start(x1[:, :, :], x1_d.rearrange("(b p) f -> p b f", p=P)).then_inc(x1_in, 16)
            sp.dma_start(b2_bc[:, :], t["gcn_b2"].partition_broadcast(P)).then_inc(b2_in, 16)
            for n in range(NB):
                b = (n + HNB) % NB
                sp.wait_ge(norm_step, NORM_STEPS * (n + 1))
                sp.dma_start(out[b * P:(b + 1) * P, :], x1[:, b, :]).then_inc(out_done, 16)
            sp.wait_ge(out_done, 16 * NB)

        @block.gpsimd
        def _(pool):
            pool.wait_ge(x1_in, 16)
            pool.wait_ge(b2_in, 16)
            for n in range(NB):
                b = (n + HNB) % NB
                nc.gpsimd.tensor_tensor(x1[:, b, :], x1[:, b, :], b2_bc[:, :], ALU.add).then_inc(xb, 1)

        @block.scalar
        def _(act):
            def chunk_high(g):
                act.wait_ge(w_in[g % RAW], 16 * (g // RAW + 1))
                if g >= PARTS:
                    act.wait_ge(w_used, g - PARTS + 1)
                nc.scalar.copy(wh[:, g % PARTS, :], wr[:, g % RAW, :]).then_inc(w_hi, 1)

            for half in range(2):
                for f in range(FB):
                    if f < PARTS:
                        chunk_high(half * CH + f)
                    act.wait_ge(y_out, half * FB + f + 1)
                    nc.scalar.copy(yh[:, f, :], yf[:, f % 2, :]).then_inc(y_hi, 1)
                for k in range(FB):
                    n = half * FB + k
                    act.wait_ge(w_used, half * CH + k + 1)
                    if n >= 2:
                        act.wait_ge(h_lo, n - 1)
                    nc.scalar.activation(hh[:, k, :], banks[2 + k % 2][:, :], ACT.Relu, bias=gcn_bias1[:, k:k + 1])
                    nc.scalar.activation(hf[:, k % 2, :], banks[2 + k % 2][:, :], ACT.Relu, bias=gcn_bias1[:, k:k + 1]).then_inc(h_out, 1)
                    if k + PARTS < CH:
                        chunk_high(half * CH + k + PARTS)
                if half == 0:
                    for i in range(NB):
                        counts_high(nc, ch, countT, 1, i).then_inc(c_hi, 1)
                for s in range(FB + PARTS, CH):
                    chunk_high(half * CH + s)
                if half == 1:
                    act.wait_ge(row_done[0], HNB)
                    act.wait_ge(row_done[1], HNB)
                    for b in range(HNB):
                        nc.scalar.copy(xh[:, b, :], rows[:, b, :]).then_inc(rows_hi, 1)
                for c in range(HNB):
                    row_full(act, half, c)
                    if half == 0:
                        nc.scalar.activation(rows[:, c, 0:HC], banks[2 * c][:, 0:HC], ACT.Copy, scale=dinv[:, c:c + 1]).then_inc(row_done[0], 1)
                    else:
                        for i in range(2):
                            nc.scalar.activation(xh[:, HNB + c, i * HC:(i + 1) * HC], banks[2 * c + i][:, 0:HC], ACT.Copy,
                                                 scale=dinv[:, HNB + c:HNB + c + 1]).then_inc(rows_hi, 1)
            for i in range(NB):
                counts_high(nc, ch2, countT, 0, i).then_inc(c_hi, 1)
            for n in range(NB):
                b = (n + HNB) % NB
                act.wait_ge(norm_step, NORM_STEPS * n + NORM_ROOT)
                nc.scalar.activation(root[:, b:b + 1], root[:, b:b + 1], ACT.Sqrt).then_inc(root_done, 1)

        @block.vector
        def _(dve):
            def chunk_low(g):
                dve.wait_ge(w_hi, g + 1)
                nc.vector.tensor_tensor(wl[:, g % PARTS, :], wr[:, g % RAW, :], wh[:, g % PARTS, :].bitcast(F32), ALU.subtract).then_inc(w_lo, 1)

            counts_low(nc, dve, cl, ch, countT, ident, 0, 0, c_step, c_lo)
            for half in range(2):
                hs = slice(half * HALF, (half + 1) * HALF)
                for f in range(FB + 1):
                    if f < PARTS:
                        chunk_low(half * CH + f)
                    if f == 0 and half == 0:
                        dve.wait_ge(dinv_in, 16)
                    if f < FB:
                        n = half * FB + f
                        dve.wait_ge(y_full, n + 1)
                        if n >= 2:
                            dve.wait_ge(y_lo, n - 1)
                        nc.vector.tensor_tensor(yf[:, f % 2, :], banks[f % 2][:, :], dinv_bc[:, hs], ALU.mult).then_inc(y_out, 1)
                    if f >= 1:
                        dve.wait_ge(y_hi, half * FB + f)
                        nc.vector.tensor_tensor(yl[:, f - 1, :], yf[:, (f - 1) % 2, :], yh[:, f - 1, :].bitcast(F32), ALU.subtract).then_inc(y_lo, 1)
                for k in range(FB):
                    dve.wait_ge(h_out, half * FB + k + 1)
                    nc.vector.tensor_tensor(hl[:, k, :], hf[:, k % 2, :], hh[:, k, :].bitcast(F32), ALU.subtract).then_inc(h_lo, 1)
                    if k + PARTS < CH:
                        chunk_low(half * CH + k + PARTS)
                if half == 0:
                    dve.wait_ge(c_hi, NB)
                    for c in range(HNB):
                        loops_high(nc, ch, countT, ident, 1, c).then_inc(c_loops, 1)
                    dve.wait_ge(c_loops, HNB)
                    counts_low(nc, dve, cl, ch, countT, ident, 1, 1, c_step, c_lo)
                for s in range(FB + PARTS, CH):
                    chunk_low(half * CH + s)
                if half == 1:
                    for b in range(HNB):
                        dve.wait_ge(rows_hi, b + 1)
                        nc.vector.tensor_tensor(xl[:, b, :], rows[:, b, :], xh[:, b, :].bitcast(F32), ALU.subtract).then_inc(rows_lo, 1)
                for c in range(HNB):
                    if half == 0:
                        row_full(dve, half, c)
                        nc.vector.tensor_scalar(rows[:, c, HC:D], banks[2 * c + 1][:, 0:HC], dinv[:, c:c + 1], None, ALU.mult).then_inc(row_done[1], 1)
                    else:
                        for i in range(2):
                            cs = slice(i * HC, (i + 1) * HC)
                            dve.wait_ge(rows_hi, HNB + 2 * c + i + 1)
                            nc.vector.scalar_tensor_tensor(out=xl[:, HNB + c, cs], in0=banks[2 * c + i][:, 0:HC], scalar=dinv[:, HNB + c:HNB + c + 1],
                                                           in1=xh[:, HNB + c, cs].bitcast(F32), op0=ALU.mult, op1=ALU.subtract).then_inc(rows_lo, 1)
            dve.wait_ge(c_hi, 2 * NB)
            for c in range(HNB):
                loops_high(nc, ch2, countT, ident, 0, c).then_inc(c_loops, 1)
            dve.wait_ge(c_loops, 2 * HNB)
            counts_low(nc, dve, cl2, ch2, countT, ident, 0, 2, c_step, c_lo)
            for n in range(NB):
                b = (n + HNB) % NB
                dve.wait_ge(agg_full, n + 1)
                dve.wait_ge(xb, n + 1)
                for i in range(2):
                    cs = slice(i * HC, (i + 1) * HC)
                    nc.vector.scalar_tensor_tensor(out=x1[:, b, cs], in0=banks[2 * (n % 4) + i][:, 0:HC], scalar=dinv[:, b:b + 1], in1=x1[:, b, cs],
                                                   op0=ALU.mult, op1=ALU.add).then_inc(added, 1)
                normalise(nc, dve, x1[:, b, :], stats[:, b, :, :], moments[:, b, :], root[:, b:b + 1], n, added, norm_step, root_done)

        @block.tensor
        def _(pe):
            many = pe.value_load(many_i[0:1, 0:1], min_val=0, max_val=N * NB)

            for half in range(2):
                if half:
                    pe.wait_ge(c_hi, NB)
                    pe.wait_ge(c_loops, HNB)
                for f in range(FB):
                    bank = banks[f % 2]
                    if f >= 2:
                        pe.wait_ge(y_out, half * FB + f - 1)
                    elif half:
                        pe.wait_ge(row_done[f], 1)
                    fs = slice(f * P, (f + 1) * P)
                    for b in range(NB):
                        nc.tensor.matmul(bank[:, :], xh[:, b, fs], ch[:, b, :], start=(b == 0), stop=False)
                    with pe.If(many > 0):
                        pe.wait_ge(c_lo, NB * (half + 1))
                        for b in range(NB):
                            nc.tensor.matmul(bank[:, :], xh[:, b, fs], cl[:, b, :], start=False, stop=False)
                    for b in range(NB):
                        last = nc.tensor.matmul(bank[:, :], xl[:, b, fs], ch[:, b, :], start=False, stop=(b == NB - 1))
                    last.then_inc(y_full, 1)
                for k in range(FB):
                    g = half * CH + k
                    pe.wait_ge(w_lo, g + 1)
                    if k >= 2:
                        pe.wait_ge(h_out, half * FB + k - 1)
                    elif half:
                        pe.wait_ge(row_done[k], 2)
                    for f in range(FB):
                        if k == 0:
                            pe.wait_ge(y_lo, half * FB + f + 1)
                        fs = slice(f * P, (f + 1) * P)
                        last = split_products(nc, banks[2 + k % 2][:, :], (wh[:, g % PARTS, fs], wl[:, g % PARTS, fs]), (yh[:, f, :], yl[:, f, :]),
                                              f == 0, f == FB - 1)
                    last.then_inc(w_used, 1)
                for k in range(FB):
                    g = half * CH + FB + k
                    pe.wait_ge(w_lo, g + 1)
                    pe.wait_ge(h_lo, half * FB + k + 1)
                    for c in (0, 2, 3, 1) if k == 0 else range(HNB):
                        if k == 0 and c == 1:
                            pe.wait_ge(h_out, half * FB + FB)
                        elif k == 0 and half:
                            for i in range(2):
                                pe.wait_ge(row_done[i], HNB)
                        bs = slice(c * P, (c + 1) * P)
                        for i in range(2):
                            cs = slice(i * HC, (i + 1) * HC)
                            last = split_products(nc, banks[2 * c + i][:, 0:HC], (hh[:, k, bs], hl[:, k, bs]), (wh[:, g % PARTS, cs], wl[:, g % PARTS, cs]),
                                                  k == 0, k == FB - 1)
                        if k == FB - 1 and c < HNB - 1:
                            last.then_inc(rows_full, 1)
                    last.then_inc(w_used, 1)
            for n in range(NB):
                high, low = ((ch, cl), (ch2, cl2))[n // HNB]
                c = n % HNB
                if n == HNB:
                    pe.wait_ge(c_hi, 2 * NB)
                    pe.wait_ge(c_loops, 2 * HNB)
                pair = banks[2 * (n % 4)], banks[2 * (n % 4) + 1]
                if n >= 4:
                    pe.wait_ge(added, 2 * (n - 3))
                else:
                    pe.wait_ge(rows_lo, HNB + 2 * n + 2)
                bs = slice(c * P, (c + 1) * P)
                for i, bank in enumerate(pair):
                    cs = slice(i * HC, (i + 1) * HC)
                    for s in range(NB):
                        if n == 0:
                            pe.wait_ge(rows_hi, s + 1 if s < HNB else HNB + 2 * (s - HNB) + 2)
                        nc.tensor.matmul(bank[:, 0:HC], high[:, s, bs], xh[:, s, cs], start=(s == 0), stop=False)
                    with pe.If(many > 0):
                        pe.wait_ge(c_lo, NB * (2 + n // HNB))
                        for s in range(NB):
                            nc.tensor.matmul(bank[:, 0:HC], low[:, s, bs], xh[:, s, cs], start=False, stop=False)
                    for s in range(NB):
                        if n == 0:
                            pe.wait_ge(rows_lo, s + 1 if s < HNB else HNB + 2 * (s - HNB) + 2)
                        last = nc.tensor.matmul(bank[:, 0:HC], high[:, s, bs], xl[:, s, cs], start=False, stop=(s == NB - 1))
                last.then_inc(agg_full, 1)


_INS = ["x", "src", "dst", "L0_gnn_W1", "L0_gnn_a_src1", "L0_gnn_a_dst1", "L0_gnn_b1", "L0_gnn_W2", "L0_gnn_a_src2", "L0_gnn_a_dst2",
        "L0_gnn_b2", "L1_gnn_W1", "L1_gnn_b1", "L1_gnn_W2", "L1_gnn_b2"]


def kernel(**inputs):
    import numpy as _np
    import concourse.bacc as _bacc
    from concourse import mybir as _mybir
    from concourse.bass_utils import run_bass_kernel_spmd as _run

    nc = _bacc.Bacc("TRN2", target_bir_lowering=False, num_devices=1)
    arrays, args = {}, []
    for name in _INS:
        a = _np.ascontiguousarray(inputs[name])
        arrays[f"in_{name}"] = a
        args.append(nc.dram_tensor(f"in_{name}", a.shape, _mybir.dt.from_np(a.dtype), kind="ExternalInput").ap())
    out = nc.dram_tensor("out_0", (N, D), _mybir.dt.float32, kind="ExternalOutput").ap()
    gnn_resnorm(nc, *args, out)
    r = _run(nc, [arrays], core_ids=[0])
    return r.results[0]["out_0"]
```
